# Optimizing a Trainium2 kernel written in Bass

```python
import numpy as np
import jax
import jax.numpy as jnp

def _softmax(x, axis=-1):
    return jax.nn.softmax(x, axis=axis)

def _gelu(x):
    return jax.nn.gelu(x, approximate=True)

def _silu(x):
    return jax.nn.silu(x)

def _sigmoid(x):
    return jax.nn.sigmoid(x)

def _layernorm(x, axis=-1, eps=1e-05):
    m = jnp.mean(x, axis=axis, keepdims=True)
    v = jnp.var(x, axis=axis, keepdims=True)
    return (x - m) / jnp.sqrt(v + eps)

def _scatter_add(tgt, idx, src, axis=0):
    return tgt.at[idx].add(src)

def _segment_sum(src, seg, n):
    return jax.ops.segment_sum(src, seg, n)
kernel_name = 'mk_early_fusion_d2_tok_img768_r4_1cc73a'

def setup_inputs(seed: int=0):
    np.random.seed(seed)
    _w = jnp.asarray

    def _rec_inputs():
        import jax
        import jax.numpy as jnp
        _rk = jax.random.key(seed)
        x = -0.000356955 + 1 * jax.random.normal(jax.random.fold_in(_rk, 1), (16, 3, 84, 84), jnp.float32)
        txt = 0.000369155 + 0.554878 * jax.random.normal(jax.random.fold_in(_rk, 2), (16, 128, 192), jnp.float32)
        return (x, txt)
    x, txt = _rec_inputs()

    def _L0_tok_setup():
        import jax, jax.numpy as jnp
        import numpy as np
        NBITS = 8
        QN = -2 ** (NBITS - 1)
        QP = 2 ** (NBITS - 1) - 1
        PATCH = 16

        def _ste_round(v):
            return v + jax.lax.stop_gradient(jnp.round(v) - v)

        def lsq_quant(x, alpha, qn, qp):
            return _ste_round(jnp.clip(x / alpha, qn, qp)) * alpha
        key = jax.random.key(seed)
        k1, k2 = jax.random.split(key)
        x = jax.random.normal(k1, (128, 3, 224, 224), jnp.float32)
        W = jax.random.normal(k2, (192, 3, 16, 16), jnp.float32) * 0.02
        b = jnp.zeros((192,), jnp.float32)
        alpha_w = (2.0 * jnp.mean(jnp.abs(W)) / jnp.sqrt(jnp.float32(QP))).astype(jnp.float32)
        alpha_a = (2.0 * jnp.mean(jnp.abs(x)) / jnp.sqrt(jnp.float32(QP))).astype(jnp.float32)
        return {'x': x, 'W': W, 'b': b, 'alpha_w': alpha_w, 'alpha_a': alpha_a}
    _L0_tok_all = _L0_tok_setup()
    _L0_tok_in = {k: v for k, v in _L0_tok_all.items() if k in ('W', 'b', 'alpha_w', 'alpha_a')}
    del _L0_tok_all

    def _L0_attn_setup():
        import jax, jax.numpy as jnp
        import numpy as np
        TAU = 2.0
        BN_EPS = 1e-05
        SG_ALPHA = 2.0

        @jax.custom_vjp
        def spike(u):
            return (u >= 0).astype(u.dtype)

        def _spike_fwd(u):
            return (spike(u), u)

        def _spike_bwd(u, g):
            sg = SG_ALPHA / 2.0 / (1.0 + (jnp.pi / 2.0 * SG_ALPHA * u) ** 2)
            return (g * sg,)
        spike.defvjp(_spike_fwd, _spike_bwd)

        def lif(x, v_th):
            return spike(x / TAU - v_th)

        def bn_eval(x, gamma, beta, mean, var):
            inv = gamma / jnp.sqrt(var + BN_EPS)
            return x * inv + (beta - mean * inv)
        key = jax.random.key(seed)
        ks = jax.random.split(key, 7)
        B, N, D = (2, 512, 192)
        x = jax.random.normal(ks[0], (B, N, D), dtype=jnp.float32)
        W = jax.random.normal(ks[1], (4, D, D), dtype=jnp.float32) * 0.02
        b = jnp.zeros((4, D), dtype=jnp.float32)
        bn_gamma = jax.random.uniform(ks[2], (4, D), dtype=jnp.float32, minval=0.5, maxval=1.5)
        bn_beta = jax.random.normal(ks[3], (4, D), dtype=jnp.float32) * 0.1
        bn_mean = jax.random.normal(ks[4], (4, D), dtype=jnp.float32) * 0.1
        bn_var = jax.random.uniform(ks[5], (4, D), dtype=jnp.float32, minval=0.5, maxval=1.5)
        return {'x': x, 'W': W, 'b': b, 'bn_gamma': bn_gamma, 'bn_beta': bn_beta, 'bn_mean': bn_mean, 'bn_var': bn_var}
    _L0_attn_all = _L0_attn_setup()
    _L0_attn_in = {k: v for k, v in _L0_attn_all.items() if k in ('W', 'b', 'bn_gamma', 'bn_beta', 'bn_mean', 'bn_var')}
    del _L0_attn_all

    def _L0_ffn_setup():
        import jax, jax.numpy as jnp
        import numpy as np
        B, L, D = (4, 256, 192)
        E, S, H = (32, 32, 768)
        EPS = 1e-12

        def _l2norm(v, axis):
            n = jnp.sqrt(jnp.sum(v * v, axis=axis, keepdims=True))
            return v / jnp.maximum(n, EPS)
        key = jax.random.key(seed)
        ks = jax.random.split(key, 6)
        x = jax.random.normal(ks[0], (B, L, D), dtype=jnp.float32)
        phi = jax.random.normal(ks[1], (D, E, S), dtype=jnp.float32) / np.sqrt(D)
        scale = jnp.ones((1,), dtype=jnp.float32)
        w1 = jax.random.normal(ks[2], (E, D, H), dtype=jnp.float32) / np.sqrt(D)
        b1 = jax.random.normal(ks[3], (E, H), dtype=jnp.float32) * 0.01
        w2 = jax.random.normal(ks[4], (E, H, D), dtype=jnp.float32) / np.sqrt(H)
        b2 = jax.random.normal(ks[5], (E, D), dtype=jnp.float32) * 0.01
        return {'x': x, 'phi': phi, 'scale': scale, 'w1': w1, 'b1': b1, 'w2': w2, 'b2': b2}
    _L0_ffn_all = _L0_ffn_setup()
    _L0_ffn_in = {k: v for k, v in _L0_ffn_all.items() if k in ('phi', 'scale', 'w1', 'b1', 'w2', 'b2')}
    del _L0_ffn_all

    def _L1_attn_setup():
        import jax, jax.numpy as jnp
        import numpy as np
        import math
        D_MODEL = 192
        N_HEADS = 12
        D_HEAD = D_MODEL // N_HEADS
        LATENT = 128
        HIDDEN = 512
        B, L = (1, 512)

        def _w(key, shape, scale=0.02):
            return jax.random.normal(key, shape, dtype=jnp.float32) * scale

        def rmsnorm(x, w, eps=1e-06):
            xf = x.astype(jnp.float32)
            rms = jax.lax.rsqrt(jnp.mean(xf * xf, axis=-1, keepdims=True) + eps)
            return w * (xf * rms).astype(x.dtype)

        def rope(x):
            Lx, Dh = (x.shape[1], x.shape[3])
            inv_freq = 1.0 / 10000.0 ** (jnp.arange(0, Dh, 2, dtype=jnp.float32) / Dh)
            t = jnp.arange(Lx, dtype=jnp.float32)
            freqs = jnp.outer(t, inv_freq)
            emb = jnp.concatenate([freqs, freqs], -1)
            cos = jnp.cos(emb)[None, :, None, :]
            sin = jnp.sin(emb)[None, :, None, :]
            x1, x2 = jnp.split(x, 2, axis=-1)
            x_rot = jnp.concatenate([-x2, x1], axis=-1)
            return x * cos + x_rot * sin
        key = jax.random.key(seed)
        ks = jax.random.split(key, 12)
        return {'x': jax.random.normal(ks[0], (B, L, D_MODEL), dtype=jnp.float32), 'ln_w': jnp.ones((D_MODEL,), jnp.float32), 'w_comp': _w(ks[1], (D_MODEL, LATENT)), 'w_qkv': _w(ks[2], (LATENT, 3 * D_MODEL)), 'w_reso': _w(ks[3], (LATENT, N_HEADS * 4)), 'qn_w': jnp.ones((D_HEAD,), jnp.float32), 'kn_w': jnp.ones((D_HEAD,), jnp.float32), 'w_outgate': _w(ks[4], (LATENT, D_MODEL)), 'head_decay': jnp.linspace(-3.0, 1.0, N_HEADS, dtype=jnp.float32), 'temperature': jnp.ones((1,), jnp.float32) * 0.5, 'w_proj': _w(ks[5], (D_MODEL, D_MODEL)), 'memn_w': jnp.ones((D_MODEL,), jnp.float32), 'ffn_ln_w': jnp.ones((D_MODEL,), jnp.float32), 'w1': _w(ks[6], (D_MODEL, HIDDEN)), 'w2': _w(ks[7], (D_MODEL, HIDDEN)), 'w3': _w(ks[8], (HIDDEN, D_MODEL))}
    _L1_attn_all = _L1_attn_setup()
    _L1_attn_in = {k: v for k, v in _L1_attn_all.items() if k in ('ln_w', 'w_comp', 'w_qkv', 'w_reso', 'qn_w', 'kn_w', 'w_outgate', 'head_decay', 'temperature', 'w_proj', 'memn_w', 'ffn_ln_w', 'w1', 'w2', 'w3')}
    del _L1_attn_all

    def _L1_ffn_setup():
        import jax, jax.numpy as jnp
        import numpy as np
        B, S, D = (2, 512, 192)
        E, K, F = (8, 2, 384)

        def _swiglu(xf, wg, wu, wd):
            return jax.nn.silu(xf @ wg.T) * (xf @ wu.T) @ wd.T
        key = jax.random.key(seed)
        ks = jax.random.split(key, 9)
        scale = 0.02
        x = jax.random.normal(ks[0], (B, S, D), dtype=jnp.float32)
        w_router = jax.random.normal(ks[1], (E, D), dtype=jnp.float32) * scale
        expert_bias = jnp.zeros((E,), dtype=jnp.float32)
        Wg = jax.random.normal(ks[2], (E, F, D), dtype=jnp.float32) * scale
        Wu = jax.random.normal(ks[3], (E, F, D), dtype=jnp.float32) * scale
        Wd = jax.random.normal(ks[4], (E, D, F), dtype=jnp.float32) * scale
        sg = jax.random.normal(ks[5], (F, D), dtype=jnp.float32) * scale
        su = jax.random.normal(ks[6], (F, D), dtype=jnp.float32) * scale
        sd = jax.random.normal(ks[7], (D, F), dtype=jnp.float32) * scale
        return {'x': x, 'w_router': w_router, 'expert_bias': expert_bias, 'Wg': Wg, 'Wu': Wu, 'Wd': Wd, 'sg': sg, 'su': su, 'sd': sd}
    _L1_ffn_all = _L1_ffn_setup()
    _L1_ffn_in = {k: v for k, v in _L1_ffn_all.items() if k in ('w_router', 'expert_bias', 'Wg', 'Wu', 'Wd', 'sg', 'su', 'sd')}
    del _L1_ffn_all
    return {'x': x, 'txt': txt, 'L0_tok_W': _L0_tok_in['W'], 'L0_tok_b': _L0_tok_in['b'], 'L0_tok_alpha_w': _L0_tok_in['alpha_w'], 'L0_tok_alpha_a': _L0_tok_in['alpha_a'], 'L0_attn_W': _L0_attn_in['W'], 'L0_attn_b': _L0_attn_in['b'], 'L0_attn_bn_gamma': _L0_attn_in['bn_gamma'], 'L0_attn_bn_beta': _L0_attn_in['bn_beta'], 'L0_attn_bn_mean': _L0_attn_in['bn_mean'], 'L0_attn_bn_var': _L0_attn_in['bn_var'], 'L0_ffn_phi': _L0_ffn_in['phi'], 'L0_ffn_scale': _L0_ffn_in['scale'], 'L0_ffn_w1': _L0_ffn_in['w1'], 'L0_ffn_b1': _L0_ffn_in['b1'], 'L0_ffn_w2': _L0_ffn_in['w2'], 'L0_ffn_b2': _L0_ffn_in['b2'], 'L1_attn_ln_w': _L1_attn_in['ln_w'], 'L1_attn_w_comp': _L1_attn_in['w_comp'], 'L1_attn_w_qkv': _L1_attn_in['w_qkv'], 'L1_attn_w_reso': _L1_attn_in['w_reso'], 'L1_attn_qn_w': _L1_attn_in['qn_w'], 'L1_attn_kn_w': _L1_attn_in['kn_w'], 'L1_attn_w_outgate': _L1_attn_in['w_outgate'], 'L1_attn_head_decay': _L1_attn_in['head_decay'], 'L1_attn_temperature': _L1_attn_in['temperature'], 'L1_attn_w_proj': _L1_attn_in['w_proj'], 'L1_attn_memn_w': _L1_attn_in['memn_w'], 'L1_attn_ffn_ln_w': _L1_attn_in['ffn_ln_w'], 'L1_attn_w1': _L1_attn_in['w1'], 'L1_attn_w2': _L1_attn_in['w2'], 'L1_attn_w3': _L1_attn_in['w3'], 'L1_ffn_w_router': _L1_ffn_in['w_router'], 'L1_ffn_expert_bias': _L1_ffn_in['expert_bias'], 'L1_ffn_Wg': _L1_ffn_in['Wg'], 'L1_ffn_Wu': _L1_ffn_in['Wu'], 'L1_ffn_Wd': _L1_ffn_in['Wd'], 'L1_ffn_sg': _L1_ffn_in['sg'], 'L1_ffn_su': _L1_ffn_in['su'], 'L1_ffn_sd': _L1_ffn_in['sd']}

def reference(x, txt, L0_tok_W, L0_tok_b, L0_tok_alpha_w, L0_tok_alpha_a, L0_attn_W, L0_attn_b, L0_attn_bn_gamma, L0_attn_bn_beta, L0_attn_bn_mean, L0_attn_bn_var, L0_ffn_phi, L0_ffn_scale, L0_ffn_w1, L0_ffn_b1, L0_ffn_w2, L0_ffn_b2, L1_attn_ln_w, L1_attn_w_comp, L1_attn_w_qkv, L1_attn_w_reso, L1_attn_qn_w, L1_attn_kn_w, L1_attn_w_outgate, L1_attn_head_decay, L1_attn_temperature, L1_attn_w_proj, L1_attn_memn_w, L1_attn_ffn_ln_w, L1_attn_w1, L1_attn_w2, L1_attn_w3, L1_ffn_w_router, L1_ffn_expert_bias, L1_ffn_Wg, L1_ffn_Wu, L1_ffn_Wd, L1_ffn_sg, L1_ffn_su, L1_ffn_sd):
    import jax
    import jax.numpy as jnp

    def _L0_tok_ref(x, W, b, alpha_w, alpha_a):
        import jax, jax.numpy as jnp
        import numpy as np
        NBITS = 8
        QN = -2 ** (NBITS - 1)
        QP = 2 ** (NBITS - 1) - 1
        PATCH = 16

        def _ste_round(v):
            return v + jax.lax.stop_gradient(jnp.round(v) - v)

        def lsq_quant(x, alpha, qn, qp):
            return _ste_round(jnp.clip(x / alpha, qn, qp)) * alpha
        xq = lsq_quant(x, alpha_a, QN, QP)
        wq = lsq_quant(W, alpha_w, QN, QP)
        y = jax.lax.conv_general_dilated(xq, wq, window_strides=(PATCH, PATCH), padding='VALID', dimension_numbers=('NCHW', 'OIHW', 'NCHW'))
        y = y + b[None, :, None, None]
        B, E, Hp, Wp = y.shape
        return jnp.transpose(y.reshape(B, E, Hp * Wp), (0, 2, 1))

    def _L0_attn_ref(x, W, b, bn_gamma, bn_beta, bn_mean, bn_var):
        import jax, jax.numpy as jnp
        import numpy as np
        TAU = 2.0
        BN_EPS = 1e-05
        SG_ALPHA = 2.0

        @jax.custom_vjp
        def spike(u):
            return (u >= 0).astype(u.dtype)

        def _spike_fwd(u):
            return (spike(u), u)

        def _spike_bwd(u, g):
            sg = SG_ALPHA / 2.0 / (1.0 + (jnp.pi / 2.0 * SG_ALPHA * u) ** 2)
            return (g * sg,)
        spike.defvjp(_spike_fwd, _spike_bwd)

        def lif(x, v_th):
            return spike(x / TAU - v_th)

        def bn_eval(x, gamma, beta, mean, var):
            inv = gamma / jnp.sqrt(var + BN_EPS)
            return x * inv + (beta - mean * inv)
        B, N, D = x.shape
        H = 12
        Hd = D // H
        scale = Hd ** (-0.125)

        def branch(inp, i, v_th=1.0):
            y = jnp.einsum('bnd,od->bno', inp, W[i]) + b[i]
            y = bn_eval(y, bn_gamma[i], bn_beta[i], bn_mean[i], bn_var[i])
            return lif(y, v_th)
        q = branch(x, 0)
        k = branch(x, 1)
        v = branch(x, 2)
        q = q.reshape(B, N, H, Hd).transpose(0, 2, 1, 3)
        k = k.reshape(B, N, H, Hd).transpose(0, 2, 1, 3)
        v = v.reshape(B, N, H, Hd).transpose(0, 2, 1, 3)
        attn = jnp.einsum('bhnd,bhmd->bhnm', q, k) * scale
        xa = jnp.einsum('bhnm,bhmd->bhnd', attn, v)
        xa = xa.transpose(0, 2, 1, 3).reshape(B, N, D)
        xa = lif(xa, 0.5)
        xa = branch(xa, 3)
        return xa

    def _L0_ffn_ref(x, phi, scale, w1, b1, w2, b2):
        import jax, jax.numpy as jnp
        import numpy as np
        B, L, D = (4, 256, 192)
        E, S, H = (32, 32, 768)
        EPS = 1e-12

        def _l2norm(v, axis):
            n = jnp.sqrt(jnp.sum(v * v, axis=axis, keepdims=True))
            return v / jnp.maximum(n, EPS)
        b, l, d = x.shape
        xn = _l2norm(x, axis=2)
        phin = scale * _l2norm(phi, axis=0)
        logits = jnp.einsum('bld,des->bles', xn, phin)
        d_w = jax.nn.softmax(logits, axis=-1)
        c_w = jax.nn.softmax(logits.reshape(b, l, E * S), axis=-1)
        slots = jnp.einsum('bld,bles->besd', xn, d_w)
        h = jax.nn.gelu(jnp.einsum('besd,edh->besh', slots, w1) + b1[:, None, :], approximate=False)
        eo = jnp.einsum('besh,ehd->besd', h, w2) + b2[:, None, :]
        eo = eo.reshape(b, E * S, d)
        return jnp.einsum('bkd,blk->bld', eo, c_w)

    def _L1_attn_ref(x, ln_w, w_comp, w_qkv, w_reso, qn_w, kn_w, w_outgate, head_decay, temperature, w_proj, memn_w, ffn_ln_w, w1, w2, w3):
        import jax, jax.numpy as jnp
        import numpy as np
        import math
        D_MODEL = 192
        N_HEADS = 12
        D_HEAD = D_MODEL // N_HEADS
        LATENT = 128
        HIDDEN = 512
        B, L = (1, 512)

        def _w(key, shape, scale=0.02):
            return jax.random.normal(key, shape, dtype=jnp.float32) * scale

        def rmsnorm(x, w, eps=1e-06):
            xf = x.astype(jnp.float32)
            rms = jax.lax.rsqrt(jnp.mean(xf * xf, axis=-1, keepdims=True) + eps)
            return w * (xf * rms).astype(x.dtype)

        def rope(x):
            Lx, Dh = (x.shape[1], x.shape[3])
            inv_freq = 1.0 / 10000.0 ** (jnp.arange(0, Dh, 2, dtype=jnp.float32) / Dh)
            t = jnp.arange(Lx, dtype=jnp.float32)
            freqs = jnp.outer(t, inv_freq)
            emb = jnp.concatenate([freqs, freqs], -1)
            cos = jnp.cos(emb)[None, :, None, :]
            sin = jnp.sin(emb)[None, :, None, :]
            x1, x2 = jnp.split(x, 2, axis=-1)
            x_rot = jnp.concatenate([-x2, x1], axis=-1)
            return x * cos + x_rot * sin
        Bx, Lx, D = x.shape
        H, Dh = (N_HEADS, D_HEAD)
        x_norm = rmsnorm(x, ln_w)
        latent = jax.nn.silu(x_norm @ w_comp)
        qkv = latent @ w_qkv
        q, k, v = jnp.split(qkv, 3, axis=-1)
        q = q.reshape(Bx, Lx, H, Dh)
        k = k.reshape(Bx, Lx, H, Dh)
        v = v.reshape(Bx, Lx, H, Dh)
        q = rope(rmsnorm(q, qn_w))
        k = rope(rmsnorm(k, kn_w))
        q_f = jax.nn.elu(q.astype(jnp.float32)) + 1.0
        k_f = jax.nn.elu(k.astype(jnp.float32)) + 1.0
        v_f = v.astype(jnp.float32)
        params = (latent @ w_reso).reshape(Bx, Lx, H, 4)
        sem_amp = jax.nn.sigmoid(params[..., 0])
        sem_phase = jax.nn.sigmoid(params[..., 1]) * math.pi
        ctx_amp = jax.nn.sigmoid(params[..., 2])
        ctx_phase = jax.nn.sigmoid(params[..., 3]) * math.pi
        raw_decay = 0.3 + 0.65 * jax.nn.sigmoid(head_decay.reshape(1, 1, H))
        decay_rate = jnp.clip(raw_decay, 1e-05, 0.999)
        dt = 1.0 - decay_rate
        base_gate = jax.nn.sigmoid(sem_amp * ctx_amp * jnp.cos(sem_phase - ctx_phase) * temperature)
        gate = jnp.clip(base_gate * 1.2 - 0.1, 0.05, 0.95)
        kv_input = jnp.einsum('blhd,blhe->blhde', k_f, v_f) * gate[..., None, None]
        kv_input = kv_input * dt[..., None, None]
        z_input = k_f * dt[..., None]
        log_decay = jnp.log(decay_rate)[..., None]
        cum_log_decay = jnp.cumsum(jnp.broadcast_to(log_decay, (Bx, Lx, H, 1)), axis=1)
        df = jnp.exp(cum_log_decay)
        safe_df_z = df + 1e-08
        kv_states = jnp.cumsum(kv_input / safe_df_z[..., None], axis=1) * df[..., None]
        z_states = jnp.cumsum(z_input / safe_df_z, axis=1) * df
        out_num = jnp.einsum('blhd,blhde->blhe', q_f, kv_states)
        den = jnp.clip(jnp.sum(q_f * z_states, axis=-1, keepdims=True), 1e-05, None)
        out = (out_num / den).reshape(Bx, Lx, D)
        out = rmsnorm(out, memn_w)
        attn_out = out @ w_proj * jax.nn.silu(latent @ w_outgate)
        x = x + attn_out
        xn = rmsnorm(x, ffn_ln_w)
        ffn_out = jax.nn.silu(xn @ w1) * (xn @ w2) @ w3
        return x + ffn_out

    def _L1_ffn_ref(x, w_router, expert_bias, Wg, Wu, Wd, sg, su, sd):
        import jax, jax.numpy as jnp
        import numpy as np
        B, S, D = (2, 512, 192)
        E, K, F = (8, 2, 384)

        def _swiglu(xf, wg, wu, wd):
            return jax.nn.silu(xf @ wg.T) * (xf @ wu.T) @ wd.T
        b, s, d = x.shape
        xf = x.reshape(-1, d)
        T = xf.shape[0]
        e = w_router.shape[0]
        logits = xf @ w_router.T
        scores = jax.nn.softmax(logits, axis=-1)
        selection = scores + expert_bias[None, :]
        _, top_idx = jax.lax.top_k(selection, K)
        top_s = jnp.take_along_axis(scores, top_idx, axis=-1)
        top_s = top_s / (jnp.sum(top_s, axis=-1, keepdims=True) + 1e-09)
        comb = jnp.zeros((T, e), dtype=x.dtype).at[jnp.arange(T)[:, None], top_idx].add(top_s)

        def body(acc, p):
            wg, wu, wd, c = p
            return (acc + c[:, None] * _swiglu(xf, wg, wu, wd), None)
        routed, _ = jax.lax.scan(body, jnp.zeros_like(xf), (Wg, Wu, Wd, comb.T))
        out = routed + _swiglu(xf, sg, su, sd)
        return out.reshape(b, s, d)
    h = _L0_tok_ref(x, L0_tok_W, L0_tok_b, L0_tok_alpha_w, L0_tok_alpha_a)
    h = jnp.concatenate([h, txt], axis=1)
    h = h + _L0_attn_ref(_layernorm(h, axis=-1), L0_attn_W, L0_attn_b, L0_attn_bn_gamma, L0_attn_bn_beta, L0_attn_bn_mean, L0_attn_bn_var)
    h = h + _L0_ffn_ref(_layernorm(h, axis=-1), L0_ffn_phi, L0_ffn_scale, L0_ffn_w1, L0_ffn_b1, L0_ffn_w2, L0_ffn_b2)
    h = h + _L1_attn_ref(_layernorm(h, axis=-1), L1_attn_ln_w, L1_attn_w_comp, L1_attn_w_qkv, L1_attn_w_reso, L1_attn_qn_w, L1_attn_kn_w, L1_attn_w_outgate, L1_attn_head_decay, L1_attn_temperature, L1_attn_w_proj, L1_attn_memn_w, L1_attn_ffn_ln_w, L1_attn_w1, L1_attn_w2, L1_attn_w3)
    h = h + _L1_ffn_ref(_layernorm(h, axis=-1), L1_ffn_w_router, L1_ffn_expert_bias, L1_ffn_Wg, L1_ffn_Wu, L1_ffn_Wd, L1_ffn_sg, L1_ffn_su, L1_ffn_sd)
    return h

_drawn_inputs = setup_inputs


def setup_inputs(seed=0):
    import zlib

    import numpy as np

    out = dict(_drawn_inputs(seed))
    spreads = {'L0_tok_b': (0.0, 0.1),
     'L0_attn_b': (0.0, 0.1),
     'L1_attn_ln_w': (1.0, 0.6),
     'L1_attn_qn_w': (1.0, 0.6),
     'L1_attn_kn_w': (1.0, 0.6),
     'L1_attn_memn_w': (1.0, 0.6),
     'L1_attn_ffn_ln_w': (1.0, 0.6),
     'L1_ffn_expert_bias': (0.0, 0.8)}
    factors = {'L0_ffn_phi': 8.0,
     'L0_ffn_w1': 8.0,
     'L0_ffn_b1': 8.0,
     'L0_ffn_w2': 8.0,
     'L0_ffn_b2': 8.0,
     'L1_attn_w_comp': 8.0,
     'L1_attn_w_qkv': 8.0,
     'L1_attn_w_reso': 8.0,
     'L1_attn_w_outgate': 8.0,
     'L1_attn_head_decay': 8.0,
     'L1_attn_w_proj': 8.0,
     'L1_attn_w1': 4.571,
     'L1_attn_w2': 4.525,
     'L1_attn_w3': 4.529,
     'L1_ffn_w_router': 8.0,
     'L1_ffn_Wg': 7.436,
     'L1_ffn_Wu': 6.928,
     'L1_ffn_Wd': 6.935,
     'L1_ffn_sg': 5.743,
     'L1_ffn_su': 5.677,
     'L1_ffn_sd': 5.707}
    for name, (base, spread) in spreads.items():
        noise = np.random.default_rng([zlib.crc32(name.encode()), seed]).standard_normal(out[name].shape)
        drawn = base * np.exp(spread * noise) if base else spread * noise
        out[name] = jnp.asarray(drawn.astype(out[name].dtype))
    for name, factor in factors.items():
        out[name] = (out[name] * factor).astype(out[name].dtype)
    return out
```

```python
import concourse.bass as bass
from concourse import mybir
from contextlib import ExitStack

FP32 = mybir.dt.float32
BF16 = mybir.dt.bfloat16
ALU = mybir.AluOpType
ACT = mybir.ActivationFunctionType
AXX = mybir.AxisListType.X

B = 16
D = 192
DC = 96
NPATCH = 25
NTXT = 128
N = NPATCH + NTXT
PATCH = 16
KPATCH = 3 * PATCH * PATCH
LN_EPS = 1e-5
RMS_EPS = 1e-6
E0, S0, H0 = 32, 32, 768
SLOTS = E0 * S0
NG = SLOTS // 128
HEADS, DH = 12, 16
E1, F1 = 8, 384
ROUND = 1.5 * 2.0 ** 23

TILE_AT = (NPATCH, 0)
TILE_ROWS = (NTXT, NPATCH)


class Chain:

    def __init__(self, eng, sem, passed=None):
        self.eng, self.sem, self.base, self.n, self.passed = eng, sem, 0, 0, passed

    def link(self, ins, apart=False):
        self.n += 1
        ins.then_inc(self.sem, 1)
        self.eng.wait_ge(self.sem, self.base + self.n)
        if apart:
            self.eng.sem_inc(self.passed, 1)

    def start_loop(self, i, per_turn):
        self.before = self.n
        self.per_turn = per_turn
        self.base = self.before + i * per_turn
        self.n = 0

    def end_loop(self, turns):
        assert self.n == self.per_turn, (self.n, self.per_turn)
        self.base = 0
        self.n = self.before + turns * self.per_turn


def phase_sems(ctx, nc, phase, names):
    sems = {name: nc.alloc_semaphore(name=f"{phase}_{name}") for name in names.split()}

    def clear():
        nc.clear_and_free_semaphores(list(sems.values()))
        nc.all_engine_barrier()
    ctx.callback(clear)
    return sems


def row_bc(ap, parts):
    return ap.unsqueeze(0).to_broadcast([parts] + list(ap.shape))


def patches(nc, t, psum):
    KC = KPATCH // 128
    with ExitStack() as ctx:
        def sb(name, shape, dt=FP32):
            return ctx.enter_context(nc.sbuf_tensor("tok_" + name, shape, dt))

        img = sb("img", [B * 5, 3, PATCH, 80])
        imgq = sb("imgq", [B * 5, 5, 3 * PATCH, PATCH], BF16)
        w = sb("w", [DC, 2, KPATCH])
        wq = sb("wq", [DC, 2, KPATCH], BF16)
        alpha = sb("alpha", [128, 2])
        ralpha = sb("ralpha", [128, 2])
        yscale = sb("yscale", [128, 1])
        bias = sb("bias", [128, D])
        ident = sb("ident", [128, 128])
        identb = sb("identb", [128, 128], BF16)
        imgT = sb("imgT", [128, KC, B, 5, 5], BF16)
        wT = sb("wT", [128, KC, D], BF16)
        emb = sb("emb", [100, 4, D])
        s = phase_sems(ctx, nc, "tok", "consts_in img_in txt_copied img_q w_q identb_ready turned evacuated "
                 "product scaled stored chain")
        block = ctx.enter_context(nc.Block())
        turn_ps = [psum[:, k, :].bitcast(BF16) for k in range(2)]

        @block.sync
        def _(sp):
            sp.dma_start(ident[:, :], t["ident"]).then_inc(s["consts_in"], 16)
            sp.dma_start(w[:, :, :], t["tok_W"].rearrange("(c o) i a b -> o c (i a b)", o=DC)).then_inc(s["consts_in"], 16)
            sp.dma_start(alpha[:, 0:1], row_bc(t["tok_alpha_a"], 128)).then_inc(s["consts_in"], 16)
            sp.dma_start(alpha[:, 1:2], row_bc(t["tok_alpha_w"], 128)).then_inc(s["consts_in"], 16)
            sp.dma_start(bias[:, :], row_bc(t["tok_b"], 128)).then_inc(s["consts_in"], 16)
            for c in range(3):
                for py in range(5):
                    sp.dma_start(img[py:B * 5:5, c, :, :],
                                 t["x"][:, c, PATCH * py:PATCH * py + PATCH, 0:80]).then_inc(s["img_in"], 16)
            sp.dma_start(t["h_dram"][:, NPATCH:N, :], t["txt"]).then_inc(s["txt_copied"], 16)
            for q in range(4):
                sp.wait_ge(s["scaled"], q + 1)
                for k in range(4):
                    sp.dma_start(t["h_dram"][4 * q + k, 0:NPATCH, :],
                                 emb[NPATCH * k:NPATCH * k + NPATCH, q, :]).then_inc(s["stored"], 16)
            sp.wait_ge(s["stored"], 16 * 16)
            sp.wait_ge(s["txt_copied"], 16)

        @block.vector
        def _(dve):
            ch = Chain(dve, s["chain"])
            dve.wait_ge(s["consts_in"], 5 * 16)
            nc.vector.tensor_copy(identb[:, :], ident[:, :]).then_inc(s["identb_ready"], 1)
            ch.link(nc.vector.reciprocal(ralpha[:, :], alpha[:, :]))

            def quantise(src, dst, ra, out_sem):
                ch.link(nc.vector.tensor_scalar(src, src, ra, -128.0, ALU.mult, ALU.max))
                ch.link(nc.vector.tensor_scalar(src, src, 127.0, ROUND, ALU.min, ALU.add))
                nc.vector.tensor_scalar(dst, src, -ROUND, None, ALU.add).then_inc(out_sem, 1)

            quantise(w[:, :, :], wq[:, :, :], ralpha[0:DC, 1:2], s["w_q"])
            dve.wait_ge(s["img_in"], 16 * 15)
            quantise(img[:, :, :, :].rearrange("p c i (x j) -> p (c i) x j", j=PATCH),
                     imgq[:, :, :, :].rearrange("p x r j -> p r x j"), ralpha[0:80, 0:1], s["img_q"])
            ch.link(nc.vector.tensor_tensor(yscale[:, :], alpha[:, 0:1], alpha[:, 1:2], ALU.mult))
            for q in range(4):
                dve.wait_ge(s["product"], q + 1)
                nc.vector.scalar_tensor_tensor(emb[:, q, :], psum[0:100, 2 + q, 0:D], yscale[0:100, :],
                                               bias[0:100, :], ALU.mult, ALU.add).then_inc(s["scaled"], 1)

        @block.tensor
        def _(pe):
            pe.wait_ge(s["identb_ready"], 1)
            pe.wait_ge(s["w_q"], 1)
            for k in range(KC):
                if k >= 2:
                    pe.wait_ge(s["evacuated"], k - 1)
                for c in range(2):
                    mm = nc.tensor.transpose(turn_ps[k % 2][:, c * DC:c * DC + DC], wq[:, c, 128 * k:128 * k + 128],
                                             identb[0:DC, 0:DC])
                mm.then_inc(s["turned"], 1)
            pe.wait_ge(s["img_q"], 1)
            for k in range(KC):
                pe.wait_ge(s["evacuated"], KC + k - 1)
                for px in range(5):
                    src = imgq[:, px, 8 * k:8 * k + 8, :].rearrange("p r j -> p (r j)")
                    mm = nc.tensor.transpose(turn_ps[k % 2][:, px * 80:px * 80 + 80], src, identb[0:80, 0:80])
                mm.then_inc(s["turned"], 1)
            pe.wait_ge(s["evacuated"], 2 * KC)
            for q in range(4):
                for k in range(KC):
                    mm = nc.tensor.matmul(psum[0:100, 2 + q, 0:D],
                                          imgT[:, k, 4 * q:4 * q + 4, :, :].rearrange("p b y x -> p (b y x)"), wT[:, k, :],
                                          start=(k == 0), stop=(k == KC - 1))
                mm.then_inc(s["product"], 1)

        @block.scalar
        def _(act):
            for k in range(KC):
                act.wait_ge(s["turned"], k + 1)
                nc.scalar.copy(wT[:, k, :], turn_ps[k % 2][:, 0:D]).then_inc(s["evacuated"], 1)
            for k in range(KC):
                act.wait_ge(s["turned"], KC + k + 1)
                nc.scalar.copy(imgT[:, k, :, :, :].rearrange("p b y x -> p (b y) x"),
                               turn_ps[k % 2][:, 0:400].rearrange("p (x a) -> p a x", x=5)).then_inc(s["evacuated"], 1)


def spiking_attention(nc, t, psum):
    TURNS = B // 2
    with ExitStack() as ctx:
        def sb(name, shape, dt=FP32):
            return ctx.enter_context(nc.sbuf_tensor("spk_" + name, shape, dt))

        ident = sb("ident", [128, 128])
        heads_mask = sb("heads_mask", [DC, DC])
        wrow = sb("wrow", [DC, 8, D])
        prm_c = sb("prm_c", [DC, 5, 8])
        prm_r = sb("prm_r", [128, 5, 4 * D])
        inv_c = sb("inv_c", [DC, 8])
        inv_r = sb("inv_r", [128, 4 * D])
        thr_c = sb("thr_c", [DC, 8])
        thr_r = sb("thr_r", [128, 4 * D])
        wT = sb("wT", [DC, 2, 4 * D])
        half = sb("half", [128, 8])
        h = sb("h", [128, 2, 4, D])
        stats = sb("stats", [128, 4, 6])
        mv = sb("mv", [128, 4, 2])
        rstd = sb("rstd", [128, 4])
        y = sb("y", [128, 4, D])
        yT = sb("yT", [DC, 2, 2, N])
        q = sb("q", [DC, 2, 2, N], BF16)
        kv = sb("kv", [128, 4, 2 * D], BF16)
        kvh = sb("kvh", [DC, 2, 2, DC], BF16)
        xs = sb("xs", [DC, 2, 2, N])
        spike = sb("spike", [128, 4, D])
        h1 = sb("h1", [128, 4, D])
        stats1 = sb("stats1", [128, 4, 6])
        mv1 = sb("mv1", [128, 4, 2])
        g = sb("g", [128, 5, 4])
        xn = sb("xn", [128, 4, D])
        xnT = sb("xnT", [DC, 2, 2, N])
        s = phase_sems(ctx, nc, "spk", "consts_in w_turned w_out wrow_ready thr_ready in0 in1 bn rstd_ready y_ready yT_ps yT_ready "
                 "q_ps q_ready kv_ps kv_ready kvh_ps kvh_ready xa_ps xs_ready sp_ps spike_ready h1_ready mv1_ready norm_ready "
                 "xn_ready xnT_ps xnT_ready h1_out xn_out xnT_out half_ready chain passed root")
        block = ctx.enter_context(nc.Block())
        s_in = (s["in0"], s["in1"])

        @block.sync
        def _(sp):
            sp.dma_start(ident[:, :], t["ident"]).then_inc(s["consts_in"], 16)
            sp.dma_start(heads_mask[:, :], t["heads_mask"]).then_inc(s["consts_in"], 16)
            sp.dma_start(wrow[:, :, :], t["attn_W"].rearrange("l (c o) d -> o (l c) d", o=DC)).then_inc(s["consts_in"], 16)
            for n, p in enumerate(t["attn_params"]):
                sp.dma_start(prm_c[:, n, :], p.rearrange("l (c o) -> o (l c)", o=DC), allow_slow_non_contiguous=True).then_inc(s["consts_in"], 16)
                sp.dma_start(prm_r[:, n, :], row_bc(p.rearrange("l d -> (l d)"), 128)).then_inc(s["consts_in"], 16)

            def load(batch0, u):
                for b in range(2):
                    for tile in range(2):
                        sp.dma_start(h[:, u, 2 * b + tile, :],
                                     t["h_dram"][batch0 + b, TILE_AT[tile]:TILE_AT[tile] + 128, :]).then_inc(s_in[u], 16)

            load(0, 0)
            with sp.Fori(0, TURNS // 2) as pair:
                i0 = pair * 2
                for u in range(2):
                    i = i0 + u
                    sp.wait_ge(s["h1_ready"], i)
                    nxt = (i0 * 2 + 2) if u == 0 else ((i0 * 2 + 4) % B)
                    load(nxt, 1 - u)
                    for b in range(2):
                        b_at = 2 * i + b
                        sp.wait_ge(s["h1_ready"], i + 1)
                        sp.dma_start(t["h1_dram"][b_at, NPATCH:N, :], h1[:, 2 * b, :]).then_inc(s["h1_out"], 16)
                        sp.dma_start(t["h1_dram"][b_at, 0:NPATCH, :], h1[0:NPATCH, 2 * b + 1, :]).then_inc(s["h1_out"], 16)
                    sp.wait_ge(s["xn_ready"], i + 1)
                    for b in range(2):
                        b_at = 2 * i + b
                        sp.dma_start(t["xn_dram"][b_at, NPATCH:N, :], xn[:, 2 * b, :]).then_inc(s["xn_out"], 16)
                        sp.dma_start(t["xn_dram"][b_at, 0:NPATCH, :], xn[0:NPATCH, 2 * b + 1, :]).then_inc(s["xn_out"], 16)
                    sp.wait_ge(s["xnT_ready"], i + 1)
                    for b in range(2):
                        sp.dma_start(t["xnT_dram"][2 * i + b, :, :, :].rearrange("c p n -> p c n"),
                                     xnT[:, :, b, :]).then_inc(s["xnT_out"], 16)
            sp.wait_ge(s["h1_out"], 64 * TURNS)
            sp.wait_ge(s["xn_out"], 64 * TURNS)
            sp.wait_ge(s["xnT_out"], 32 * TURNS)
            sp.wait_ge(s["in0"], 64 * (TURNS // 2 + 1))

        @block.gpsimd
        def _(pool):
            nc.gpsimd.memset(half[:, :], -0.5).then_inc(s["half_ready"], 1)
            pool.wait_ge(s["half_ready"], 1)
            with pool.Fori(0, TURNS) as i:
                pool.wait_ge(s["bn"], i + 1)
                pool.wait_ge(s["y_ready"], i)
                nc.gpsimd.tensor_tensor(rstd[:, :], mv[:, :, 1], half[:, 0:4], ALU.pow).then_inc(s["rstd_ready"], 1)
                pool.wait_ge(s["mv1_ready"], i + 1)
                nc.gpsimd.tensor_tensor(g[:, 2:4, :], g[:, 0:2, :],
                                        half[:, :].rearrange("p (a j) -> p a j", a=2), ALU.pow).then_inc(s["norm_ready"], 1)

        @block.vector
        def _(dve):
            ch = Chain(dve, s["chain"], s["passed"])
            dve.wait_ge(s["consts_in"], 13 * 16)
            for prm, inv, thr in ((prm_c, inv_c, thr_c), (prm_r, inv_r, thr_r)):
                ch.link(nc.vector.tensor_scalar(inv[:, :], prm[:, 4, :], LN_EPS, None, ALU.add))
                if prm is prm_c:
                    nc.vector.tensor_copy(prm[:, 4, :], inv[:, :]).then_inc(s["root"], 1)
                    dve.wait_ge(s["root"], 2)
                else:
                    nc.vector.tensor_copy(prm[:, 4, :], inv[:, :]).then_inc(s["root"], 1)
                    dve.wait_ge(s["root"], 4)
                ch.link(nc.vector.reciprocal(inv[:, :], prm[:, 4, :]))
                ch.link(nc.vector.tensor_tensor(inv[:, :], inv[:, :], prm[:, 1, :], ALU.mult))
                ch.link(nc.vector.tensor_tensor(thr[:, :], prm[:, 0, :], prm[:, 3, :], ALU.subtract))
                ch.link(nc.vector.tensor_tensor(thr[:, :], thr[:, :], inv[:, :], ALU.mult))
                ch.link(nc.vector.tensor_tensor(thr[:, :], thr[:, :], prm[:, 2, :], ALU.add))
                ch.link(nc.vector.tensor_scalar(thr[:, :], thr[:, :], -1.0, 2.0, ALU.mult, ALU.add))
            nc.vector.tensor_tensor(wrow[:, :, :], wrow[:, :, :],
                                    inv_c[:, :].unsqueeze(2).to_broadcast([DC, 8, D]), ALU.mult).then_inc(s["wrow_ready"], 1)
            with dve.Fori(0, TURNS // 2) as pair:
                i0 = pair * 2
                ch.start_loop(pair, 2 * 8)
                for u in range(2):
                    i = i0 + u
                    dve.wait_ge(s_in[u], pair * 64 + 64)
                    dve.wait_ge(s["rstd_ready"], i)
                    for j in range(4):
                        st = nc.vector.bn_stats(stats[:, j, :], h[:, u, j, :])
                    ch.link(st, apart=True)
                    for j in range(4):
                        st = nc.vector.bn_aggr(mv[:, j, :], stats[:, j, :])
                    ch.link(st)
                    nc.vector.tensor_scalar(mv[:, :, 1], mv[:, :, 1], LN_EPS, None, ALU.add).then_inc(s["bn"], 1)
                    dve.wait_ge(s["rstd_ready"], i + 1)
                    dve.wait_ge(s["yT_ps"], i)
                    for j in range(4):
                        st = nc.vector.tensor_scalar(y[:, j, :], h[:, u, j, :], mv[:, j, 0:1], rstd[:, j:j + 1],
                                                     ALU.subtract, ALU.mult)
                    st.then_inc(s["y_ready"], 1)
                    dve.wait_ge(s["q_ps"], i + 1)
                    dve.wait_ge(s["xa_ps"], i)
                    for c in range(2):
                        st = nc.vector.tensor_scalar(q[:, c, :, :], psum[0:DC, 2 + c, 0:2 * N].rearrange("p (b n) -> p b n", b=2),
                                                     thr_c[:, c:c + 1], None, ALU.is_ge)
                    st.then_inc(s["q_ready"], 1)
                    dve.wait_ge(s["kv_ps"], i + 1)
                    dve.wait_ge(s["kvh_ps"], i)
                    nc.vector.tensor_tensor(kv[:, :, :], psum[:, 4:8, 0:2 * D],
                                            thr_r[:, D:3 * D].unsqueeze(1).to_broadcast([128, 4, 2 * D]),
                                            ALU.is_ge).then_inc(s["kv_ready"], 1)
                    dve.wait_ge(s["kvh_ps"], i + 1)
                    for b in range(2):
                        st = nc.vector.tensor_tensor(kvh[:, b, :, :],
                                                     psum[0:DC, b, 0:2 * DC].rearrange("p (c e) -> p c e", c=2),
                                                     heads_mask[:, :].unsqueeze(1).to_broadcast([DC, 2, DC]), ALU.mult)
                    st.then_inc(s["kvh_ready"], 1)
                    dve.wait_ge(s["xa_ps"], i + 1)
                    dve.wait_ge(s["sp_ps"], i)
                    for c in range(2):
                        st = nc.vector.tensor_scalar(xs[:, c, :, :], psum[0:DC, 2 + c, 0:2 * N].rearrange("p (b n) -> p b n", b=2),
                                                     float(DH) ** -0.125, 1.0, ALU.mult, ALU.is_ge)
                    st.then_inc(s["xs_ready"], 1)
                    dve.wait_ge(s["sp_ps"], i + 1)
                    nc.vector.tensor_tensor(spike[:, :, :], psum[:, 4:8, 0:D],
                                            thr_r[:, 3 * D:4 * D].unsqueeze(1).to_broadcast([128, 4, D]),
                                            ALU.is_ge).then_inc(s["spike_ready"], 1)
                    dve.wait_ge(s["spike_ready"], i + 1)
                    dve.wait_ge(s["h1_out"], i * 64)
                    dve.wait_ge(s["xn_ready"], i)
                    nc.vector.tensor_tensor(h1[:, :, :], h[:, u, :, :], spike[:, :, :], ALU.add).then_inc(s["h1_ready"], 1)
                    dve.wait_ge(s["h1_ready"], i + 1)
                    dve.wait_ge(s["norm_ready"], i)
                    for j in range(4):
                        st = nc.vector.bn_stats(stats1[:, j, :], h1[:, j, :])
                    ch.link(st, apart=True)
                    for j in range(4):
                        st = nc.vector.bn_aggr(mv1[:, j, :], stats1[:, j, :])
                    ch.link(st)
                    ch.link(nc.vector.tensor_scalar(g[:, 0, :], mv1[:, :, 1], LN_EPS, None, ALU.add))
                    ch.link(nc.vector.reciprocal(g[:, 1, :], g[:, 0, :]))
                    ch.link(nc.vector.tensor_tensor(g[:, 1, :], g[:, 1, :], mv1[:, :, 1], ALU.mult))
                    nc.vector.tensor_scalar(g[:, 1, :], g[:, 1, :], float(D), 1e-24, ALU.mult, ALU.max).then_inc(s["mv1_ready"], 1)
                    dve.wait_ge(s["norm_ready"], i + 1)
                    ch.link(nc.vector.tensor_tensor(g[:, 4, :], g[:, 2, :], g[:, 3, :], ALU.mult))
                    dve.wait_ge(s["xn_out"], i * 64)
                    dve.wait_ge(s["xnT_ps"], i)
                    for j in range(4):
                        st = nc.vector.tensor_scalar(xn[:, j, :], h1[:, j, :], mv1[:, j, 0:1], g[:, 4, j:j + 1],
                                                     ALU.subtract, ALU.mult)
                    st.then_inc(s["xn_ready"], 1)

        @block.scalar
        def _(act):
            act.wait_ge(s["root"], 1)
            nc.scalar.activation(prm_c[:, 4, :], prm_c[:, 4, :], ACT.Sqrt).then_inc(s["root"], 1)
            act.wait_ge(s["root"], 3)
            nc.scalar.activation(prm_r[:, 4, :], prm_r[:, 4, :], ACT.Sqrt).then_inc(s["root"], 1)
            for c in range(2):
                act.wait_ge(s["w_turned"], c + 1)
                nc.scalar.copy(wT[:, c, :].rearrange("p (k o) -> p k o", k=2),
                               psum[0:DC, 2 * c:2 * c + 2, 0:4 * DC]).then_inc(s["w_out"], 1)
            with act.Fori(0, TURNS) as i:
                act.wait_ge(s["yT_ps"], i + 1)
                act.wait_ge(s["kv_ps"], i)
                nc.scalar.copy(yT[:, :, :, :], psum[0:DC, 0:2, 0:2 * N].rearrange("p c (b n) -> p c b n", b=2)).then_inc(s["yT_ready"], 1)
                act.wait_ge(s["xnT_ps"], i + 1)
                act.wait_ge(s["xnT_out"], i * 32)
                nc.scalar.copy(xnT[:, :, :, :], psum[0:DC, 0:2, 0:2 * N].rearrange("p c (b n) -> p c b n", b=2)).then_inc(s["xnT_ready"], 1)

        @block.tensor
        def _(pe):
            pe.wait_ge(s["wrow_ready"], 1)
            for c in range(2):
                for k in range(8):
                    mm = nc.tensor.transpose(psum[0:DC, 2 * c + k // 4, (k % 4) * DC:(k % 4) * DC + DC],
                                             wrow[:, k, c * DC:c * DC + DC], ident[0:DC, 0:DC])
                mm.then_inc(s["w_turned"], 1)
            pe.wait_ge(s["w_out"], 2)

            def turn(src):
                for c in range(2):
                    for b in range(2):
                        for tile in range(2):
                            rows, at = TILE_ROWS[tile], b * N + TILE_AT[tile]
                            mm = nc.tensor.transpose(psum[0:DC, c, at:at + rows],
                                                     src[0:rows, 2 * b + tile, c * DC:c * DC + DC], ident[0:rows, 0:rows])
                return mm

            with pe.Fori(0, TURNS) as i:
                pe.wait_ge(s["y_ready"], i + 1)
                pe.wait_ge(s["xnT_ready"], i)
                turn(y).then_inc(s["yT_ps"], 1)
                pe.wait_ge(s["yT_ready"], i + 1)
                pe.wait_ge(s["xs_ready"], i)
                for m in range(2):
                    for c in range(2):
                        mm = nc.tensor.matmul(psum[0:DC, 2 + m, 0:2 * N], wT[:, c, m * DC:m * DC + DC],
                                              yT[:, c, :, :], start=(c == 0), stop=(c == 1))
                mm.then_inc(s["q_ps"], 1)
                pe.wait_ge(s["spike_ready"], i)
                for j in range(4):
                    at = TILE_AT[j % 2]
                    for c in range(2):
                        mm = nc.tensor.matmul(psum[:, 4 + j, 0:2 * D], yT[:, c, j // 2, at:at + 128],
                                              wT[:, c, D:3 * D], start=(c == 0), stop=(c == 1))
                mm.then_inc(s["kv_ps"], 1)
                pe.wait_ge(s["kv_ready"], i + 1)
                for b in range(2):
                    for c in range(2):
                        for tile in range(2):
                            rows = TILE_ROWS[tile]
                            mm = nc.tensor.matmul(psum[0:DC, b, c * DC:c * DC + DC],
                                                  kv[0:rows, 2 * b + tile, c * DC:c * DC + DC],
                                                  kv[0:rows, 2 * b + tile, D + c * DC:D + c * DC + DC],
                                                  start=(tile == 0), stop=(tile == 1))
                mm.then_inc(s["kvh_ps"], 1)
                pe.wait_ge(s["kvh_ready"], i + 1)
                pe.wait_ge(s["q_ready"], i + 1)
                for b in range(2):
                    for c in range(2):
                        mm = nc.tensor.matmul(psum[0:DC, 2 + c, b * N:b * N + N], kvh[:, b, c, :], q[:, c, b, :],
                                              start=True, stop=True)
                mm.then_inc(s["xa_ps"], 1)
                pe.wait_ge(s["xs_ready"], i + 1)
                for j in range(4):
                    at = TILE_AT[j % 2]
                    for c in range(2):
                        mm = nc.tensor.matmul(psum[:, 4 + j, 0:D], xs[:, c, j // 2, at:at + 128],
                                              wT[:, c, 3 * D:4 * D], start=(c == 0), stop=(c == 1))
                mm.then_inc(s["sp_ps"], 1)
                pe.wait_ge(s["xn_ready"], i + 1)
                turn(xn).then_inc(s["xnT_ps"], 1)


def dispatch(nc, t, psum, slotsT):
    HALF = 512
    with ExitStack() as ctx:
        def sb(name, shape, dt=FP32):
            return ctx.enter_context(nc.sbuf_tensor("dsp_" + name, shape, dt))

        ident = sb("ident", [128, 128])
        ones = sb("ones", [DC, DC])
        phin = sb("phin", [DC, 2, SLOTS])
        scale = sb("scale", [DC, 1])
        xn = sb("xn", [128, 2, 2, D])
        xnT = sb("xnT", [DC, 2, 2, N])
        e = sb("e", [128, 2, 2, SLOTS])
        dw = sb("dw", [128, 2, 2, SLOTS])
        m = sb("m", [128, 2, E0])
        top = sb("top", [128, 2])
        mg = sb("mg", [128, 2, E0])
        se = sb("se", [128, 2, E0])
        rse = sb("rse", [128, 2, E0])
        sg = sb("sg", [128, 2, E0])
        z = sb("z", [128, 2])
        kc = sb("kc", [128, 2, 2, E0])
        cwT = sb("cwT", [128, NG, N])
        s = phase_sems(ctx, nc, "dsp", "consts_in ones_ready sq_ready norm_ps norm2 root phin_ready in0 in1 logits shifted mg_ready exped gexped "
                 "dw_ready kc_ready cw_ready slots_ps slots_out cwT_ps cwT_out cwT_stored chain")
        block = ctx.enter_context(nc.Block())
        s_in = (s["in0"], s["in1"])
        sq = dw[0:DC, 0, :, :]
        nrm = dw[0:DC, 1, 0, :]

        def run(eng, turn):
            turn(0, 0, 0)
            with eng.Fori(0, B // 2 - 1) as pair:
                turn(pair * 2 + 1, 1, pair)
                turn(pair * 2 + 2, 0, pair + 1)
            turn(B - 1, 1, B // 2 - 1)

        @block.sync
        def _(sp):
            sp.dma_start(ident[:, :], t["ident"]).then_inc(s["consts_in"], 16)
            sp.dma_start(phin[:, :, :], t["ffn_phi"].rearrange("(c p) e s -> p c (e s)", p=DC)).then_inc(s["consts_in"], 16)
            sp.dma_start(scale[:, :], row_bc(t["ffn_scale"], DC)).then_inc(s["consts_in"], 16)

            def load(b, u):
                sp.dma_start(xn[:, u, 0, :], t["xn_dram"][b, NPATCH:N, :]).then_inc(s_in[u], 16)
                sp.dma_start(xn[0:NPATCH, u, 1, :], t["xn_dram"][b, 0:NPATCH, :]).then_inc(s_in[u], 16)
                sp.dma_start(xnT[:, u, :, :], t["xnT_dram"][b, :, :, :].rearrange("c p n -> p c n")).then_inc(s_in[u], 16)

            def store(b):
                sp.wait_ge(s["cwT_out"], 3 * b + 3)
                sp.dma_start(t["cwT_dram"][b, :, :, :].rearrange("g p n -> p g n"), cwT[:, :, :]).then_inc(s["cwT_stored"], 16)

            load(0, 0)
            load(1, 1)
            with sp.Fori(0, B // 2 - 1) as pair:
                for u in range(2):
                    b = pair * 2 + u
                    sp.wait_ge(s["slots_ps"], 2 * b + 2)
                    load(b + 2, u)
                    store(b)
            store(B - 2)
            store(B - 1)
            sp.wait_ge(s["cwT_stored"], 16 * B)

        @block.vector
        def _(dve):
            ch = Chain(dve, s["chain"])
            nc.vector.memset(ones[:, :], 1.0).then_inc(s["ones_ready"], 1)
            dve.wait_ge(s["consts_in"], 48)
            nc.vector.tensor_tensor(sq, phin[:, :, :], phin[:, :, :], ALU.mult).then_inc(s["sq_ready"], 1)
            dve.wait_ge(s["norm_ps"], 1)
            nc.vector.tensor_scalar(nrm, psum[0:DC, 0:2, :].rearrange("p a b -> p (a b)"), 1e-24, None, ALU.max).then_inc(s["norm2"], 1)
            dve.wait_ge(s["root"], 1)
            ch.link(nc.vector.reciprocal(nrm, nrm))
            ch.link(nc.vector.tensor_scalar(nrm, nrm, scale[:, :], None, ALU.mult))
            nc.vector.tensor_tensor(phin[:, :, :], phin[:, :, :], nrm.unsqueeze(1).to_broadcast([DC, 2, SLOTS]),
                                    ALU.mult).then_inc(s["phin_ready"], 1)
            dve.wait_ge(s["phin_ready"], 1)
            LINKS = 6

            def turn(b, u, k):
                ch.base, ch.n = 3 - 1 + b * LINKS, 0
                lg = psum[:, 0:4, :].rearrange("p k (e s) -> p (k e) s", s=S0)
                dve.wait_ge(s["logits"], b + 1)
                ch.link(nc.vector.tensor_reduce(m[:, :, :].rearrange("p t e -> p (t e)"), lg, AXX, ALU.max))
                dve.wait_ge(s["gexped"], b)
                if not (isinstance(b, int) and b < 2):
                    dve.wait_ge(s["cwT_ps"], b - 1)
                nc.vector.tensor_tensor(e[:, u, :, :].rearrange("p t (e s) -> p (t e) s", s=S0), lg,
                                        m[:, :, :].rearrange("p t e -> p (t e)").unsqueeze(2).to_broadcast([128, 2 * E0, S0]),
                                        ALU.subtract).then_inc(s["shifted"], 1)
                ch.link(nc.vector.tensor_reduce(top[:, :], m[:, :, :], AXX, ALU.max))
                nc.vector.tensor_tensor(mg[:, :, :], m[:, :, :], top[:, :].unsqueeze(2).to_broadcast([128, 2, E0]),
                                        ALU.subtract).then_inc(s["mg_ready"], 1)
                dve.wait_ge(s["exped"], b + 1)
                ch.link(nc.vector.tensor_reduce(se[:, :, :].rearrange("p t e -> p (t e)"),
                                                e[:, u, :, :].rearrange("p t (e s) -> p (t e) s", s=S0), AXX, ALU.add))
                dve.wait_ge(s["gexped"], b + 1)
                nc.vector.reciprocal(rse[:, :, :], se[:, :, :])
                ch.link(nc.vector.tensor_tensor(sg[:, :, :], se[:, :, :], mg[:, :, :], ALU.mult))
                ch.link(nc.vector.tensor_reduce(z[:, :], sg[:, :, :], AXX, ALU.add))
                ch.link(nc.vector.reciprocal(z[:, :], z[:, :]))
                nc.vector.tensor_tensor(kc[:, u, :, :], mg[:, :, :], z[:, :].unsqueeze(2).to_broadcast([128, 2, E0]),
                                        ALU.mult).then_inc(s["kc_ready"], 1)
                if not (isinstance(b, int) and b < 2):
                    dve.wait_ge(s["slots_ps"], 2 * b - 2)
                nc.vector.tensor_tensor(dw[:, u, :, :].rearrange("p t (e s) -> p (t e) s", s=S0),
                                        e[:, u, :, :].rearrange("p t (e s) -> p (t e) s", s=S0),
                                        rse[:, :, :].rearrange("p t e -> p (t e)").unsqueeze(2).to_broadcast([128, 2 * E0, S0]),
                                        ALU.mult).then_inc(s["dw_ready"], 1)
                dve.wait_ge(s["dw_ready"], b + 1)
            run(dve, turn)

        @block.gpsimd
        def _(pool):
            def turn(b, u, k):
                pool.wait_ge(s["kc_ready"], b + 1)
                pool.wait_ge(s["dw_ready"], b + 1)
                for tile in range(2):
                    ev = e[:, u, tile, :].rearrange("p (e s) -> p e s", s=S0)
                    nc.gpsimd.tensor_tensor(ev, ev, kc[:, u, tile, :].unsqueeze(2).to_broadcast([128, E0, S0]),
                                            ALU.mult).then_inc(s["cw_ready"], 1)
            run(pool, turn)

        @block.scalar
        def _(act):
            act.wait_ge(s["norm2"], 1)
            nc.scalar.activation(nrm, nrm, ACT.Sqrt).then_inc(s["root"], 1)

            def softmax(b, u):
                act.wait_ge(s["shifted"], b + 1)
                nc.scalar.activation(e[:, u, :, :], e[:, u, :, :], ACT.Exp).then_inc(s["exped"], 1)
                act.wait_ge(s["mg_ready"], b + 1)
                nc.scalar.activation(mg[:, :, :], mg[:, :, :], ACT.Exp).then_inc(s["gexped"], 1)

            def evacuate(b, u):
                for c in range(2):
                    act.wait_ge(s["slots_ps"], 2 * b + c + 1)
                    nc.scalar.copy(slotsT[:, c, :, b, :],
                                   psum[0:DC, 4 + 2 * c:6 + 2 * c, :].rearrange("p k (e s) -> p (k e) s", s=S0)).then_inc(s["slots_out"], 1)
                act.wait_ge(s["cwT_ps"], b + 1)
                act.wait_ge(s["cwT_stored"], b * 16)
                for k in range(3):
                    n = min(3, NG - 3 * k)
                    nc.scalar.copy(cwT[:, 3 * k:3 * k + n, :],
                                   psum[:, 4 + k, 0:n * N].rearrange("p (g n) -> p g n", g=n)).then_inc(s["cwT_out"], 1)

            def turn(b, u, k):
                softmax(b, u)
                if not isinstance(b, int) or b:
                    evacuate(b - 1, 1 - u)
            run(act, turn)
            evacuate(B - 1, 1)

        @block.tensor
        def _(pe):
            pe.wait_ge(s["ones_ready"], 1)
            pe.wait_ge(s["sq_ready"], 1)
            for k in range(2):
                for c in range(2):
                    mm = nc.tensor.matmul(psum[0:DC, k, :], ones[:, :], sq[:, c, k * HALF:k * HALF + HALF],
                                          start=(c == 0), stop=(c == 1))
            mm.then_inc(s["norm_ps"], 1)
            pe.wait_ge(s["phin_ready"], 1)

            def logits(b, u, k):
                pe.wait_ge(s_in[u], 48 * k + 48)
                pe.wait_ge(s["shifted"], b)
                for tile in range(2):
                    at = TILE_AT[tile]
                    for k in range(2):
                        for c in range(2):
                            mm = nc.tensor.matmul(psum[:, 2 * tile + k, :], xnT[:, u, c, at:at + 128],
                                                  phin[:, c, k * HALF:k * HALF + HALF], start=(c == 0), stop=(c == 1))
                mm.then_inc(s["logits"], 1)

            def slots(b, u):
                pe.wait_ge(s["dw_ready"], b + 1)
                pe.wait_ge(s["cwT_out"], 3 * b)
                pe.wait_ge(s["slots_out"], 2 * b)
                for c in range(2):
                    for k in range(2):
                        for tile in range(2):
                            rows = TILE_ROWS[tile]
                            mm = nc.tensor.matmul(psum[0:DC, 4 + 2 * c + k, :], xn[0:rows, u, tile, c * DC:c * DC + DC],
                                                  dw[0:rows, u, tile, k * HALF:k * HALF + HALF],
                                                  start=(tile == 0), stop=(tile == 1))
                    mm.then_inc(s["slots_ps"], 1)
                pe.wait_ge(s["cw_ready"], 2 * b + 2)
                pe.wait_ge(s["slots_out"], 2 * b + 2)
                for g in range(NG):
                    for tile in range(2):
                        rows, at = TILE_ROWS[tile], (g % 3) * N + TILE_AT[tile]
                        mm = nc.tensor.transpose(psum[:, 4 + g // 3, at:at + rows],
                                                 e[0:rows, u, tile, 128 * g:128 * g + 128], ident[0:rows, 0:rows])
                mm.then_inc(s["cwT_ps"], 1)

            def turn(b, u, k):
                logits(b, u, k)
                if not isinstance(b, int) or b:
                    slots(b - 1, 1 - u)
            run(pe, turn)
            slots(B - 1, 1)


def soft_experts(nc, t, psum, slotsT):
    HJ = H0 // 128
    ROWS = B * S0
    with ExitStack() as ctx:
        def sb(name, shape, dt=FP32):
            return ctx.enter_context(nc.sbuf_tensor("exp_" + name, shape, dt))

        ident = sb("ident", [128, 128])
        b1rows = sb("b1rows", [DC, 2, 128])
        b1T = sb("b1T", [128, E0 * HJ])
        w1 = sb("w1", [DC, 2, 2, H0])
        w2 = sb("w2", [128, 2, HJ, D])
        b2 = sb("b2", [128, 2, D])
        hT = sb("hT", [128, 2, HJ, ROWS])
        eo = sb("eo", [128, 2, 4, D])
        s = phase_sems(ctx, nc, "exp", "consts_in b1_ps b1_ready w1_in0 w1_in1 w2_in0 w2_in1 h_ps h_ready o_ps o_ready0 o_ready1 stored0 stored1")
        block = ctx.enter_context(nc.Block())
        o_ready = (s["o_ready0"], s["o_ready1"])
        w1_in, w2_in, stored = (s["w1_in0"], s["w1_in1"]), (s["w2_in0"], s["w2_in1"]), (s["stored0"], s["stored1"])
        eo_view = t["eo_dram"].rearrange("(t q) k d -> q k t d", q=4)

        def run(eng, turn):
            turn(0, 0, 0, 0)
            with eng.Fori(0, E0 // 2 - 1) as pair:
                turn(pair * 2 + 1, 1, pair, pair)
                turn(pair * 2 + 2, 0, pair + 1, pair)
            turn(E0 - 1, 1, E0 // 2 - 1, E0 // 2 - 1)

        @block.sync
        def _(sp):
            sp.dma_start(ident[:, :], t["ident"]).then_inc(s["consts_in"], 16)
            sp.dma_start(b1rows[:, :, :], t["ffn_b1"].rearrange("(c e) (j p) -> (e j) c p", c=2, p=128)).then_inc(s["consts_in"], 16)

            def load(e, u):
                sp.dma_start(w1[:, u, :, :], t["ffn_w1"][e, :, :].rearrange("(c p) h -> p c h", p=DC)).then_inc(w1_in[u], 16)
                sp.dma_start(w2[:, u, :, :], t["ffn_w2"][e, :, :].rearrange("(j p) d -> p j d", p=128)).then_inc(w2_in[u], 16)
                sp.dma_start(b2[:, u, :], row_bc(t["ffn_b2"][e, :], 128)).then_inc(w2_in[u], 16)

            load(0, 0)
            load(1, 1)
            with sp.Fori(0, E0 // 2 - 1) as pair:
                for u in range(2):
                    e = pair * 2 + u
                    sp.wait_ge(s["o_ready0"], e + 1)
                    sp.wait_ge(s["o_ready1"], e + 1)
                    load(e + 2, u)

        @block.gpsimd
        def _(pool):
            def turn(e, u, k, before):
                pool.wait_ge(s["o_ready0"], e + 1)
                pool.wait_ge(s["o_ready1"], e + 1)
                for q in range(4):
                    pool.dma_start(eo_view[q, bass.ds(e * S0, S0), :, :], eo[S0 * q:S0 * q + S0, u, :, :]).then_inc(stored[u], 16)
            run(pool, turn)
            for u in range(2):
                pool.wait_ge(stored[u], 64 * (E0 // 2))

        @block.scalar
        def _(act):
            act.wait_ge(s["b1_ps"], 1)
            nc.scalar.copy(b1T[:, :], psum[:, 0, 0:E0 * HJ]).then_inc(s["b1_ready"], 1)
            act.wait_ge(s["b1_ready"], 1)

            def turn(e, u, k, before):
                if not (isinstance(e, int) and e < 2):
                    act.wait_ge(s["o_ps"], 2 * e - 2)
                for j in range(HJ):
                    act.wait_ge(s["h_ps"], HJ * e + j + 1)
                    nc.scalar.activation(hT[:, u, j, :], psum[:, j, :], ACT.Gelu,
                                         bias=b1T[:, bass.ds(e * HJ + j, 1)]).then_inc(s["h_ready"], 1)
            run(act, turn)

        @block.vector
        def _(dve):
            def turn(e, u, k, before):
                dve.wait_ge(w2_in[u], 32 * k + 32)
                dve.wait_ge(stored[u], 64 * k)
                for n in range(2):
                    dve.wait_ge(s["o_ps"], 2 * e + n + 1)
                    nc.vector.tensor_tensor(eo[:, u, 2 * n:2 * n + 2, :],
                                            psum[:, 6 + n, 0:2 * D].rearrange("p (a d) -> p a d", a=2),
                                            b2[:, u, :].unsqueeze(1).to_broadcast([128, 2, D]), ALU.add).then_inc(o_ready[n], 1)
            run(dve, turn)

        @block.tensor
        def _(pe):
            pe.wait_ge(s["consts_in"], 32)
            for c in range(2):
                mm = nc.tensor.transpose(psum[:, 0, c * DC:c * DC + DC], b1rows[:, c, :], ident[0:DC, 0:DC])
            mm.then_inc(s["b1_ps"], 1)
            pe.wait_ge(s["b1_ready"], 1)

            def hidden(e, u, k):
                pe.wait_ge(w1_in[u], 16 * k + 16)
                for j in range(HJ):
                    if not (isinstance(e, int) and e == 0):
                        pe.wait_ge(s["h_ready"], HJ * (e - 1) + j + 1)
                    for c in range(2):
                        mm = nc.tensor.matmul(psum[:, j, :], w1[:, u, c, 128 * j:128 * j + 128], slotsT[:, c, e, :, :],
                                              start=(c == 0), stop=(c == 1))
                    mm.then_inc(s["h_ps"], 1)

            def output(e, u, k):
                pe.wait_ge(w2_in[u], 32 * k + 32)
                pe.wait_ge(s["h_ready"], HJ * e + HJ)
                for n in range(2):
                    pe.wait_ge(o_ready[n], e)
                    for a in range(2):
                        for j in range(HJ):
                            at = 128 * (2 * n + a)
                            mm = nc.tensor.matmul(psum[:, 6 + n, a * D:a * D + D], hT[:, u, j, at:at + 128], w2[:, u, j, :],
                                                  start=(j == 0), stop=(j == HJ - 1))
                    mm.then_inc(s["o_ps"], 1)

            def turn(e, u, k, before):
                hidden(e, u, k)
                if not (isinstance(e, int) and e == 0):
                    output(e - 1, 1 - u, before)
            run(pe, turn)
            output(E0 - 1, 1, E0 // 2 - 1)


def soft_mixture(nc, t, psum):
    with nc.sbuf_tensor("slotsT", [DC, 2, E0, B, S0], FP32) as slotsT:
        dispatch(nc, t, psum, slotsT)
        soft_experts(nc, t, psum, slotsT)


def combine(nc, t, psum, th):
    RESO = 4 * HEADS
    with ExitStack() as ctx:
        def sb(name, shape, dt=FP32):
            return ctx.enter_context(nc.sbuf_tensor("cmb_" + name, shape, dt))

        ident = sb("ident", [128, 128])
        half = sb("half", [128, 2])
        lnw = sb("lnw", [DC, 2])
        wcomp = sb("wcomp", [DC, 2, 128])
        wreso = sb("wreso", [128, RESO])
        cw = sb("cw", [128, 2, NG, N])
        eo = sb("eo", [128, 2, NG, D])
        h1 = sb("h1", [128, 2, 2, D])
        h2 = sb("h2", [128, 2, D])
        stats = sb("stats", [128, 2, 6])
        mv = sb("mv", [128, 2, 2])
        g = sb("g", [128, 3, 2])
        r = sb("r", [128, 2, 2])
        y = sb("y", [128, 2, D])
        xr = sb("xr", [128, 2, D])
        xrT = sb("xrT", [DC, 2, N])
        lth = sb("lth", [128, N])
        lat = sb("lat", [128, N])
        s = phase_sems(ctx, nc, "cmb", "consts_in wcomp_ready half_ready in0 in1 comb_ps h2_ready var_ready r_ready y_ready y_stored h2_stored xr_ready "
                 "xrT_ps xrT_ready lat_ps lth_ready lat_ready lat_stored reso_ps th_ready chain passed")
        block = ctx.enter_context(nc.Block())
        s_in = (s["in0"], s["in1"])
        LOADS = 4 * 16

        def run(eng, turn):
            turn(0, 0, 0)
            with eng.Fori(0, B // 2 - 1) as pair:
                turn(pair * 2 + 1, 1, pair)
                turn(pair * 2 + 2, 0, pair + 1)
            turn(B - 1, 1, B // 2 - 1)

        @block.sync
        def _(sp):
            sp.dma_start(ident[:, :], t["ident"]).then_inc(s["consts_in"], 16)
            sp.dma_start(lnw[:, :], t["attn_ln_w"].rearrange("(c p) -> p c", p=DC), allow_slow_non_contiguous=True).then_inc(s["consts_in"], 16)
            sp.dma_start(wcomp[:, :, :], t["attn_w_comp"].rearrange("(c p) k -> p c k", p=DC)).then_inc(s["consts_in"], 16)
            sp.dma_start(wreso[:, :], t["attn_w_reso"]).then_inc(s["consts_in"], 16)

            def load(b, u):
                sp.dma_start(cw[:, u, :, :], t["cwT_dram"][b, :, :, :].rearrange("g p n -> p g n")).then_inc(s_in[u], 16)
                sp.dma_start(eo[:, u, :, :], t["eo_dram"][b, :, :].rearrange("(g p) d -> p g d", p=128)).then_inc(s_in[u], 16)
                for tile in range(2):
                    sp.dma_start(h1[:, u, tile, :], t["h1_dram"][b, TILE_AT[tile]:TILE_AT[tile] + 128, :]).then_inc(s_in[u], 16)

            def store(b):
                sp.wait_ge(s["h2_ready"], b + 1)
                sp.dma_start(t["h2_dram"][b, NPATCH:N, :], h2[:, 0, :]).then_inc(s["h2_stored"], 16)
                sp.dma_start(t["h2_dram"][b, 0:NPATCH, :], h2[0:NPATCH, 1, :]).then_inc(s["h2_stored"], 16)
                sp.wait_ge(s["y_ready"], b + 1)
                sp.dma_start(t["y3_dram"][b, NPATCH:N, :], y[:, 0, :]).then_inc(s["y_stored"], 16)
                sp.dma_start(t["y3_dram"][b, 0:NPATCH, :], y[0:NPATCH, 1, :]).then_inc(s["y_stored"], 16)
                sp.wait_ge(s["lat_ready"], b + 1)
                sp.dma_start(t["lat_dram"][b, :, :], lat[:, :]).then_inc(s["lat_stored"], 16)

            load(0, 0)
            load(1, 1)
            with sp.Fori(0, B // 2 - 1) as pair:
                for u in range(2):
                    b = pair * 2 + u
                    sp.wait_ge(s["h2_ready"], b + 1)
                    load(b + 2, u)
                    store(b)
            store(B - 2)
            store(B - 1)
            sp.wait_ge(s["h2_stored"], 32 * B)
            sp.wait_ge(s["y_stored"], 32 * B)
            sp.wait_ge(s["lat_stored"], 16 * B)

        @block.gpsimd
        def _(pool):
            nc.gpsimd.memset(half[:, :], -0.5).then_inc(s["half_ready"], 1)
            pool.wait_ge(s["half_ready"], 1)

            def turn(b, u, k):
                pool.wait_ge(s["var_ready"], b + 1)
                nc.gpsimd.tensor_tensor(r[:, :, :], g[:, 0:2, :], half[:, :].unsqueeze(1).to_broadcast([128, 2, 2]),
                                        ALU.pow).then_inc(s["r_ready"], 1)
            run(pool, turn)

        @block.vector
        def _(dve):
            ch = Chain(dve, s["chain"], s["passed"])
            dve.wait_ge(s["consts_in"], 64)
            nc.vector.tensor_tensor(wcomp[:, :, :], wcomp[:, :, :], lnw[:, :].unsqueeze(2).to_broadcast([DC, 2, 128]),
                                    ALU.mult).then_inc(s["wcomp_ready"], 1)
            LINKS = 5

            def turn(b, u, k):
                ch.base, ch.n = b * LINKS, 0
                dve.wait_ge(s_in[u], LOADS * k + LOADS)
                dve.wait_ge(s["comb_ps"], b + 1)
                dve.wait_ge(s["h2_stored"], 32 * b)
                nc.vector.tensor_tensor(h2[:, :, :], psum[:, 0:2, 0:D], h1[:, u, :, :], ALU.add).then_inc(s["h2_ready"], 1)
                dve.wait_ge(s["h2_ready"], b + 1)
                for j in range(2):
                    st = nc.vector.bn_stats(stats[:, j, :], h2[:, j, :])
                ch.link(st, apart=True)
                for j in range(2):
                    st = nc.vector.bn_aggr(mv[:, j, :], stats[:, j, :])
                ch.link(st)
                dve.wait_ge(s["r_ready"], b)
                dve.wait_ge(s["xr_ready"], b)
                ch.link(nc.vector.tensor_scalar(g[:, 0, :], mv[:, :, 1], LN_EPS, None, ALU.add))
                ch.link(nc.vector.reciprocal(g[:, 2, :], g[:, 0, :]))
                ch.link(nc.vector.tensor_tensor(g[:, 2, :], g[:, 2, :], mv[:, :, 1], ALU.mult))
                nc.vector.tensor_scalar(g[:, 1, :], g[:, 2, :], RMS_EPS, None, ALU.add).then_inc(s["var_ready"], 1)
                dve.wait_ge(s["r_ready"], b + 1)
                dve.wait_ge(s["y_stored"], 32 * b)
                for j in range(2):
                    st = nc.vector.tensor_scalar(y[:, j, :], h2[:, j, :], mv[:, j, 0:1], r[:, 0, j:j + 1],
                                                 ALU.subtract, ALU.mult)
                st.then_inc(s["y_ready"], 1)
                dve.wait_ge(s["y_ready"], b + 1)
                dve.wait_ge(s["xrT_ps"], b)
                for j in range(2):
                    st = nc.vector.tensor_scalar(xr[:, j, :], y[:, j, :], r[:, 1, j:j + 1], None, ALU.mult)
                st.then_inc(s["xr_ready"], 1)
                dve.wait_ge(s["lth_ready"], b + 1)
                dve.wait_ge(s["lat_stored"], 16 * b)
                dve.wait_ge(s["reso_ps"], b)
                nc.vector.scalar_tensor_tensor(lat[:, :], lth[:, :], 1.0, psum[:, 4, 0:N], ALU.add, ALU.mult).then_inc(s["lat_ready"], 1)
            run(dve, turn)

        @block.scalar
        def _(act):
            def turn(b, u, k):
                act.wait_ge(s["xrT_ps"], b + 1)
                act.wait_ge(s["lat_ps"], b)
                nc.scalar.copy(xrT[:, :, :], psum[0:DC, 2:4, 0:N]).then_inc(s["xrT_ready"], 1)
                act.wait_ge(s["lat_ps"], b + 1)
                act.wait_ge(s["lat_ready"], b)
                nc.scalar.activation(lth[:, :], psum[:, 4, 0:N], ACT.Tanh, scale=0.5).then_inc(s["lth_ready"], 1)
                act.wait_ge(s["reso_ps"], b + 1)
                nc.scalar.activation(th[:, b, :, :], psum[:, 5, 0:2 * RESO].rearrange("p (t k) -> p t k", t=2),
                                     ACT.Tanh, scale=0.25).then_inc(s["th_ready"], 1)
            run(act, turn)

        @block.tensor
        def _(pe):
            pe.wait_ge(s["consts_in"], 64)

            def product(b, u, k):
                pe.wait_ge(s_in[u], LOADS * k + LOADS)
                pe.wait_ge(s["h2_ready"], b)
                for tile in range(2):
                    at = TILE_AT[tile]
                    for n in range(NG):
                        mm = nc.tensor.matmul(psum[:, tile, 0:D], cw[:, u, n, at:at + 128], eo[:, u, n, :],
                                              start=(n == 0), stop=(n == NG - 1))
                mm.then_inc(s["comb_ps"], 1)

            def latent(b):
                pe.wait_ge(s["xr_ready"], b + 1)
                pe.wait_ge(s["xrT_ready"], b)
                for c in range(2):
                    for tile in range(2):
                        rows, at = TILE_ROWS[tile], TILE_AT[tile]
                        mm = nc.tensor.transpose(psum[0:DC, 2 + c, at:at + rows], xr[0:rows, tile, c * DC:c * DC + DC],
                                                 ident[0:rows, 0:rows])
                mm.then_inc(s["xrT_ps"], 1)
                pe.wait_ge(s["xrT_ready"], b + 1)
                pe.wait_ge(s["lat_ready"], b)
                pe.wait_ge(s["wcomp_ready"], 1)
                for c in range(2):
                    mm = nc.tensor.matmul(psum[:, 4, 0:N], wcomp[:, c, :], xrT[:, c, :], start=(c == 0), stop=(c == 1))
                mm.then_inc(s["lat_ps"], 1)
                pe.wait_ge(s["lat_ready"], b + 1)
                pe.wait_ge(s["th_ready"], b)
                for tile in range(2):
                    at = TILE_AT[tile]
                    mm = nc.tensor.matmul(psum[:, 5, tile * RESO:tile * RESO + RESO], lat[:, at:at + 128], wreso[:, :],
                                          start=True, stop=True)
                mm.then_inc(s["reso_ps"], 1)

            def turn(b, u, k):
                product(b, u, k)
                if not (isinstance(b, int) and b == 0):
                    latent(b - 1)
            run(pe, turn)
            latent(B - 1)


def gates(nc, t, psum, th, vgate, decay):
    A = 2 * B
    PI = 3.141592653589793
    with ExitStack() as ctx:
        def sb(name, shape, dt=FP32):
            return ctx.enter_context(nc.sbuf_tensor("gat_" + name, shape, dt))

        hd = sb("hd", [128, HEADS])
        temp = sb("temp", [128, 1])
        pos = sb("pos", [128, 2])
        rate = sb("rate", [128, HEADS])
        ln = sb("ln", [128, HEADS])
        dt = sb("dt", [128, HEADS])
        rdf = sb("rdf", [128, 2, HEADS])
        z = sb("z", [128, A, HEADS])
        w = sb("w", [128, A, HEADS])
        p = sb("p", [128, A, HEADS])
        s = phase_sems(ctx, nc, "gat", "in_ sig ln_ready rate_ready df_arg df_ready arg arg_th chain")
        block = ctx.enter_context(nc.Block())
        q4 = th[:, :, :, :].rearrange("p b t (h k) -> p (b t) h k", k=4)

        @block.sync
        def _(sp):
            sp.dma_start(hd[:, :], row_bc(t["attn_head_decay"], 128)).then_inc(s["in_"], 16)
            sp.dma_start(temp[:, :], row_bc(t["attn_temperature"], 128)).then_inc(s["in_"], 16)
            sp.dma_start(pos[:, :], t["pos"]).then_inc(s["in_"], 16)

        @block.scalar
        def _(act):
            act.wait_ge(s["in_"], 48)
            nc.scalar.activation(rate[:, :], hd[:, :], ACT.Tanh, scale=0.5).then_inc(s["sig"], 1)
            act.wait_ge(s["rate_ready"], 1)
            nc.scalar.activation(ln[:, :], rate[:, :], ACT.Ln).then_inc(s["ln_ready"], 1)
            act.wait_ge(s["df_arg"], 1)
            nc.scalar.activation(decay[:, :, :], decay[:, :, :], ACT.Exp).then_inc(s["df_ready"], 1)
            act.wait_ge(s["arg"], 1)
            nc.scalar.activation(p[:, :, :], p[:, :, :], ACT.Tanh, scale=0.5).then_inc(s["arg_th"], 1)

        @block.vector
        def _(dve):
            ch = Chain(dve, s["chain"])
            dve.wait_ge(s["in_"], 48)
            dve.wait_ge(s["sig"], 1)
            ch.link(nc.vector.tensor_scalar(rate[:, :], rate[:, :], 0.65 / 2, 0.3 + 0.65 / 2, ALU.mult, ALU.add))
            nc.vector.tensor_scalar(rate[:, :], rate[:, :], 1e-5, 0.999, ALU.max, ALU.min).then_inc(s["rate_ready"], 1)
            dve.wait_ge(s["rate_ready"], 1)
            ch.link(nc.vector.tensor_scalar(dt[:, :], rate[:, :], -1.0, 1.0, ALU.mult, ALU.add))
            dve.wait_ge(s["ln_ready"], 1)
            for tile in range(2):
                st = nc.vector.tensor_scalar(decay[:, tile, :], ln[:, :], pos[:, tile:tile + 1], None, ALU.mult)
            st.then_inc(s["df_arg"], 1)
            ch.link(nc.vector.tensor_tensor(z[:, :, :], q4[:, :, :, 1], q4[:, :, :, 3], ALU.subtract))
            ch.link(nc.vector.tensor_scalar(z[:, :, :], z[:, :, :], PI / 4, None, ALU.mult))
            ch.link(nc.vector.tensor_tensor(w[:, :, :], z[:, :, :], z[:, :, :], ALU.mult))
            ch.link(nc.vector.tensor_scalar(p[:, :, :], w[:, :, :], 1 / 6227020800.0, None, ALU.mult))
            for c in (-1 / 39916800.0, 1 / 362880.0, -1 / 5040.0, 1 / 120.0, -1 / 6.0):
                ch.link(nc.vector.scalar_tensor_tensor(p[:, :, :], p[:, :, :], c, w[:, :, :], ALU.add, ALU.mult))
            ch.link(nc.vector.scalar_tensor_tensor(p[:, :, :], p[:, :, :], 1.0, z[:, :, :], ALU.add, ALU.mult))
            ch.link(nc.vector.tensor_tensor(p[:, :, :], p[:, :, :], p[:, :, :], ALU.mult))
            ch.link(nc.vector.tensor_scalar(p[:, :, :], p[:, :, :], -2.0, 1.0, ALU.mult, ALU.add))
            for k in (0, 2):
                ch.link(nc.vector.tensor_scalar(w[:, :, :], q4[:, :, :, k], 0.5, 0.5, ALU.mult, ALU.add))
                ch.link(nc.vector.tensor_tensor(p[:, :, :], p[:, :, :], w[:, :, :], ALU.mult))
            nc.vector.tensor_scalar(p[:, :, :], p[:, :, :], temp[:, :], None, ALU.mult).then_inc(s["arg"], 1)
            dve.wait_ge(s["df_ready"], 1)
            ch.link(nc.vector.tensor_scalar(rdf[:, :, :], decay[:, :, :], 1e-8, None, ALU.add))
            ch.link(nc.vector.reciprocal(rdf[:, :, :], rdf[:, :, :]))
            ch.link(nc.vector.tensor_tensor(rdf[:, :, :], rdf[:, :, :], dt[:, :].unsqueeze(1).to_broadcast([128, 2, HEADS]), ALU.mult))
            dve.wait_ge(s["arg_th"], 1)
            ch.link(nc.vector.tensor_scalar(p[:, :, :], p[:, :, :], 0.6, 0.5, ALU.mult, ALU.add))
            ch.link(nc.vector.tensor_scalar(p[:, :, :], p[:, :, :], 0.05, 0.95, ALU.max, ALU.min))
            for tile in range(2):
                ch.link(nc.vector.tensor_tensor(vgate[:, 0:B, tile, :],
                                                p[:, :, :].rearrange("p (b t) h -> p b t h", t=2)[:, :, tile, :],
                                                rdf[:, tile, :].unsqueeze(1).to_broadcast([128, B, HEADS]), ALU.mult))
            ch.link(nc.vector.tensor_copy(vgate[:, B, :, :], rdf[:, :, :]))


def decay_attention(nc, t, psum, vgate, decay):
    V0, OG0 = 0, D
    with ExitStack() as ctx:
        def sb(name, shape, dt=FP32):
            return ctx.enter_context(nc.sbuf_tensor("dec_" + name, shape, dt))

        ident = sb("ident", [128, 128])
        half = sb("half", [128, 2 * 2 * HEADS])
        causal = sb("causal", [128, 128])
        causal_p = sb("causal_p", [NPATCH, N])
        cosw = sb("cosw", [128, 2, 2, DH])
        sinw = sb("sinw", [128, 2, 2, DH])
        nw = sb("nw", [128, 2, DH])
        nwx = sb("nwx", [128, 2, DH])
        wqkv = sb("wqkv", [128, 3 * D])
        wog = sb("wog", [128, D])
        memn = sb("memn", [DC, 2])
        wproj = sb("wproj", [DC, 2, D])
        lat = sb("lat", [128, 2, N])
        y3 = sb("y3", [128, 2, 2, D])
        qk = sb("qk", [128, 2, 2 * D])
        vo = sb("vo", [128, 2, 2 * D])
        sq = sb("sq", [128, 2, 2 * D])
        ms = sb("ms", [128, 4 * HEADS])
        rq = sb("rq", [128, 4 * HEADS])
        qa = sb("qa", [128, 2, 2 * D])
        qb = sb("qb", [128, 2, 2 * D])
        qe = sb("qe", [128, 2, 2 * D])
        qkf = sb("qkf", [128, 2, 2 * HEADS, 32])
        qkT = sb("qkT", [128, 2, 3, N])
        ogt = sb("ogt", [128, 2, D])
        og = sb("og", [128, 2, 2, D])
        vg = sb("vg", [128, 2, 2, HEADS, DH + 1])
        at_ = sb("at", [128, 2, 4, 128])
        ap_ = sb("ap", [NPATCH, 2, 4, N])
        den = sb("den", [128, 2, HEADS])
        o = sb("o", [128, 2, D])
        osq = sb("osq", [128, D])
        oss = sb("oss", [128, 2])
        ro = sb("ro", [128, 2])
        oT = sb("oT", [DC, 2, N])
        x2 = sb("x2", [128, 2, D])
        s = phase_sems(ctx, nc, "dec", "consts_in half_ready wproj_ready tables_ready zeroed in0 in1 y_in0 y_in1 wl_ps qk_out vo_out sq_ready ms_ready rq_ready "
                 "qn_ready qb_ready qm_ready qe_ready qkf_ready turned qkT_ready ogt_ready og_ready vg_ready sc_ps masked av0 o_ps "
                 "o_ready oss_ready mso_ready ro_ready oT_ps oT_ready pr_ps x2_ready x2_stored chain")
        block = ctx.enter_context(nc.Block())
        s_in, y_in = (s["in0"], s["in1"]), (s["y_in0"], s["y_in1"])

        def run(eng, turn):
            turn(0, 0, 0, 0)
            with eng.Fori(0, B // 2 - 1) as pair:
                turn(pair * 2 + 1, 1, pair, pair)
                turn(pair * 2 + 2, 0, pair + 1, pair)
            turn(B - 1, 1, B // 2 - 1, B // 2 - 1)

        def first(b):
            return isinstance(b, int) and b == 0

        @block.sync
        def _(sp):
            for dst, src in ((ident[:, :], t["ident"]), (causal[:, :], t["causal"]), (causal_p[:, :], t["causal_p"]),
                             (cosw[:, :, 0, :], t["cos"]), (cosw[:, :, 1, :], t["cos"]), (sinw[:, :, 0, :], t["sin"]), (sinw[:, :, 1, :], t["sin"]),
                             (wqkv[:, :], t["attn_w_qkv"]), (wog[:, :], t["attn_w_outgate"]),
                             (wproj[:, :, :], t["attn_w_proj"].rearrange("(c p) k -> p c k", p=DC))):
                sp.dma_start(dst, src).then_inc(s["consts_in"], 16)
            for n, wn in enumerate((t["attn_qn_w"], t["attn_kn_w"])):
                sp.dma_start(nw[:, n, :], row_bc(wn, 128)).then_inc(s["consts_in"], 16)
                for k in range(2):
                    sp.dma_start(nwx[:, n, 8 * k:8 * k + 8], row_bc(wn[8 - 8 * k:16 - 8 * k], 128)).then_inc(s["consts_in"], 16)
            sp.dma_start(memn[:, :], t["attn_memn_w"].rearrange("(c p) -> p c", p=DC), allow_slow_non_contiguous=True).then_inc(s["consts_in"], 16)

            def load_lat(b, u):
                sp.dma_start(lat[:, u, :], t["lat_dram"][b, :, :]).then_inc(s_in[u], 16)

            def load_y(b, u):
                for tile in range(2):
                    sp.dma_start(y3[:, u, tile, :], t["y3_dram"][b, TILE_AT[tile]:TILE_AT[tile] + 128, :]).then_inc(y_in[u], 16)

            def store(b):
                sp.wait_ge(s["x2_ready"], b + 1)
                sp.dma_start(t["x2_dram"][b, NPATCH:N, :], x2[:, 0, :]).then_inc(s["x2_stored"], 16)
                sp.dma_start(t["x2_dram"][b, 0:NPATCH, :], x2[0:NPATCH, 1, :]).then_inc(s["x2_stored"], 16)

            for u in range(2):
                load_lat(u, u)
                load_y(u, u)
            with sp.Fori(0, B // 2 - 1) as pair:
                for u in range(2):
                    b = pair * 2 + u
                    sp.wait_ge(s["wl_ps"], 2 * b + 2)
                    load_lat(b + 2, u)
                    store(b)
                    load_y(b + 2, u)
            store(B - 2)
            store(B - 1)
            sp.wait_ge(s["x2_stored"], 32 * B)

        @block.gpsimd
        def _(pool):
            nc.gpsimd.memset(half[:, :], -0.5).then_inc(s["half_ready"], 1)
            pool.wait_ge(s["half_ready"], 1)
            pool.wait_ge(s["tables_ready"], 1)

            def front(b):
                pool.wait_ge(s["ms_ready"], b + 1)
                pool.wait_ge(s["qn_ready"], b)
                nc.gpsimd.tensor_tensor(rq[:, :], ms[:, :], half[:, :], ALU.pow).then_inc(s["rq_ready"], 1)
                pool.wait_ge(s["qn_ready"], b + 1)
                pool.wait_ge(s["qm_ready"], b)
                for tile in range(2):
                    for k in range(2):
                        src = qa[:, tile, :].rearrange("p (a h d) -> p a h d", a=2, d=DH)[:, :, :, 8 - 8 * k:16 - 8 * k]
                        dst = qb[:, tile, :].rearrange("p (a h d) -> p a h d", a=2, d=DH)[:, :, :, 8 * k:8 * k + 8]
                        for a in range(2):
                            st = nc.gpsimd.tensor_tensor(dst[:, a, :, :], src[:, a, :, :],
                                                         sinw[:, tile, a, 8 * k:8 * k + 8].unsqueeze(1).to_broadcast([128, HEADS, 8]), ALU.mult)
                st.then_inc(s["qb_ready"], 1)

            def back(b):
                pool.wait_ge(s["mso_ready"], b + 1)
                pool.wait_ge(s["x2_ready"], b)
                nc.gpsimd.tensor_tensor(ro[:, :], oss[:, :], half[:, 0:2], ALU.pow).then_inc(s["ro_ready"], 1)

            def turn(b, u, k, before):
                front(b)
                if not first(b):
                    back(b - 1)
            run(pool, turn)
            back(B - 1)

        @block.vector
        def _(dve):
            ch = Chain(dve, s["chain"])
            nc.vector.memset(qkf[:, :, :, :], 0.0).then_inc(s["zeroed"], 1)
            for u in range(2):
                ch.link(nc.vector.tensor_copy(vg[:, u, :, :, DH], vgate[:, B, :, :]))
            dve.wait_ge(s["consts_in"], 17 * 16)
            nc.vector.tensor_tensor(wproj[:, :, :], wproj[:, :, :], memn[:, :].unsqueeze(2).to_broadcast([DC, 2, D]),
                                    ALU.mult).then_inc(s["wproj_ready"], 1)
            for tile in range(2):
                nc.vector.tensor_tensor(cosw[:, tile, :, :], cosw[:, tile, :, :], nw[:, :, :], ALU.mult)
                st = nc.vector.tensor_tensor(sinw[:, tile, :, :], sinw[:, tile, :, :], nwx[:, :, :], ALU.mult)
            st.then_inc(s["tables_ready"], 1)
            dve.wait_ge(s["tables_ready"], 1)
            dve.wait_ge(s["zeroed"], 1)
            SETUP = ch.n
            LINKS = 8

            def heads(x):
                return x.rearrange("p t (h d) -> p (t h) d", d=DH)

            def front1(b, u):
                dve.wait_ge(s["sq_ready"], b + 1)
                ch.link(nc.vector.tensor_reduce(ms[:, :], heads(sq[:, :, :]), AXX, ALU.add))
                nc.vector.tensor_scalar(ms[:, :], ms[:, :], 1.0 / DH, RMS_EPS, ALU.mult, ALU.add).then_inc(s["ms_ready"], 1)
                dve.wait_ge(s["vo_out"], 2 * b + 2)
                if not (isinstance(b, int) and b < 2):
                    dve.wait_ge(s["o_ps"], b - 1)
                for tile in range(2):
                    st = nc.vector.tensor_tensor(vg[:, u, tile, :, 0:DH], vo[:, tile, 0:D].rearrange("p (h d) -> p h d", d=DH),
                                                 vgate[:, b, tile, :].unsqueeze(2).to_broadcast([128, HEADS, DH]), ALU.mult)
                st.then_inc(s["vg_ready"], 1)
                dve.wait_ge(s["rq_ready"], b + 1)
                nc.vector.tensor_tensor(heads(qa[:, :, :]), heads(qk[:, :, :]),
                                        rq[:, :].unsqueeze(2).to_broadcast([128, 4 * HEADS, DH]), ALU.mult).then_inc(s["qn_ready"], 1)

            def front2(b, u):
                dve.wait_ge(s["qn_ready"], b + 1)
                dve.wait_ge(s["qb_ready"], b + 1)
                for tile in range(2):
                    for a in range(2):
                        st = nc.vector.tensor_tensor(qa[:, tile, a * D:a * D + D].rearrange("p (h d) -> p h d", d=DH),
                                                     qa[:, tile, a * D:a * D + D].rearrange("p (h d) -> p h d", d=DH),
                                                     cosw[:, tile, a, :].unsqueeze(1).to_broadcast([128, HEADS, DH]), ALU.mult)
                ch.link(st)
                ch.link(nc.vector.tensor_tensor(qa[:, :, :], qa[:, :, :], qb[:, :, :], ALU.add))
                nc.vector.tensor_scalar(qe[:, :, :], qa[:, :, :], 0.0, None, ALU.min).then_inc(s["qm_ready"], 1)

            def front3(b, u):
                dve.wait_ge(s["qe_ready"], b + 1)
                dve.wait_ge(s["turned"], b)
                for tile in range(2):
                    st = nc.vector.scalar_tensor_tensor(qkf[:, tile, :, 0:DH], qa[:, tile, :].rearrange("p (h d) -> p h d", d=DH), 0.0,
                                                        qe[:, tile, :].rearrange("p (h d) -> p h d", d=DH), ALU.max, ALU.add)
                st.then_inc(s["qkf_ready"], 1)
                dve.wait_ge(s["ogt_ready"], b + 1)
                nc.vector.scalar_tensor_tensor(og[:, u, :, :], ogt[:, :, :], 1.0, vo[:, :, D:2 * D], ALU.add, ALU.mult).then_inc(s["og_ready"], 1)

            def mask(b, g):
                n = g % 2
                dve.wait_ge(s["sc_ps"], 3 * b + g + 1)
                if g >= 2:
                    dve.wait_ge(s["o_ps"], b)
                    dve.wait_ge(s["av0"], b + 1)
                else:
                    dve.wait_ge(s["o_ps"], b)
                nc.vector.tensor_tensor(at_[:, n, :, :], psum[:, 4:8, 0:128],
                                        causal[:, :].unsqueeze(1).to_broadcast([128, 4, 128]), ALU.mult)
                nc.vector.tensor_tensor(ap_[:, n, :, :], psum[0:NPATCH, 4:8, 128:128 + N],
                                        causal_p[:, :].unsqueeze(1).to_broadcast([NPATCH, 4, N]), ALU.mult).then_inc(s["masked"], 1)

            def post(b, u, k):
                dve.wait_ge(s["o_ps"], b + 1)
                dve.wait_ge(s["oT_ps"], b)
                dve.wait_ge(s["oss_ready"], 2 * b)
                acc = psum[:, 1:4:2, 0:HEADS * (DH + 1)].rearrange("p t (h d) -> p t h d", d=DH + 1)
                ch.link(nc.vector.tensor_tensor(den[:, :, :], acc[:, :, :, DH], decay[:, :, :], ALU.mult))
                ch.link(nc.vector.tensor_scalar(den[:, :, :], den[:, :, :], 1e-5, None, ALU.max))
                ch.link(nc.vector.reciprocal(den[:, :, :], den[:, :, :]))
                ch.link(nc.vector.tensor_tensor(den[:, :, :], den[:, :, :], decay[:, :, :], ALU.mult))
                for tile in range(2):
                    st = nc.vector.tensor_tensor(o[:, tile, :].rearrange("p (h d) -> p h d", d=DH), acc[:, tile, :, 0:DH],
                                                 den[:, tile, :].unsqueeze(2).to_broadcast([128, HEADS, DH]), ALU.mult)
                st.then_inc(s["o_ready"], 1)
                dve.wait_ge(s["oss_ready"], 2 * b + 2)
                dve.wait_ge(s["ro_ready"], b)
                nc.vector.tensor_scalar(oss[:, :], oss[:, :], 4.0 / D, 4.0 * RMS_EPS, ALU.mult, ALU.add).then_inc(s["mso_ready"], 1)
                dve.wait_ge(s["pr_ps"], b + 1)
                dve.wait_ge(s["ro_ready"], b + 1)
                dve.wait_ge(y_in[u], 32 * k + 32)
                dve.wait_ge(s["x2_stored"], 32 * b)
                dve.wait_ge(s["og_ready"], b + 1)
                for tile in range(2):
                    st = nc.vector.scalar_tensor_tensor(x2[:, tile, :], psum[:, 2, tile * D:tile * D + D], ro[:, tile:tile + 1],
                                                        og[:, u, tile, :], ALU.mult, ALU.mult)
                ch.link(st)
                nc.vector.tensor_tensor(x2[:, :, :], x2[:, :, :], y3[:, u, :, :], ALU.add).then_inc(s["x2_ready"], 1)

            def turn(b, u, k, before):
                if first(b):
                    ch.base, ch.n = SETUP, 0
                    front1(b, u), front2(b, u), front3(b, u)
                else:
                    ch.base, ch.n = SETUP + 3 + (b - 1) * LINKS, 0
                    mask(b - 1, 0)
                    front1(b, u)
                    mask(b - 1, 1)
                    front2(b, u)
                    mask(b - 1, 2)
                    front3(b, u)
                    post(b - 1, 1 - u, before)
            run(dve, turn)
            ch.base, ch.n = SETUP + 3 + (B - 1) * LINKS, 0
            for g in range(3):
                mask(B - 1, g)
            post(B - 1, 1, B // 2 - 1)

        @block.scalar
        def _(act):
            def back1(b):
                act.wait_ge(s["turned"], b + 1)
                act.wait_ge(s["sc_ps"], 3 * b)
                nc.scalar.copy(qkT[:, :, :, :], psum[:, 0:3:2, 0:3 * N].rearrange("p a (g n) -> p a g n", g=3)).then_inc(s["qkT_ready"], 1)

            def back2(b):
                act.wait_ge(s["o_ready"], b + 1)
                act.wait_ge(s["mso_ready"], b)
                act.wait_ge(s["ro_ready"], b)
                for tile in range(2):
                    act.wait_ge(s["oss_ready"], 2 * b + tile)
                    nc.scalar.activation(osq[:, :], o[:, tile, :], ACT.Square, accum_out=oss[:, tile:tile + 1]).then_inc(s["oss_ready"], 1)
                act.wait_ge(s["oT_ps"], b + 1)
                act.wait_ge(s["pr_ps"], b)
                nc.scalar.copy(oT[:, :, :], psum[0:DC, 0, 0:2 * N].rearrange("p (c n) -> p c n", c=2)).then_inc(s["oT_ready"], 1)

            def front_a(b):
                for tile in range(2):
                    act.wait_ge(s["wl_ps"], 2 * b + tile + 1)
                    act.wait_ge(s["qn_ready"], b)
                    act.wait_ge(s["sq_ready"], b)
                    act.wait_ge(s["vg_ready"], b)
                    act.wait_ge(s["og_ready"], b)
                    nc.scalar.mul(qk[:, tile, :], psum[:, 2 * tile, 0:2 * D], 0.5).then_inc(s["qk_out"], 1)
                    nc.scalar.mul(vo[:, tile, :], psum[:, 2 * tile + 1, 0:2 * D], 0.5).then_inc(s["vo_out"], 1)

            def front_b(b):
                act.wait_ge(s["qk_out"], 2 * b + 2)
                act.wait_ge(s["ms_ready"], b)
                nc.scalar.activation(sq[:, :, :], qk[:, :, :], ACT.Square).then_inc(s["sq_ready"], 1)
                act.wait_ge(s["vo_out"], 2 * b + 2)
                act.wait_ge(s["og_ready"], b)
                nc.scalar.activation(ogt[:, :, :], vo[:, :, D:2 * D], ACT.Tanh, scale=0.5).then_inc(s["ogt_ready"], 1)

            def front_c(b):
                act.wait_ge(s["qm_ready"], b + 1)
                nc.scalar.activation(qe[:, :, :], qe[:, :, :], ACT.Exp).then_inc(s["qe_ready"], 1)

            def turn(b, u, k, before):
                front_a(b)
                if not first(b):
                    back1(b - 1)
                front_b(b)
                front_c(b)
                if not first(b):
                    back2(b - 1)
            run(act, turn)
            back1(B - 1)
            back2(B - 1)

        @block.tensor
        def _(pe):
            pe.wait_ge(s["consts_in"], 17 * 16)
            pe.wait_ge(s["wproj_ready"], 1)

            def project(b, u, k):
                pe.wait_ge(s_in[u], 16 * k + 16)
                if not first(b):
                    pe.wait_ge(s["qk_out"], 2 * b)
                    pe.wait_ge(s["vo_out"], 2 * b)
                    pe.wait_ge(s["x2_ready"], b - 1)
                for tile in range(2):
                    at = TILE_AT[tile]
                    lhs = lat[:, u, at:at + 128]
                    nc.tensor.matmul(psum[:, 2 * tile, 0:2 * D], lhs, wqkv[:, 0:2 * D], start=True, stop=True)
                    nc.tensor.matmul(psum[:, 2 * tile + 1, 0:D], lhs, wqkv[:, 2 * D:3 * D], start=True, stop=True)
                    nc.tensor.matmul(psum[:, 2 * tile + 1, D:2 * D], lhs, wog[:, :], start=True, stop=True).then_inc(s["wl_ps"], 1)

            def turn_qk(b):
                pe.wait_ge(s["qkf_ready"], b + 1)
                pe.wait_ge(s["x2_ready"], b)
                pe.wait_ge(s["qk_out"], 2 * b + 4 if not (isinstance(b, int) and b == B - 1) else 2 * B)
                for a in range(2):
                    for g in range(3):
                        for tile in range(2):
                            rows, at = TILE_ROWS[tile], g * N + TILE_AT[tile]
                            mm = nc.tensor.transpose(psum[:, 2 * a, at:at + rows],
                                                     qkf[0:rows, tile, 12 * a + 4 * g:12 * a + 4 * g + 4, :].rearrange("p h d -> p (h d)"),
                                                     ident[0:rows, 0:rows])
                mm.then_inc(s["turned"], 1)

            def scores(b, g):
                if g == 0:
                    pe.wait_ge(s["qkT_ready"], b + 1)
                pe.wait_ge(s["masked"], 3 * b + g)
                for r in range(4):
                    lo = 32 * r
                    nc.tensor.matmul(psum[:, 4 + r, 0:128], qkT[lo:lo + DH, 1, g, NPATCH:N], qkT[lo:lo + DH, 0, g, NPATCH:N],
                                     start=True, stop=True)
                    mm = nc.tensor.matmul(psum[0:NPATCH, 4 + r, 128:128 + N], qkT[lo:lo + DH, 1, g, 0:NPATCH], qkT[lo:lo + DH, 0, g, :],
                                          start=True, stop=True)
                mm.then_inc(s["sc_ps"], 1)

            def values(b, u, g):
                n = g % 2
                pe.wait_ge(s["masked"], 3 * b + g + 1)
                if g == 0:
                    pe.wait_ge(s["vg_ready"], b + 1)
                    pe.wait_ge(s["vo_out"], 2 * b + 4 if not (isinstance(b, int) and b == B - 1) else 2 * B)
                for r in range(4):
                    h = 4 * g + r
                    col = h * (DH + 1)
                    nc.tensor.matmul(psum[:, 1, col:col + DH + 1], at_[:, n, r, :], vg[:, u, 0, h, :], start=True, stop=False)
                    nc.tensor.matmul(psum[:, 1, col:col + DH + 1], ap_[:, n, r, NPATCH:N], vg[0:NPATCH, u, 1, h, :], start=False, stop=True)
                    mm = nc.tensor.matmul(psum[:, 3, col:col + DH + 1], ap_[:, n, r, 0:128], vg[0:NPATCH, u, 1, h, :], start=True, stop=True)
                if g == 0:
                    mm.then_inc(s["av0"], 1)
                if g == 2:
                    mm.then_inc(s["o_ps"], 1)

            def out(b):
                pe.wait_ge(s["o_ready"], b + 1)
                for c in range(2):
                    for tile in range(2):
                        rows, at = TILE_ROWS[tile], c * N + TILE_AT[tile]
                        mm = nc.tensor.transpose(psum[0:DC, 0, at:at + rows], o[0:rows, tile, c * DC:c * DC + DC], ident[0:rows, 0:rows])
                mm.then_inc(s["oT_ps"], 1)
                pe.wait_ge(s["oT_ready"], b + 1)
                for tile in range(2):
                    at = TILE_AT[tile]
                    for c in range(2):
                        mm = nc.tensor.matmul(psum[:, 2, tile * D:tile * D + D], oT[:, c, at:at + 128], wproj[:, c, :],
                                              start=(c == 0), stop=(c == 1))
                mm.then_inc(s["pr_ps"], 1)

            def back(b, u):
                turn_qk(b)
                scores(b, 0)
                scores(b, 1)
                values(b, u, 0)
                scores(b, 2)
                values(b, u, 1)
                values(b, u, 2)
                out(b)

            def turn(b, u, k, before):
                project(b, u, k)
                if not first(b):
                    back(b - 1, 1 - u)
            run(pe, turn)
            back(B - 1, 1)


def gated_ffn(nc, t, psum):
    TURNS = B // 2
    HID = 512
    HJ = HID // 128
    with ExitStack() as ctx:
        def sb(name, shape, dt=FP32):
            return ctx.enter_context(nc.sbuf_tensor("ffn_" + name, shape, dt))

        ident = sb("ident", [128, 128])
        half = sb("half", [128, 4])
        nwt = sb("nwt", [DC, 2])
        w1 = sb("w1", [DC, 2, HID])
        w2 = sb("w2", [DC, 2, HID])
        w3 = sb("w3", [128, HJ, D])
        x2 = sb("x2", [128, 2, 4, D])
        h2 = sb("h2", [128, 2, 4, D])
        xsq = sb("xsq", [128, D])
        ss = sb("ss", [128, 4])
        r = sb("r", [128, 4])
        xr = sb("xr", [128, 4, D])
        xrT = sb("xrT", [DC, 2, 2, N])
        gth = sb("gth", [128, HJ, 2 * N])
        hid = sb("hid", [128, HJ, 2 * N])
        h3 = sb("h3", [128, 4, D])
        s = phase_sems(ctx, nc, "ffn", "consts_in half_ready w_ready in0 in1 ss_ready mss r_ready xr_ready xrT_ps xrT_ready g_ps gth_ready g2_ready "
                 "hid_ready o_ps sum_ready h3_ready h3_stored chain")
        block = ctx.enter_context(nc.Block())
        s_in = (s["in0"], s["in1"])

        def run(eng, turn):
            turn(0, 0, 0)
            with eng.Fori(0, TURNS // 2 - 1) as pair:
                turn(pair * 2 + 1, 1, pair)
                turn(pair * 2 + 2, 0, pair + 1)
            turn(TURNS - 1, 1, TURNS // 2 - 1)

        @block.sync
        def _(sp):
            for dst, src in ((ident[:, :], t["ident"]), (w1[:, :, :], t["attn_w1"].rearrange("(c p) k -> p c k", p=DC)),
                             (w2[:, :, :], t["attn_w2"].rearrange("(c p) k -> p c k", p=DC)),
                             (w3[:, :, :], t["attn_w3"].rearrange("(j p) k -> p j k", p=128))):
                sp.dma_start(dst, src).then_inc(s["consts_in"], 16)
            sp.dma_start(nwt[:, :], t["attn_ffn_ln_w"].rearrange("(c p) -> p c", p=DC), allow_slow_non_contiguous=True).then_inc(s["consts_in"], 16)

            def load(i, u):
                for j in range(4):
                    at = TILE_AT[j % 2]
                    sp.dma_start(x2[:, u, j, :], t["x2_dram"][2 * i + j // 2, at:at + 128, :]).then_inc(s_in[u], 16)
                    sp.dma_start(h2[:, u, j, :], t["h2_dram"][2 * i + j // 2, at:at + 128, :]).then_inc(s_in[u], 16)

            def store(i):
                sp.wait_ge(s["h3_ready"], i + 1)
                for b in range(2):
                    sp.dma_start(t["h3_dram"][2 * i + b, NPATCH:N, :], h3[:, 2 * b, :]).then_inc(s["h3_stored"], 16)
                    sp.dma_start(t["h3_dram"][2 * i + b, 0:NPATCH, :], h3[0:NPATCH, 2 * b + 1, :]).then_inc(s["h3_stored"], 16)

            load(0, 0)
            load(1, 1)
            with sp.Fori(0, TURNS // 2 - 1) as pair:
                for u in range(2):
                    store(pair * 2 + u)
                    load(pair * 2 + u + 2, u)
            store(TURNS - 2)
            store(TURNS - 1)
            sp.wait_ge(s["h3_stored"], 64 * TURNS)

        @block.gpsimd
        def _(pool):
            nc.gpsimd.memset(half[:, :], -0.5).then_inc(s["half_ready"], 1)
            pool.wait_ge(s["half_ready"], 1)

            def turn(i, u, k):
                pool.wait_ge(s["mss"], i + 1)
                pool.wait_ge(s["xr_ready"], i)
                nc.gpsimd.tensor_tensor(r[:, :], ss[:, :], half[:, :], ALU.pow).then_inc(s["r_ready"], 1)
            run(pool, turn)

        @block.vector
        def _(dve):
            dve.wait_ge(s["consts_in"], 5 * 16)
            for w in (w1, w2):
                nc.vector.tensor_tensor(w[:, :, :], w[:, :, :], nwt[:, :].unsqueeze(2).to_broadcast([DC, 2, HID]),
                                        ALU.mult).then_inc(s["w_ready"], 1)

            def front(i, u, k):
                dve.wait_ge(s["ss_ready"], 4 * i + 4)
                nc.vector.tensor_scalar(ss[:, :], ss[:, :], 1.0 / D, RMS_EPS, ALU.mult, ALU.add).then_inc(s["mss"], 1)
                dve.wait_ge(s_in[u], 128 * k + 128)
                dve.wait_ge(s["r_ready"], i + 1)
                dve.wait_ge(s["xrT_ps"], i)
                for j in range(4):
                    st = nc.vector.tensor_scalar(xr[:, j, :], x2[:, u, j, :], r[:, j:j + 1], None, ALU.mult)
                st.then_inc(s["xr_ready"], 1)

            def middle(i, u):
                for j in range(HJ):
                    dve.wait_ge(s["gth_ready"], HJ * i + j + 1)
                    nc.vector.scalar_tensor_tensor(gth[:, j, :], gth[:, j, :], 1.0, psum[:, 2 * j, 0:2 * N], ALU.add, ALU.mult).then_inc(s["g2_ready"], 1)
                    dve.wait_ge(s["g2_ready"], HJ * i + j + 1)
                    dve.wait_ge(s["o_ps"], 2 * i)
                    nc.vector.scalar_tensor_tensor(hid[:, j, :], gth[:, j, :], 0.5, psum[:, 2 * j + 1, 0:2 * N], ALU.mult, ALU.mult).then_inc(s["hid_ready"], 1)

            def last(i, u):
                dve.wait_ge(s["h3_stored"], 64 * i)
                dve.wait_ge(s["h3_ready"], i)
                nc.vector.tensor_tensor(h3[:, :, :], x2[:, u, :, :], h2[:, u, :, :], ALU.add).then_inc(s["sum_ready"], 1)
                dve.wait_ge(s["sum_ready"], i + 1)
                for b in range(2):
                    dve.wait_ge(s["o_ps"], 2 * i + b + 1)
                    st = nc.vector.tensor_tensor(h3[:, 2 * b:2 * b + 2, :], h3[:, 2 * b:2 * b + 2, :],
                                                 psum[:, b, 0:2 * D].rearrange("p (a d) -> p a d", a=2), ALU.add)
                st.then_inc(s["h3_ready"], 1)

            def turn(i, u, k):
                if isinstance(i, int) and i == 0:
                    front(0, 0, 0)
                else:
                    middle(i - 1, 1 - u)
                    front(i, u, k)
                    last(i - 1, 1 - u)
            run(dve, turn)
            middle(TURNS - 1, 1)
            last(TURNS - 1, 1)

        @block.scalar
        def _(act):
            def front(i, u, k):
                act.wait_ge(s_in[u], 128 * k + 128)
                act.wait_ge(s["r_ready"], i)
                for j in range(4):
                    act.wait_ge(s["ss_ready"], 4 * i + j)
                    nc.scalar.activation(xsq[:, :], x2[:, u, j, :], ACT.Square, accum_out=ss[:, j:j + 1]).then_inc(s["ss_ready"], 1)

            def copy(i):
                act.wait_ge(s["xrT_ps"], i + 1)
                act.wait_ge(s["g_ps"], 2 * HJ * i)
                nc.scalar.copy(xrT[:, :, :, :], psum[0:DC, 2:4, 0:2 * N].rearrange("p c (b n) -> p c b n", b=2)).then_inc(s["xrT_ready"], 1)

            def tanh(i):
                for j in range(HJ):
                    act.wait_ge(s["g_ps"], 2 * HJ * i + 2 * j + 2)
                    act.wait_ge(s["hid_ready"], HJ * i)
                    nc.scalar.activation(gth[:, j, :], psum[:, 2 * j, 0:2 * N], ACT.Tanh, scale=0.5).then_inc(s["gth_ready"], 1)

            def turn(i, u, k):
                front(i, u, k)
                if not (isinstance(i, int) and i == 0):
                    tanh(i - 1)
                copy(i)
            run(act, turn)
            tanh(TURNS - 1)

        @block.tensor
        def _(pe):
            pe.wait_ge(s["consts_in"], 5 * 16)
            pe.wait_ge(s["w_ready"], 2)

            def turned(i):
                pe.wait_ge(s["xr_ready"], i + 1)
                pe.wait_ge(s["hid_ready"], HJ * i)
                for c in range(2):
                    for j in range(4):
                        rows, at = TILE_ROWS[j % 2], (j // 2) * N + TILE_AT[j % 2]
                        mm = nc.tensor.transpose(psum[0:DC, 2 + c, at:at + rows], xr[0:rows, j, c * DC:c * DC + DC], ident[0:rows, 0:rows])
                mm.then_inc(s["xrT_ps"], 1)

            def hidden(i):
                pe.wait_ge(s["xrT_ready"], i + 1)
                pe.wait_ge(s["h3_ready"], i)
                for j in range(HJ):
                    for n, w in enumerate((w1, w2)):
                        for c in range(2):
                            mm = nc.tensor.matmul(psum[:, 2 * j + n, 0:2 * N], w[:, c, 128 * j:128 * j + 128],
                                                  xrT[:, c, :, :], start=(c == 0), stop=(c == 1))
                        mm.then_inc(s["g_ps"], 1)

            def output(i):
                pe.wait_ge(s["hid_ready"], HJ * i + HJ)
                for b in range(2):
                    for a in range(2):
                        at = b * N + TILE_AT[a]
                        for j in range(HJ):
                            mm = nc.tensor.matmul(psum[:, b, a * D:a * D + D], hid[:, j, at:at + 128], w3[:, j, :],
                                                  start=(j == 0), stop=(j == HJ - 1))
                    mm.then_inc(s["o_ps"], 1)

            turned(0)

            def turn(i, u, k):
                hidden(i)
                turned(i + 1)
                output(i)
            with pe.Fori(0, TURNS - 1) as i:
                turn(i, 0, 0)
            hidden(TURNS - 1)
            output(TURNS - 1)


def temporal_layer(nc, t, psum):
    with ExitStack() as ctx:
        def sb(name, shape):
            return ctx.enter_context(nc.sbuf_tensor("l1_" + name, shape, FP32))

        vgate = sb("vgate", [128, B + 1, 2, HEADS])
        decay = sb("decay", [128, 2, HEADS])
        with nc.sbuf_tensor("l1_th", [128, B, 2, 4 * HEADS], FP32) as th:
            combine(nc, t, psum, th)
            gates(nc, t, psum, th, vgate, decay)
        decay_attention(nc, t, psum, vgate, decay)
        gated_ffn(nc, t, psum)


def routed_mixture(nc, t, psum):
    TM = 102
    NT = B * N // TM
    PER = 4
    BLOCKS = NT // PER
    BT = PER * TM
    FJ = F1 // 128
    NE = E1 + 1
    ORDER = [E1] + list(range(E1))
    with ExitStack() as ctx:
        def sb(name, shape, dt=FP32):
            return ctx.enter_context(nc.sbuf_tensor("moe_" + name, shape, dt))

        ident = sb("ident", [128, 128])
        half = sb("half", [128, NT])
        before = sb("before", [128, E1, E1])
        ebias = sb("ebias", [128, E1])
        wr = sb("wr", [E1, D])
        wrT = sb("wrT", [DC, 2, E1])
        stage_gu = sb("stage_gu", [128, 2, 2, FJ, D])
        stage_d = sb("stage_d", [DC, 2, 2, F1])
        wguT = sb("wguT", [DC, NE, 2, 2, F1])
        wdT = sb("wdT", [128, NE, FJ, D])
        h3 = sb("h3", [TM, NT, D])
        y = sb("y", [TM, NT, D])
        stats = sb("stats", [TM, NT, 6])
        mv = sb("mv", [TM, NT, 2])
        rstd = sb("rstd", [TM, NT])
        yT = sb("yT", [DC, 2, B * N])
        lg = sb("lg", [TM, NT, E1])
        sel = sb("sel", [TM, NT, E1])
        v1 = sb("v1", [TM, NT])
        cmp = sb("cmp", [TM, NT, E1, E1])
        eq = sb("eq", [TM, NT, E1, E1])
        comb = sb("comb", [TM, NT, E1])
        cb = sb("cb", [TM, PER, E1])
        sg = sb("sg", [128, FJ, BT])
        hT = sb("hT", [128, 2, FJ, BT])
        acc = sb("acc", [TM, PER, D])
        s = phase_sems(ctx, nc, "moe", "consts_in h_in half_ready w_in0 w_in1 wt_ps wt_out stats_done mv_ready rstd_ready y_ready yT_ps yT_out wrT_ps wrT_out "
                 "lg_ps lg_ready lg_exp comb_ready cb_ready g_ps sg_ready h_ready o_ps o_used0 o_used1 acc_ready out_stored chain passed")
        block = ctx.enter_context(nc.Block())
        w_in, o_used = (s["w_in0"], s["w_in1"]), (s["o_used0"], s["o_used1"])
        out_v = t["out"].rearrange("b n d -> (b n) d").rearrange("(k p) d -> p k d", p=TM)
        h3_v = t["h3_dram"].rearrange("b n d -> (b n) d").rearrange("(k p) d -> p k d", p=TM)

        def experts(eng, turn):
            with eng.Fori(0, E1 // 2) as pair:
                turn(pair * 2, 0, pair)
                turn(pair * 2 + 1, 1, pair)
            turn(E1, 0, E1 // 2)

        @block.sync
        def _(sp):
            for dst, src in ((ident[:, :], t["ident"]), (before[:, :, :], t["before"].unsqueeze(0).to_broadcast([128, E1, E1])),
                             (ebias[:, :], row_bc(t["ffn_expert_bias"], 128)), (wr[:, :], t["ffn_w_router"])):
                sp.dma_start(dst, src).then_inc(s["consts_in"], 16)
            sp.dma_start(h3[:, :, :], h3_v).then_inc(s["h_in"], 16)

            def load(e, u, gate, up, down):
                sp.dma_start(stage_gu[:, u, 0, :, :], gate.rearrange("(j p) d -> p j d", p=128)).then_inc(w_in[u], 16)
                sp.dma_start(stage_gu[:, u, 1, :, :], up.rearrange("(j p) d -> p j d", p=128)).then_inc(w_in[u], 16)
                sp.dma_start(stage_d[:, u, :, :], down.rearrange("(c p) f -> p c f", p=DC)).then_inc(w_in[u], 16)

            def turn(e, u, k):
                if isinstance(e, int):
                    sp.wait_ge(s["wt_ps"], 3 * (e - 1))
                    load(e, u, t["ffn_sg"], t["ffn_su"], t["ffn_sd"])
                else:
                    sp.wait_ge(s["wt_ps"], 6 * k)
                    load(e, u, t["ffn_Wg"][e, :, :], t["ffn_Wu"][e, :, :], t["ffn_Wd"][e, :, :])
            experts(sp, turn)
            with sp.Fori(0, BLOCKS) as k:
                sp.wait_ge(s["acc_ready"], k + 1)
                sp.dma_start(out_v[:, bass.ds(k * PER, PER), :], acc[:, :, :]).then_inc(s["out_stored"], 16)
            sp.wait_ge(s["out_stored"], 16 * BLOCKS)

        @block.gpsimd
        def _(pool):
            nc.gpsimd.memset(half[:, :], -0.5).then_inc(s["half_ready"], 1)
            pool.wait_ge(s["half_ready"], 1)
            pool.wait_ge(s["mv_ready"], 1)
            nc.gpsimd.tensor_tensor(rstd[:, :], mv[:, :, 1], half[0:TM, :], ALU.pow).then_inc(s["rstd_ready"], 1)

        @block.vector
        def _(dve):
            ch = Chain(dve, s["chain"])
            dve.wait_ge(s["h_in"], 16)
            for k in range(NT):
                st = nc.vector.bn_stats(stats[:, k, :], h3[:, k, :])
            ch.link(st)
            for k in range(NT):
                st = nc.vector.bn_aggr(mv[:, k, :], stats[:, k, :])
            ch.link(st)
            nc.vector.tensor_scalar(mv[:, :, 1], mv[:, :, 1], LN_EPS, None, ALU.add).then_inc(s["mv_ready"], 1)
            dve.wait_ge(s["rstd_ready"], 1)
            for k in range(NT):
                nc.vector.tensor_scalar(y[:, k, :], h3[:, k, :], mv[:, k, 0:1], rstd[:, k:k + 1],
                                        ALU.subtract, ALU.mult).then_inc(s["y_ready"], 1)
            dve.wait_ge(s["consts_in"], 64)
            dve.wait_ge(s["lg_ps"], 1)
            lps = psum[0:TM, 0, 0:NT * E1].rearrange("p (k e) -> p k e", e=E1)

            def over_experts(x):
                return x.unsqueeze(2).to_broadcast([TM, NT, E1])

            ch.link(nc.vector.tensor_reduce(v1[:, :], lps, AXX, ALU.max))
            nc.vector.tensor_tensor(lg[:, :, :], lps, over_experts(v1[:, :]), ALU.subtract).then_inc(s["lg_ready"], 1)
            dve.wait_ge(s["lg_exp"], 1)
            ch.link(nc.vector.tensor_reduce(v1[:, :], lg[:, :, :], AXX, ALU.add))
            ch.link(nc.vector.reciprocal(v1[:, :], v1[:, :]))
            ch.link(nc.vector.tensor_tensor(lg[:, :, :], lg[:, :, :], over_experts(v1[:, :]), ALU.mult))
            ch.link(nc.vector.tensor_tensor(sel[:, :, :], lg[:, :, :], ebias[0:TM, :].unsqueeze(1).to_broadcast([TM, NT, E1]), ALU.add))
            for k in range(NT):
                mine = sel[:, k, :].unsqueeze(2).to_broadcast([TM, E1, E1])
                other = sel[:, k, :].unsqueeze(1).to_broadcast([TM, E1, E1])
                nc.vector.tensor_tensor(cmp[:, k, :, :], other, mine, ALU.is_gt)
                st = nc.vector.tensor_tensor(eq[:, k, :, :], other, mine, ALU.is_equal)
            ch.link(st)
            ch.link(nc.vector.tensor_tensor(eq[:, :, :, :].rearrange("p k a b -> p k (a b)"), eq[:, :, :, :].rearrange("p k a b -> p k (a b)"),
                                            before[0:TM, :, :].rearrange("p a b -> p (a b)").unsqueeze(1).to_broadcast([TM, NT, E1 * E1]), ALU.mult))
            ch.link(nc.vector.tensor_tensor(cmp[:, :, :, :], cmp[:, :, :, :], eq[:, :, :, :], ALU.add))
            ch.link(nc.vector.tensor_reduce(sel[:, :, :].rearrange("p k e -> p (k e)"), cmp[:, :, :, :].rearrange("p k a b -> p (k a) b"), AXX, ALU.add))
            ch.link(nc.vector.tensor_scalar(sel[:, :, :], sel[:, :, :], 2.0, None, ALU.is_lt))
            ch.link(nc.vector.tensor_tensor(comb[:, :, :], sel[:, :, :], lg[:, :, :], ALU.mult))
            ch.link(nc.vector.tensor_reduce(v1[:, :], comb[:, :, :], AXX, ALU.add))
            ch.link(nc.vector.tensor_scalar(v1[:, :], v1[:, :], 1e-9, None, ALU.add))
            ch.link(nc.vector.reciprocal(v1[:, :], v1[:, :]))
            nc.vector.tensor_tensor(comb[:, :, :], comb[:, :, :], over_experts(v1[:, :]), ALU.mult).then_inc(s["comb_ready"], 1)
            dve.wait_ge(s["comb_ready"], 1)
            SETUP = ch.n
            ADDS = 2 * NE

            def hidden(k, n):
                for j in range(FJ):
                    dve.wait_ge(s["sg_ready"], (k * NE + n) * FJ + j + 1)
                    if n >= 2:
                        dve.wait_ge(s["o_ps"], (k * NE + n - 2) * 2 + 2)
                    else:
                        dve.wait_ge(s["o_ps"], k * NE * 2)
                    nc.vector.tensor_tensor(hT[:, n % 2, j, :], sg[:, j, :], psum[:, 2 * j + 1, 0:BT], ALU.mult).then_inc(s["h_ready"], 1)

            def add(k, n):
                for m in range(2):
                    dve.wait_ge(s["o_ps"], (k * NE + n) * 2 + m + 1)
                    part = psum[0:TM, 6 + m, 0:2 * D].rearrange("p (a d) -> p a d", a=2)
                    if n == 0:
                        nc.vector.tensor_tensor(acc[:, 2 * m:2 * m + 2, :], part, h3[:, bass.ds(k * PER + 2 * m, 2), :],
                                                ALU.add).then_inc(o_used[m], 1)
                    else:
                        dve.wait_ge(o_used[m], k * NE + n)
                        for a in range(2):
                            st = nc.vector.scalar_tensor_tensor(acc[:, 2 * m + a, :], part[:, a, :], cb[:, 2 * m + a, ORDER[n]:ORDER[n] + 1],
                                                                acc[:, 2 * m + a, :], ALU.mult, ALU.add)
                        st.then_inc(o_used[m], 1)

            with dve.Fori(0, BLOCKS) as k:
                nc.vector.tensor_copy(cb[:, :, :], comb[:, bass.ds(k * PER, PER), :]).then_inc(s["cb_ready"], 1)
                dve.wait_ge(s["cb_ready"], k + 1)
                dve.wait_ge(s["out_stored"], 16 * k)
                for n in range(NE):
                    hidden(k, n)
                    if n:
                        add(k, n - 1)
                add(k, NE - 1)
                for m in range(2):
                    dve.wait_ge(o_used[m], k * NE + NE)
                nc.vector.tensor_copy(acc[:, 0, 0:2], acc[:, 0, 0:2]).then_inc(s["acc_ready"], 1)

        @block.scalar
        def _(act):
            act.wait_ge(s["wrT_ps"], 1)
            nc.scalar.copy(wrT[:, :, :], psum[0:DC, 6, 0:2 * E1].rearrange("p (c e) -> p c e", c=2)).then_inc(s["wrT_out"], 1)

            def turn(e, u, k):
                for n in range(2):
                    act.wait_ge(s["wt_ps"], 3 * e + n + 1)
                    nc.scalar.copy(wguT[:, e, n, :, :], psum[0:DC, 2 * n:2 * n + 2, 0:F1]).then_inc(s["wt_out"], 1)
                act.wait_ge(s["wt_ps"], 3 * e + 3)
                nc.scalar.copy(wdT[:, e, 0:2, :], psum[:, 4, 0:2 * D].rearrange("p (j d) -> p j d", j=2)).then_inc(s["wt_out"], 1)
                nc.scalar.copy(wdT[:, e, 2, :], psum[:, 5, 0:D]).then_inc(s["wt_out"], 1)
            experts(act, turn)
            for k in range(BLOCKS):
                act.wait_ge(s["yT_ps"], k + 1)
                b0 = 2 * (k % 2)
                nc.scalar.copy(yT[:, :, k * BT:k * BT + BT], psum[0:DC, b0:b0 + 2, 0:BT]).then_inc(s["yT_out"], 1)
            act.wait_ge(s["lg_ready"], 1)
            nc.scalar.activation(lg[:, :, :], lg[:, :, :], ACT.Exp).then_inc(s["lg_exp"], 1)
            with act.Fori(0, BLOCKS) as k:
                for n in range(NE):
                    for j in range(FJ):
                        act.wait_ge(s["g_ps"], (k * NE + n) * FJ + j + 1)
                        if n == 0:
                            act.wait_ge(s["h_ready"], k * NE * FJ)
                        else:
                            act.wait_ge(s["h_ready"], (k * NE + n - 1) * FJ + j + 1)
                        nc.scalar.activation(sg[:, j, :], psum[:, 2 * j, 0:BT], ACT.Silu).then_inc(s["sg_ready"], 1)

        @block.tensor
        def _(pe):
            pe.wait_ge(s["consts_in"], 64)
            for c in range(2):
                mm = nc.tensor.transpose(psum[0:DC, 6, c * E1:c * E1 + E1], wr[:, c * DC:c * DC + DC], ident[0:E1, 0:E1])
            mm.then_inc(s["wrT_ps"], 1)

            def turn(e, u, k):
                pe.wait_ge(w_in[u], 48 * k + 48)
                pe.wait_ge(s["wt_out"], 4 * e)
                for n in range(2):
                    for c in range(2):
                        for j in range(FJ):
                            mm = nc.tensor.transpose(psum[0:DC, 2 * n + c, 128 * j:128 * j + 128],
                                                     stage_gu[:, u, n, j, c * DC:c * DC + DC], ident[:, :])
                    mm.then_inc(s["wt_ps"], 1)
                for j in range(FJ):
                    for c in range(2):
                        at = (j % 2) * D + c * DC
                        mm = nc.tensor.transpose(psum[:, 4 + j // 2, at:at + DC], stage_d[:, u, c, 128 * j:128 * j + 128],
                                                 ident[0:DC, 0:DC])
                mm.then_inc(s["wt_ps"], 1)
            experts(pe, turn)
            pe.wait_ge(s["wt_out"], 4 * NE)
            for k in range(BLOCKS):
                pe.wait_ge(s["y_ready"], PER * k + PER)
                if k >= 2:
                    pe.wait_ge(s["yT_out"], k - 1)
                for c in range(2):
                    for a in range(PER):
                        mm = nc.tensor.transpose(psum[0:DC, 2 * (k % 2) + c, a * TM:a * TM + TM],
                                                 y[:, PER * k + a, c * DC:c * DC + DC], ident[0:TM, 0:TM])
                mm.then_inc(s["yT_ps"], 1)
            pe.wait_ge(s["yT_out"], BLOCKS)
            pe.wait_ge(s["wrT_out"], 1)
            for k in range(NT):
                for c in range(2):
                    mm = nc.tensor.matmul(psum[0:TM, 0, k * E1:k * E1 + E1], yT[:, c, k * TM:k * TM + TM], wrT[:, c, :],
                                          start=(c == 0), stop=(c == 1))
            mm.then_inc(s["lg_ps"], 1)
            pe.wait_ge(s["lg_ready"], 1)

            def hidden(k, n):
                for j in range(FJ):
                    if n == 0:
                        pe.wait_ge(s["h_ready"], k * NE * FJ)
                    else:
                        pe.wait_ge(s["h_ready"], (k * NE + n - 1) * FJ + j + 1)
                    for a in range(2):
                        for c in range(2):
                            mm = nc.tensor.matmul(psum[:, 2 * j + a, 0:BT], wguT[:, ORDER[n], a, c, 128 * j:128 * j + 128],
                                                  yT[:, c, bass.ds(k * BT, BT)], start=(c == 0), stop=(c == 1))
                    mm.then_inc(s["g_ps"], 1)

            def output(k, n):
                pe.wait_ge(s["h_ready"], (k * NE + n) * FJ + FJ)
                for m in range(2):
                    pe.wait_ge(o_used[m], k * NE + n)
                    for a in range(2):
                        at = (2 * m + a) * TM
                        for j in range(FJ):
                            mm = nc.tensor.matmul(psum[0:TM, 6 + m, a * D:a * D + D], hT[:, n % 2, j, at:at + TM],
                                                  wdT[:, ORDER[n], j, :], start=(j == 0), stop=(j == FJ - 1))
                    mm.then_inc(s["o_ps"], 1)

            with pe.Fori(0, BLOCKS) as k:
                for n in range(NE):
                    hidden(k, n)
                    if n:
                        output(k, n - 1)
                output(k, NE - 1)


def build(nc, ins, outs, consts, scratch):
    t = {"x": ins["x"], "txt": ins["txt"], "tok_W": ins["L0_tok_W"], "tok_b": ins["L0_tok_b"],
         "tok_alpha_w": ins["L0_tok_alpha_w"], "tok_alpha_a": ins["L0_tok_alpha_a"], "attn_W": ins["L0_attn_W"],
         "attn_params": [ins["L0_attn_" + n] for n in ("b", "bn_gamma", "bn_beta", "bn_mean", "bn_var")],
         "out": outs[0], **consts, **scratch}
    t.update({n.split("_", 1)[1]: a for n, a in ins.items() if n.startswith(("L0_ffn", "L1_"))})
    with nc.psum_tensor("banks", [128, 8, 512], FP32) as psum:
        for phase in (patches, spiking_attention, soft_mixture, temporal_layer, routed_mixture):
            phase(nc, t, psum)


_SCRATCH = {"h_dram": (B, N, D), "h1_dram": (B, N, D), "xn_dram": (B, N, D), "xnT_dram": (B, 2, DC, N),
            "cwT_dram": (B, NG, 128, N), "eo_dram": (B, SLOTS, D), "h2_dram": (B, N, D), "y3_dram": (B, N, D),
            "lat_dram": (B, 128, N), "x2_dram": (B, N, D), "h3_dram": (B, N, D)}


def _constants():
    import numpy as np
    f32 = np.float32
    token = np.stack([np.arange(128) + NPATCH, np.arange(128)], 1)
    freq = (f32(1.0) / f32(10000.0) ** (np.arange(0, DH, 2, dtype=f32) / f32(DH))).astype(f32)
    angle = token[:, :, None].astype(f32) * np.concatenate([freq, freq])
    sign = np.concatenate([-np.ones(DH // 2), np.ones(DH // 2)])
    tokens = np.arange(N)
    return {"ident": np.eye(128, dtype=f32),
            "heads_mask": np.kron(np.eye(DC // DH), np.ones((DH, DH))).astype(f32),
            "cos": np.cos(angle).astype(f32), "sin": (np.sin(angle) * sign).astype(f32),
            "pos": (token + 1).astype(f32),
            "causal": np.triu(np.ones((128, 128), f32)),
            "causal_p": (tokens[:NPATCH, None] <= tokens[None, :]).astype(f32),
            "before": np.tril(np.ones((E1, E1), f32), -1)}


def kernel(**inputs):
    import numpy as _np
    import concourse.bacc as _bacc
    from concourse import mybir as _mybir
    from concourse.bass_utils import run_bass_kernel_spmd as _run

    nc = _bacc.Bacc("TRN2", target_bir_lowering=False, num_devices=1)
    arrays, ins, consts, scratch = {}, {}, {}, {}
    for name, value in inputs.items():
        a = _np.ascontiguousarray(value)
        if a.ndim == 0:
            a = a.reshape(1)
        arrays[f"in_{name}_dram"] = a
        ins[name] = nc.dram_tensor(f"in_{name}_dram", a.shape, _mybir.dt.from_np(a.dtype), kind="ExternalInput").ap()
    for name, a in _constants().items():
        arrays[f"const_{name}_dram"] = a
        consts[name] = nc.dram_tensor(f"const_{name}_dram", a.shape, _mybir.dt.from_np(a.dtype), kind="ExternalInput").ap()
    for name, shape in _SCRATCH.items():
        scratch[name] = nc.dram_tensor(name, shape, _mybir.dt.float32, kind="Internal").ap()
    outs = [nc.dram_tensor("out_0_dram", (B, N, D), _mybir.dt.float32, kind="ExternalOutput").ap()]
    build(nc, ins, outs, consts, scratch)
    r = _run(nc, [arrays], core_ids=[0])
    return r.results[0]["out_0_dram"]
```

```python
import concourse.bass as bass
from concourse import mybir
from contextlib import ExitStack

FP32 = mybir.dt.float32
BF16 = mybir.dt.bfloat16
ALU = mybir.AluOpType
ACT = mybir.ActivationFunctionType
AXX = mybir.AxisListType.X

B = 16
D = 192
DC = 96
NPATCH = 25
NTXT = 128
N = NPATCH + NTXT
PATCH = 16
KPATCH = 3 * PATCH * PATCH
LN_EPS = 1e-5
RMS_EPS = 1e-6
E0, S0, H0 = 32, 32, 768
SLOTS = E0 * S0
NG = SLOTS // 128
HEADS, DH = 12, 16
E1, F1 = 8, 384
ROUND = 1.5 * 2.0 ** 23

TILE_AT = (NPATCH, 0)
TILE_ROWS = (NTXT, NPATCH)


class Chain:

    def __init__(self, eng, sem, passed=None):
        self.eng, self.sem, self.base, self.n, self.passed = eng, sem, 0, 0, passed

    def link(self, ins, apart=False):
        self.n += 1
        ins.then_inc(self.sem, 1)
        self.eng.wait_ge(self.sem, self.base + self.n)
        if apart:
            self.eng.sem_inc(self.passed, 1)

    def start_loop(self, i, per_turn):
        self.before = self.n
        self.per_turn = per_turn
        self.base = self.before + i * per_turn
        self.n = 0

    def end_loop(self, turns):
        assert self.n == self.per_turn, (self.n, self.per_turn)
        self.base = 0
        self.n = self.before + turns * self.per_turn


def phase_sems(ctx, nc, phase, names):
    sems = {name: nc.alloc_semaphore(name=f"{phase}_{name}") for name in names.split()}

    def clear():
        nc.clear_and_free_semaphores(list(sems.values()))
        nc.all_engine_barrier()
    ctx.callback(clear)
    return sems


def row_bc(ap, parts):
    return ap.unsqueeze(0).to_broadcast([parts] + list(ap.shape))


def patches(nc, t, psum):
    KC = KPATCH // 128
    with ExitStack() as ctx:
        def sb(name, shape, dt=FP32):
            return ctx.enter_context(nc.sbuf_tensor("tok_" + name, shape, dt))

        img = sb("img", [B * 5, 3, PATCH, 80])
        imgq = sb("imgq", [B * 5, 5, 3 * PATCH, PATCH], BF16)
        w = sb("w", [DC, 2, KPATCH])
        wq = sb("wq", [DC, 2, KPATCH], BF16)
        alpha = sb("alpha", [128, 2])
        ralpha = sb("ralpha", [128, 2])
        yscale = sb("yscale", [128, 1])
        bias = sb("bias", [128, D])
        ident = sb("ident", [128, 128])
        identb = sb("identb", [128, 128], BF16)
        imgT = sb("imgT", [128, KC, B, 5, 5], BF16)
        wT = sb("wT", [128, KC, D], BF16)
        emb = sb("emb", [100, 4, D])
        s = phase_sems(ctx, nc, "tok", "consts_in img_in txt_copied img_q w_q identb_ready turned evacuated "
                 "product scaled stored chain")
        block = ctx.enter_context(nc.Block())
        turn_ps = [psum[:, k, :].bitcast(BF16) for k in range(2)]

        @block.sync
        def _(sp):
            sp.dma_start(ident[:, :], t["ident"]).then_inc(s["consts_in"], 16)
            sp.dma_start(w[:, :, :], t["tok_W"].rearrange("(c o) i a b -> o c (i a b)", o=DC)).then_inc(s["consts_in"], 16)
            sp.dma_start(alpha[:, 0:1], row_bc(t["tok_alpha_a"], 128)).then_inc(s["consts_in"], 16)
            sp.dma_start(alpha[:, 1:2], row_bc(t["tok_alpha_w"], 128)).then_inc(s["consts_in"], 16)
            sp.dma_start(bias[:, :], row_bc(t["tok_b"], 128)).then_inc(s["consts_in"], 16)
            for c in range(3):
                for py in range(5):
                    sp.dma_start(img[py:B * 5:5, c, :, :],
                                 t["x"][:, c, PATCH * py:PATCH * py + PATCH, 0:80]).then_inc(s["img_in"], 16)
            sp.dma_start(t["h_dram"][:, NPATCH:N, :], t["txt"]).then_inc(s["txt_copied"], 16)
            for q in range(4):
                sp.wait_ge(s["scaled"], q + 1)
                for k in range(4):
                    sp.dma_start(t["h_dram"][4 * q + k, 0:NPATCH, :],
                                 emb[NPATCH * k:NPATCH * k + NPATCH, q, :]).then_inc(s["stored"], 16)
            sp.wait_ge(s["stored"], 16 * 16)
            sp.wait_ge(s["txt_copied"], 16)

        @block.vector
        def _(dve):
            ch = Chain(dve, s["chain"])
            dve.wait_ge(s["consts_in"], 5 * 16)
            nc.vector.tensor_copy(identb[:, :], ident[:, :]).then_inc(s["identb_ready"], 1)
            ch.link(nc.vector.reciprocal(ralpha[:, :], alpha[:, :]))

            def quantise(src, dst, ra, out_sem):
                ch.link(nc.vector.tensor_scalar(src, src, ra, -128.0, ALU.mult, ALU.max))
                ch.link(nc.vector.tensor_scalar(src, src, 127.0, ROUND, ALU.min, ALU.add))
                nc.vector.tensor_scalar(dst, src, -ROUND, None, ALU.add).then_inc(out_sem, 1)

            quantise(w[:, :, :], wq[:, :, :], ralpha[0:DC, 1:2], s["w_q"])
            dve.wait_ge(s["img_in"], 16 * 15)
            quantise(img[:, :, :, :].rearrange("p c i (x j) -> p (c i) x j", j=PATCH),
                     imgq[:, :, :, :].rearrange("p x r j -> p r x j"), ralpha[0:80, 0:1], s["img_q"])
            ch.link(nc.vector.tensor_tensor(yscale[:, :], alpha[:, 0:1], alpha[:, 1:2], ALU.mult))
            for q in range(4):
                dve.wait_ge(s["product"], q + 1)
                nc.vector.scalar_tensor_tensor(emb[:, q, :], psum[0:100, 2 + q, 0:D], yscale[0:100, :],
                                               bias[0:100, :], ALU.mult, ALU.add).then_inc(s["scaled"], 1)

        @block.tensor
        def _(pe):
            pe.wait_ge(s["identb_ready"], 1)
            pe.wait_ge(s["w_q"], 1)
            for k in range(KC):
                if k >= 2:
                    pe.wait_ge(s["evacuated"], k - 1)
                for c in range(2):
                    mm = nc.tensor.transpose(turn_ps[k % 2][:, c * DC:c * DC + DC], wq[:, c, 128 * k:128 * k + 128],
                                             identb[0:DC, 0:DC])
                mm.then_inc(s["turned"], 1)
            pe.wait_ge(s["img_q"], 1)
            for k in range(KC):
                pe.wait_ge(s["evacuated"], KC + k - 1)
                for px in range(5):
                    src = imgq[:, px, 8 * k:8 * k + 8, :].rearrange("p r j -> p (r j)")
                    mm = nc.tensor.transpose(turn_ps[k % 2][:, px * 80:px * 80 + 80], src, identb[0:80, 0:80])
                mm.then_inc(s["turned"], 1)
            pe.wait_ge(s["evacuated"], 2 * KC)
            for q in range(4):
                for k in range(KC):
                    mm = nc.tensor.matmul(psum[0:100, 2 + q, 0:D],
                                          imgT[:, k, 4 * q:4 * q + 4, :, :].rearrange("p b y x -> p (b y x)"), wT[:, k, :],
                                          start=(k == 0), stop=(k == KC - 1))
                mm.then_inc(s["product"], 1)

        @block.scalar
        def _(act):
            for k in range(KC):
                act.wait_ge(s["turned"], k + 1)
                nc.scalar.copy(wT[:, k, :], turn_ps[k % 2][:, 0:D]).then_inc(s["evacuated"], 1)
            for k in range(KC):
                act.wait_ge(s["turned"], KC + k + 1)
                nc.scalar.copy(imgT[:, k, :, :, :].rearrange("p b y x -> p (b y) x"),
                               turn_ps[k % 2][:, 0:400].rearrange("p (x a) -> p a x", x=5)).then_inc(s["evacuated"], 1)


def spiking_attention(nc, t, psum):
    TURNS = B // 2
    with ExitStack() as ctx:
        def sb(name, shape, dt=FP32):
            return ctx.enter_context(nc.sbuf_tensor("spk_" + name, shape, dt))

        ident = sb("ident", [128, 128])
        heads_mask = sb("heads_mask", [DC, DC])
        wrow = sb("wrow", [DC, 8, D])
        prm_c = sb("prm_c", [DC, 5, 8])
        prm_r = sb("prm_r", [128, 5, 4 * D])
        inv_c = sb("inv_c", [DC, 8])
        inv_r = sb("inv_r", [128, 4 * D])
        thr_c = sb("thr_c", [DC, 8])
        thr_r = sb("thr_r", [128, 4 * D])
        wT = sb("wT", [DC, 2, 4 * D])
        half = sb("half", [128, 8])
        h = sb("h", [128, 2, 4, D])
        stats = sb("stats", [128, 4, 6])
        mv = sb("mv", [128, 4, 2])
        rstd = sb("rstd", [128, 4])
        y = sb("y", [128, 4, D])
        yT = sb("yT", [DC, 2, 2, N])
        q = sb("q", [DC, 2, 2, N], BF16)
        kv = sb("kv", [128, 4, 2 * D], BF16)
        kvh = sb("kvh", [DC, 2, 2, DC], BF16)
        xs = sb("xs", [DC, 2, 2, N])
        spike = sb("spike", [128, 4, D])
        hr = sb("hr", [128, 2, 4, D])
        h1 = sb("h1", [128, 4, D])
        stats1 = sb("stats1", [128, 4, 6])
        mv1 = sb("mv1", [128, 4, 2])
        g = sb("g", [128, 5, 4])
        xn = sb("xn", [128, 4, D])
        xnT = sb("xnT", [DC, 2, 2, N])
        s = phase_sems(ctx, nc, "spk", "consts_in w_turned w_out wrow_ready thr_ready in0 in1 res_in0 res_in1 bn rstd_ready y_ready yT_ps yT_ready "
                 "q_ps q_ready kv_ps kv_ready kvh_ps kvh_ready xa_ps xs_ready sp_ps spike_ready h1_ready mv1_ready norm_ready "
                 "xn_ready xnT_ps xnT_ready h1_out xn_out xnT_out half_ready chain passed root")
        block = ctx.enter_context(nc.Block())
        s_in, res_in = (s["in0"], s["in1"]), (s["res_in0"], s["res_in1"])

        def turns(eng, turn):
            turn(0, 0, 0, False, False)
            turn(1, 1, 0, True, False)
            with eng.Fori(0, TURNS // 2 - 2) as pair:
                turn(pair * 2 + 2, 0, pair + 1, True, True)
                turn(pair * 2 + 3, 1, pair + 1, True, True)
            turn(TURNS - 2, 0, TURNS // 2 - 1, True, True)
            turn(TURNS - 1, 1, TURNS // 2 - 1, True, True)

        @block.sync
        def _(sp):
            sp.dma_start(ident[:, :], t["ident"]).then_inc(s["consts_in"], 16)
            sp.dma_start(heads_mask[:, :], t["heads_mask"]).then_inc(s["consts_in"], 16)
            sp.dma_start(wrow[:, :, :], t["attn_W"].rearrange("l (c o) d -> o (l c) d", o=DC)).then_inc(s["consts_in"], 16)
            for n, p in enumerate(t["attn_params"]):
                sp.dma_start(prm_c[:, n, :], p.rearrange("l (c o) -> o (l c)", o=DC), allow_slow_non_contiguous=True).then_inc(s["consts_in"], 16)
                sp.dma_start(prm_r[:, n, :], row_bc(p.rearrange("l d -> (l d)"), 128)).then_inc(s["consts_in"], 16)

            def load(dst, sem, i, u):
                for b in range(2):
                    for tile in range(2):
                        sp.dma_start(dst[:, u, 2 * b + tile, :],
                                     t["h_dram"][2 * i + b, TILE_AT[tile]:TILE_AT[tile] + 128, :]).then_inc(sem[u], 16)

            def store_h1(i):
                sp.wait_ge(s["h1_ready"], i + 1)
                for b in range(2):
                    sp.dma_start(t["h1_dram"][2 * i + b, NPATCH:N, :], h1[:, 2 * b, :]).then_inc(s["h1_out"], 16)
                    sp.dma_start(t["h1_dram"][2 * i + b, 0:NPATCH, :], h1[0:NPATCH, 2 * b + 1, :]).then_inc(s["h1_out"], 16)

            def store_xn(i):
                sp.wait_ge(s["xn_ready"], i + 1)
                for b in range(2):
                    sp.dma_start(t["xn_dram"][2 * i + b, NPATCH:N, :], xn[:, 2 * b, :]).then_inc(s["xn_out"], 16)
                    sp.dma_start(t["xn_dram"][2 * i + b, 0:NPATCH, :], xn[0:NPATCH, 2 * b + 1, :]).then_inc(s["xn_out"], 16)
                sp.wait_ge(s["xnT_ready"], i + 1)
                for b in range(2):
                    sp.dma_start(t["xnT_dram"][2 * i + b, :, :, :].rearrange("c p n -> p c n"),
                                 xnT[:, :, b, :]).then_inc(s["xnT_out"], 16)

            for u in range(2):
                load(h, s_in, u, u)
            for u in range(2):
                load(hr, res_in, u, u)

            def step(i, u):
                sp.wait_ge(s["y_ready"], i + 1)
                load(h, s_in, i + 2, u)

            def stores(i, u):
                store_xn(i - 2)
                store_h1(i - 1)
                load(hr, res_in, i + 1, 1 - u)

            step(0, 0)
            step(1, 1)
            store_h1(0)
            load(hr, res_in, 2, 0)
            with sp.Fori(0, TURNS // 2 - 2) as pair:
                for u in range(2):
                    step(pair * 2 + 2 + u, u)
                    stores(pair * 2 + 2 + u, u)
            stores(TURNS - 2, 0)
            store_xn(TURNS - 3)
            store_h1(TURNS - 2)
            store_xn(TURNS - 2)
            store_h1(TURNS - 1)
            store_xn(TURNS - 1)
            sp.wait_ge(s["h1_out"], 64 * TURNS)
            sp.wait_ge(s["xn_out"], 64 * TURNS)
            sp.wait_ge(s["xnT_out"], 32 * TURNS)

        @block.gpsimd
        def _(pool):
            nc.gpsimd.memset(half[:, :], -0.5).then_inc(s["half_ready"], 1)
            pool.wait_ge(s["half_ready"], 1)

            def factor(i):
                pool.wait_ge(s["bn"], i + 1)
                pool.wait_ge(s["y_ready"], i)
                nc.gpsimd.tensor_tensor(rstd[:, :], mv[:, :, 1], half[:, 0:4], ALU.pow).then_inc(s["rstd_ready"], 1)

            def norm(i):
                pool.wait_ge(s["mv1_ready"], i + 1)
                nc.gpsimd.tensor_tensor(g[:, 2:4, :], g[:, 0:2, :],
                                        half[:, :].rearrange("p (a j) -> p a j", a=2), ALU.pow).then_inc(s["norm_ready"], 1)

            factor(0)
            factor(1)
            with pool.Fori(0, TURNS - 2) as i:
                factor(i + 2)
                norm(i)
            norm(TURNS - 2)
            norm(TURNS - 1)

        @block.vector
        def _(dve):
            ch = Chain(dve, s["chain"], s["passed"])
            dve.wait_ge(s["consts_in"], 13 * 16)
            for prm, inv, thr in ((prm_c, inv_c, thr_c), (prm_r, inv_r, thr_r)):
                ch.link(nc.vector.tensor_scalar(inv[:, :], prm[:, 4, :], LN_EPS, None, ALU.add))
                if prm is prm_c:
                    nc.vector.tensor_copy(prm[:, 4, :], inv[:, :]).then_inc(s["root"], 1)
                    dve.wait_ge(s["root"], 2)
                else:
                    nc.vector.tensor_copy(prm[:, 4, :], inv[:, :]).then_inc(s["root"], 1)
                    dve.wait_ge(s["root"], 4)
                ch.link(nc.vector.reciprocal(inv[:, :], prm[:, 4, :]))
                ch.link(nc.vector.tensor_tensor(inv[:, :], inv[:, :], prm[:, 1, :], ALU.mult))
                ch.link(nc.vector.tensor_tensor(thr[:, :], prm[:, 0, :], prm[:, 3, :], ALU.subtract))
                ch.link(nc.vector.tensor_tensor(thr[:, :], thr[:, :], inv[:, :], ALU.mult))
                ch.link(nc.vector.tensor_tensor(thr[:, :], thr[:, :], prm[:, 2, :], ALU.add))
                ch.link(nc.vector.tensor_scalar(thr[:, :], thr[:, :], -1.0, 2.0, ALU.mult, ALU.add))
            nc.vector.tensor_tensor(wrow[:, :, :], wrow[:, :, :],
                                    inv_c[:, :].unsqueeze(2).to_broadcast([DC, 8, D]), ALU.mult).then_inc(s["wrow_ready"], 1)
            SETUP = ch.n
            ALL = 2 + 5 + 1
            FIRST = SETUP + 2 + 2 + 2 + 5

            def normed(i, u, k):
                dve.wait_ge(s_in[u], k * 64 + 64)
                dve.wait_ge(s["rstd_ready"], i)
                for j in range(4):
                    st = nc.vector.bn_stats(stats[:, j, :], h[:, u, j, :])
                ch.link(st, apart=True)
                for j in range(4):
                    st = nc.vector.bn_aggr(mv[:, j, :], stats[:, j, :])
                ch.link(st)
                nc.vector.tensor_scalar(mv[:, :, 1], mv[:, :, 1], LN_EPS, None, ALU.add).then_inc(s["bn"], 1)

            def make_y(i, u):
                dve.wait_ge(s["rstd_ready"], i + 1)
                dve.wait_ge(s["yT_ps"], i)
                for j in range(4):
                    st = nc.vector.tensor_scalar(y[:, j, :], h[:, u, j, :], mv[:, j, 0:1], rstd[:, j:j + 1],
                                                 ALU.subtract, ALU.mult)
                st.then_inc(s["y_ready"], 1)

            def mask_kv(i):
                dve.wait_ge(s["kvh_ps"], i + 1)
                for b in range(2):
                    st = nc.vector.tensor_tensor(kvh[:, b, :, :],
                                                 psum[0:DC, 4, b * D:b * D + D].rearrange("p (c e) -> p c e", c=2),
                                                 heads_mask[:, :].unsqueeze(1).to_broadcast([DC, 2, DC]), ALU.mult)
                st.then_inc(s["kvh_ready"], 1)

            def make_xn(i):
                dve.wait_ge(s["norm_ready"], i + 1)
                ch.link(nc.vector.tensor_tensor(g[:, 4, :], g[:, 2, :], g[:, 3, :], ALU.mult))
                dve.wait_ge(s["xn_out"], i * 64)
                dve.wait_ge(s["xnT_ps"], i)
                for j in range(4):
                    st = nc.vector.tensor_scalar(xn[:, j, :], h1[:, j, :], mv1[:, j, 0:1], g[:, 4, j:j + 1],
                                                 ALU.subtract, ALU.mult)
                st.then_inc(s["xn_ready"], 1)

            def make_xs(i):
                dve.wait_ge(s["xa_ps"], i + 1)
                dve.wait_ge(s["sp_ps"], i)
                for c in range(2):
                    st = nc.vector.tensor_scalar(xs[:, c, :, :], psum[0:DC, 5 + c, 0:2 * N].rearrange("p (b n) -> p b n", b=2),
                                                 float(DH) ** -0.125, 1.0, ALU.mult, ALU.is_ge)
                st.then_inc(s["xs_ready"], 1)

            def make_q(i):
                dve.wait_ge(s["q_ps"], i + 1)
                dve.wait_ge(s["xa_ps"], i)
                for c in range(2):
                    st = nc.vector.tensor_scalar(q[:, c, :, :], psum[0:DC, 2 + c, 0:2 * N].rearrange("p (b n) -> p b n", b=2),
                                                 thr_c[:, c:c + 1], None, ALU.is_ge)
                st.then_inc(s["q_ready"], 1)

            def make_kv(i):
                dve.wait_ge(s["kv_ps"], i + 1)
                dve.wait_ge(s["kvh_ps"], i)
                nc.vector.tensor_tensor(kv[:, :, :], psum[:, 4:8, 0:2 * D],
                                        thr_r[:, D:3 * D].unsqueeze(1).to_broadcast([128, 4, 2 * D]),
                                        ALU.is_ge).then_inc(s["kv_ready"], 1)

            def residual(i, u, k):
                dve.wait_ge(s["sp_ps"], i + 1)
                nc.vector.tensor_tensor(spike[:, :, :], psum[:, 0:2, 0:2 * D].rearrange("p k (a d) -> p k a d", a=2),
                                        thr_r[:, 3 * D:4 * D].unsqueeze(1).unsqueeze(1).to_broadcast([128, 2, 2, D]),
                                        ALU.is_ge).then_inc(s["spike_ready"], 1)
                dve.wait_ge(s["spike_ready"], i + 1)
                dve.wait_ge(res_in[u], k * 64 + 64)
                dve.wait_ge(s["h1_out"], i * 64)
                nc.vector.tensor_tensor(h1[:, :, :], hr[:, u, :, :], spike[:, :, :], ALU.add).then_inc(s["h1_ready"], 1)
                dve.wait_ge(s["h1_ready"], i + 1)
                for j in range(4):
                    st = nc.vector.bn_stats(stats1[:, j, :], h1[:, j, :])
                ch.link(st, apart=True)
                for j in range(4):
                    st = nc.vector.bn_aggr(mv1[:, j, :], stats1[:, j, :])
                ch.link(st)
                ch.link(nc.vector.tensor_scalar(g[:, 0, :], mv1[:, :, 1], LN_EPS, None, ALU.add))
                ch.link(nc.vector.reciprocal(g[:, 1, :], g[:, 0, :]))
                ch.link(nc.vector.tensor_tensor(g[:, 1, :], g[:, 1, :], mv1[:, :, 1], ALU.mult))
                nc.vector.tensor_scalar(g[:, 1, :], g[:, 1, :], float(D), 1e-24, ALU.mult, ALU.max).then_inc(s["mv1_ready"], 1)

            normed(0, 0, 0)
            make_y(0, 0)

            def turn(i, u, k, middle, last):
                following = not (isinstance(i, int) and i == TURNS - 1)
                before = k if u else k - 1
                if last:
                    ch.base, ch.n = FIRST + (i - 2) * ALL, 0
                if middle:
                    mask_kv(i - 1)
                if last:
                    make_xn(i - 2)
                if following:
                    normed(i + 1, 1 - u, k if not u else k + 1)
                if middle:
                    make_xs(i - 1)
                make_q(i)
                if following:
                    make_y(i + 1, 1 - u)
                make_kv(i)
                if middle:
                    residual(i - 1, 1 - u, before)
            turns(dve, turn)
            mask_kv(TURNS - 1)
            make_xn(TURNS - 2)
            make_xs(TURNS - 1)
            residual(TURNS - 1, 1, TURNS // 2 - 1)
            make_xn(TURNS - 1)

        @block.scalar
        def _(act):
            act.wait_ge(s["root"], 1)
            nc.scalar.activation(prm_c[:, 4, :], prm_c[:, 4, :], ACT.Sqrt).then_inc(s["root"], 1)
            act.wait_ge(s["root"], 3)
            nc.scalar.activation(prm_r[:, 4, :], prm_r[:, 4, :], ACT.Sqrt).then_inc(s["root"], 1)
            for c in range(2):
                act.wait_ge(s["w_turned"], c + 1)
                nc.scalar.copy(wT[:, c, :].rearrange("p (k o) -> p k o", k=2),
                               psum[0:DC, 2 * c:2 * c + 2, 0:4 * DC]).then_inc(s["w_out"], 1)

            def copy_yT(i):
                act.wait_ge(s["yT_ps"], i + 1)
                act.wait_ge(s["kv_ps"], i)
                nc.scalar.copy(yT[:, :, :, :], psum[0:DC, 0:2, 0:2 * N].rearrange("p c (b n) -> p c b n", b=2)).then_inc(s["yT_ready"], 1)

            def copy_xnT(i):
                act.wait_ge(s["xnT_ps"], i + 1)
                act.wait_ge(s["xnT_out"], i * 32)
                nc.scalar.copy(xnT[:, :, :, :], psum[0:DC, 2:4, 0:2 * N].rearrange("p c (b n) -> p c b n", b=2)).then_inc(s["xnT_ready"], 1)

            def turn(i, u, k, middle, last):
                copy_yT(i)
                if last:
                    copy_xnT(i - 2)
            turns(act, turn)
            copy_xnT(TURNS - 2)
            copy_xnT(TURNS - 1)

        @block.tensor
        def _(pe):
            pe.wait_ge(s["wrow_ready"], 1)
            for c in range(2):
                for k in range(8):
                    mm = nc.tensor.transpose(psum[0:DC, 2 * c + k // 4, (k % 4) * DC:(k % 4) * DC + DC],
                                             wrow[:, k, c * DC:c * DC + DC], ident[0:DC, 0:DC])
                mm.then_inc(s["w_turned"], 1)
            pe.wait_ge(s["w_out"], 2)

            def turned(src, bank):
                for c in range(2):
                    for b in range(2):
                        for tile in range(2):
                            rows, at = TILE_ROWS[tile], b * N + TILE_AT[tile]
                            mm = nc.tensor.transpose(psum[0:DC, bank + c, at:at + rows],
                                                     src[0:rows, 2 * b + tile, c * DC:c * DC + DC], ident[0:rows, 0:rows])
                return mm

            def turn_y(i):
                pe.wait_ge(s["y_ready"], i + 1)
                if not (isinstance(i, int) and i < 2):
                    pe.wait_ge(s["spike_ready"], i - 1)
                turned(y, 0).then_inc(s["yT_ps"], 1)

            def product_kv(i):
                pe.wait_ge(s["kv_ready"], i + 1)
                for b in range(2):
                    for c in range(2):
                        for tile in range(2):
                            rows = TILE_ROWS[tile]
                            mm = nc.tensor.matmul(psum[0:DC, 4, b * D + c * DC:b * D + c * DC + DC],
                                                  kv[0:rows, 2 * b + tile, c * DC:c * DC + DC],
                                                  kv[0:rows, 2 * b + tile, D + c * DC:D + c * DC + DC],
                                                  start=(tile == 0), stop=(tile == 1))
                mm.then_inc(s["kvh_ps"], 1)

            def project_q(i):
                pe.wait_ge(s["yT_ready"], i + 1)
                if not (isinstance(i, int) and i < 3):
                    pe.wait_ge(s["xnT_ready"], i - 2)
                pe.wait_ge(s["q_ready"], i)
                for m in range(2):
                    for c in range(2):
                        mm = nc.tensor.matmul(psum[0:DC, 2 + m, 0:2 * N], wT[:, c, m * DC:m * DC + DC],
                                              yT[:, c, :, :], start=(c == 0), stop=(c == 1))
                mm.then_inc(s["q_ps"], 1)

            def attend(i):
                pe.wait_ge(s["kvh_ready"], i + 1)
                pe.wait_ge(s["q_ready"], i + 1)
                pe.wait_ge(s["kv_ready"], i + 1)
                for b in range(2):
                    for c in range(2):
                        mm = nc.tensor.matmul(psum[0:DC, 5 + c, b * N:b * N + N], kvh[:, b, c, :], q[:, c, b, :],
                                              start=True, stop=True)
                mm.then_inc(s["xa_ps"], 1)

            def project_kv(i, middle):
                pe.wait_ge(s["kv_ready"], i)
                for n, j in enumerate((3, 0, 1, 2)):
                    if n == 1 and middle:
                        pe.wait_ge(s["kvh_ready"], i)
                    if n == 2 and middle:
                        pe.wait_ge(s["xs_ready"], i)
                    at = TILE_AT[j % 2]
                    for c in range(2):
                        mm = nc.tensor.matmul(psum[:, 4 + j, 0:2 * D], yT[:, c, j // 2, at:at + 128],
                                              wT[:, c, D:3 * D], start=(c == 0), stop=(c == 1))
                mm.then_inc(s["kv_ps"], 1)

            def turn_xn(i, latest):
                pe.wait_ge(s["xn_ready"], i + 1)
                pe.wait_ge(s["q_ready"], latest)
                pe.wait_ge(s["xnT_ready"], i)
                turned(xn, 2).then_inc(s["xnT_ps"], 1)

            def spikes(i, latest):
                pe.wait_ge(s["xs_ready"], i + 1)
                pe.wait_ge(s["yT_ready"], latest)
                for j in range(4):
                    at = TILE_AT[j % 2]
                    for c in range(2):
                        mm = nc.tensor.matmul(psum[:, j // 2, (j % 2) * D:(j % 2) * D + D], xs[:, c, j // 2, at:at + 128],
                                              wT[:, c, 3 * D:4 * D], start=(c == 0), stop=(c == 1))
                mm.then_inc(s["sp_ps"], 1)

            def turn(i, u, k, middle, last):
                turn_y(i)
                if middle:
                    product_kv(i - 1)
                project_q(i)
                if middle:
                    attend(i - 1)
                project_kv(i, middle)
                if last:
                    turn_xn(i - 2, i + 1)
                if middle:
                    spikes(i - 1, i + 1)
            turns(pe, turn)
            product_kv(TURNS - 1)
            attend(TURNS - 1)
            turn_xn(TURNS - 2, TURNS)
            pe.wait_ge(s["spike_ready"], TURNS - 1)
            spikes(TURNS - 1, TURNS)
            turn_xn(TURNS - 1, TURNS)


def dispatch(nc, t, psum, slotsT):
    HALF = 512
    with ExitStack() as ctx:
        def sb(name, shape, dt=FP32):
            return ctx.enter_context(nc.sbuf_tensor("dsp_" + name, shape, dt))

        ident = sb("ident", [128, 128])
        ones = sb("ones", [DC, DC])
        phin = sb("phin", [DC, 2, SLOTS])
        scale = sb("scale", [DC, 1])
        xn = sb("xn", [128, 2, 2, D])
        xnT = sb("xnT", [DC, 2, 2, N])
        e = sb("e", [128, 2, 2, SLOTS])
        dw = sb("dw", [128, 2, 2, SLOTS])
        m = sb("m", [128, 2, E0])
        top = sb("top", [128, 2])
        mg = sb("mg", [128, 2, E0])
        se = sb("se", [128, 2, E0])
        rse = sb("rse", [128, 2, E0])
        sg = sb("sg", [128, 2, E0])
        z = sb("z", [128, 2])
        kc = sb("kc", [128, 2, 2, E0])
        cwT = sb("cwT", [128, NG, N])
        s = phase_sems(ctx, nc, "dsp", "consts_in ones_ready sq_ready norm_ps norm2 root phin_ready in0 in1 logits shifted mg_ready exped gexped "
                 "dw_ready kc_ready cw_ready slots_ps slots_out cwT_ps cwT_out cwT_stored chain")
        block = ctx.enter_context(nc.Block())
        s_in = (s["in0"], s["in1"])
        sq = dw[0:DC, 0, :, :]
        nrm = dw[0:DC, 1, 0, :]

        def run(eng, turn):
            turn(0, 0, 0)
            with eng.Fori(0, B // 2 - 1) as pair:
                turn(pair * 2 + 1, 1, pair)
                turn(pair * 2 + 2, 0, pair + 1)
            turn(B - 1, 1, B // 2 - 1)

        @block.sync
        def _(sp):
            sp.dma_start(ident[:, :], t["ident"]).then_inc(s["consts_in"], 16)
            sp.dma_start(phin[:, :, :], t["ffn_phi"].rearrange("(c p) e s -> p c (e s)", p=DC)).then_inc(s["consts_in"], 16)
            sp.dma_start(scale[:, :], row_bc(t["ffn_scale"], DC)).then_inc(s["consts_in"], 16)

            def load(b, u):
                sp.dma_start(xn[:, u, 0, :], t["xn_dram"][b, NPATCH:N, :]).then_inc(s_in[u], 16)
                sp.dma_start(xn[0:NPATCH, u, 1, :], t["xn_dram"][b, 0:NPATCH, :]).then_inc(s_in[u], 16)
                sp.dma_start(xnT[:, u, :, :], t["xnT_dram"][b, :, :, :].rearrange("c p n -> p c n")).then_inc(s_in[u], 16)

            def store(b):
                sp.wait_ge(s["cwT_out"], 3 * b + 3)
                sp.dma_start(t["cwT_dram"][b, :, :, :].rearrange("g p n -> p g n"), cwT[:, :, :]).then_inc(s["cwT_stored"], 16)

            load(0, 0)
            load(1, 1)
            with sp.Fori(0, B // 2 - 1) as pair:
                for u in range(2):
                    b = pair * 2 + u
                    sp.wait_ge(s["slots_ps"], 2 * b + 2)
                    load(b + 2, u)
                    store(b)
            store(B - 2)
            store(B - 1)
            sp.wait_ge(s["cwT_stored"], 16 * B)

        @block.vector
        def _(dve):
            ch = Chain(dve, s["chain"])
            nc.vector.memset(ones[:, :], 1.0).then_inc(s["ones_ready"], 1)
            dve.wait_ge(s["consts_in"], 48)
            nc.vector.tensor_tensor(sq, phin[:, :, :], phin[:, :, :], ALU.mult).then_inc(s["sq_ready"], 1)
            dve.wait_ge(s["norm_ps"], 1)
            nc.vector.tensor_scalar(nrm, psum[0:DC, 0:2, :].rearrange("p a b -> p (a b)"), 1e-24, None, ALU.max).then_inc(s["norm2"], 1)
            dve.wait_ge(s["root"], 1)
            ch.link(nc.vector.reciprocal(nrm, nrm))
            ch.link(nc.vector.tensor_scalar(nrm, nrm, scale[:, :], None, ALU.mult))
            nc.vector.tensor_tensor(phin[:, :, :], phin[:, :, :], nrm.unsqueeze(1).to_broadcast([DC, 2, SLOTS]),
                                    ALU.mult).then_inc(s["phin_ready"], 1)
            dve.wait_ge(s["phin_ready"], 1)
            LINKS = 6

            def turn(b, u, k):
                ch.base, ch.n = 3 - 1 + b * LINKS, 0
                lg = psum[:, 0:4, :].rearrange("p k (e s) -> p (k e) s", s=S0)
                dve.wait_ge(s["logits"], b + 1)
                ch.link(nc.vector.tensor_reduce(m[:, :, :].rearrange("p t e -> p (t e)"), lg, AXX, ALU.max))
                dve.wait_ge(s["gexped"], b)
                if not (isinstance(b, int) and b < 2):
                    dve.wait_ge(s["cwT_ps"], b - 1)
                nc.vector.tensor_tensor(e[:, u, :, :].rearrange("p t (e s) -> p (t e) s", s=S0), lg,
                                        m[:, :, :].rearrange("p t e -> p (t e)").unsqueeze(2).to_broadcast([128, 2 * E0, S0]),
                                        ALU.subtract).then_inc(s["shifted"], 1)
                ch.link(nc.vector.tensor_reduce(top[:, :], m[:, :, :], AXX, ALU.max))
                nc.vector.tensor_tensor(mg[:, :, :], m[:, :, :], top[:, :].unsqueeze(2).to_broadcast([128, 2, E0]),
                                        ALU.subtract).then_inc(s["mg_ready"], 1)
                dve.wait_ge(s["exped"], b + 1)
                ch.link(nc.vector.tensor_reduce(se[:, :, :].rearrange("p t e -> p (t e)"),
                                                e[:, u, :, :].rearrange("p t (e s) -> p (t e) s", s=S0), AXX, ALU.add))
                dve.wait_ge(s["gexped"], b + 1)
                nc.vector.reciprocal(rse[:, :, :], se[:, :, :])
                ch.link(nc.vector.tensor_tensor(sg[:, :, :], se[:, :, :], mg[:, :, :], ALU.mult))
                ch.link(nc.vector.tensor_reduce(z[:, :], sg[:, :, :], AXX, ALU.add))
                ch.link(nc.vector.reciprocal(z[:, :], z[:, :]))
                nc.vector.tensor_tensor(kc[:, u, :, :], mg[:, :, :], z[:, :].unsqueeze(2).to_broadcast([128, 2, E0]),
                                        ALU.mult).then_inc(s["kc_ready"], 1)
                if not (isinstance(b, int) and b < 2):
                    dve.wait_ge(s["slots_ps"], 2 * b - 2)
                nc.vector.tensor_tensor(dw[:, u, :, :].rearrange("p t (e s) -> p (t e) s", s=S0),
                                        e[:, u, :, :].rearrange("p t (e s) -> p (t e) s", s=S0),
                                        rse[:, :, :].rearrange("p t e -> p (t e)").unsqueeze(2).to_broadcast([128, 2 * E0, S0]),
                                        ALU.mult).then_inc(s["dw_ready"], 1)
                dve.wait_ge(s["dw_ready"], b + 1)
            run(dve, turn)

        @block.gpsimd
        def _(pool):
            def turn(b, u, k):
                pool.wait_ge(s["kc_ready"], b + 1)
                pool.wait_ge(s["dw_ready"], b + 1)
                for tile in range(2):
                    ev = e[:, u, tile, :].rearrange("p (e s) -> p e s", s=S0)
                    nc.gpsimd.tensor_tensor(ev, ev, kc[:, u, tile, :].unsqueeze(2).to_broadcast([128, E0, S0]),
                                            ALU.mult).then_inc(s["cw_ready"], 1)
            run(pool, turn)

        @block.scalar
        def _(act):
            act.wait_ge(s["norm2"], 1)
            nc.scalar.activation(nrm, nrm, ACT.Sqrt).then_inc(s["root"], 1)

            def softmax(b, u):
                act.wait_ge(s["shifted"], b + 1)
                nc.scalar.activation(e[:, u, :, :], e[:, u, :, :], ACT.Exp).then_inc(s["exped"], 1)
                act.wait_ge(s["mg_ready"], b + 1)
                nc.scalar.activation(mg[:, :, :], mg[:, :, :], ACT.Exp).then_inc(s["gexped"], 1)

            def evacuate(b, u):
                for c in range(2):
                    act.wait_ge(s["slots_ps"], 2 * b + c + 1)
                    nc.scalar.copy(slotsT[:, c, :, b, :],
                                   psum[0:DC, 4 + 2 * c:6 + 2 * c, :].rearrange("p k (e s) -> p (k e) s", s=S0)).then_inc(s["slots_out"], 1)
                act.wait_ge(s["cwT_ps"], b + 1)
                act.wait_ge(s["cwT_stored"], b * 16)
                for k in range(3):
                    n = min(3, NG - 3 * k)
                    nc.scalar.copy(cwT[:, 3 * k:3 * k + n, :],
                                   psum[:, 4 + k, 0:n * N].rearrange("p (g n) -> p g n", g=n)).then_inc(s["cwT_out"], 1)

            def turn(b, u, k):
                softmax(b, u)
                if not isinstance(b, int) or b:
                    evacuate(b - 1, 1 - u)
            run(act, turn)
            evacuate(B - 1, 1)

        @block.tensor
        def _(pe):
            pe.wait_ge(s["ones_ready"], 1)
            pe.wait_ge(s["sq_ready"], 1)
            for k in range(2):
                for c in range(2):
                    mm = nc.tensor.matmul(psum[0:DC, k, :], ones[:, :], sq[:, c, k * HALF:k * HALF + HALF],
                                          start=(c == 0), stop=(c == 1))
            mm.then_inc(s["norm_ps"], 1)
            pe.wait_ge(s["phin_ready"], 1)

            def logits(b, u, k):
                pe.wait_ge(s_in[u], 48 * k + 48)
                pe.wait_ge(s["shifted"], b)
                for tile in range(2):
                    at = TILE_AT[tile]
                    for k in range(2):
                        for c in range(2):
                            mm = nc.tensor.matmul(psum[:, 2 * tile + k, :], xnT[:, u, c, at:at + 128],
                                                  phin[:, c, k * HALF:k * HALF + HALF], start=(c == 0), stop=(c == 1))
                mm.then_inc(s["logits"], 1)

            def slots(b, u):
                pe.wait_ge(s["dw_ready"], b + 1)
                pe.wait_ge(s["cwT_out"], 3 * b)
                pe.wait_ge(s["slots_out"], 2 * b)
                for c in range(2):
                    for k in range(2):
                        for tile in range(2):
                            rows = TILE_ROWS[tile]
                            mm = nc.tensor.matmul(psum[0:DC, 4 + 2 * c + k, :], xn[0:rows, u, tile, c * DC:c * DC + DC],
                                                  dw[0:rows, u, tile, k * HALF:k * HALF + HALF],
                                                  start=(tile == 0), stop=(tile == 1))
                    mm.then_inc(s["slots_ps"], 1)
                pe.wait_ge(s["cw_ready"], 2 * b + 2)
                pe.wait_ge(s["slots_out"], 2 * b + 2)
                for g in range(NG):
                    for tile in range(2):
                        rows, at = TILE_ROWS[tile], (g % 3) * N + TILE_AT[tile]
                        mm = nc.tensor.transpose(psum[:, 4 + g // 3, at:at + rows],
                                                 e[0:rows, u, tile, 128 * g:128 * g + 128], ident[0:rows, 0:rows])
                mm.then_inc(s["cwT_ps"], 1)

            def turn(b, u, k):
                logits(b, u, k)
                if not isinstance(b, int) or b:
                    slots(b - 1, 1 - u)
            run(pe, turn)
            slots(B - 1, 1)


def soft_experts(nc, t, psum, slotsT):
    HJ = H0 // 128
    ROWS = B * S0
    with ExitStack() as ctx:
        def sb(name, shape, dt=FP32):
            return ctx.enter_context(nc.sbuf_tensor("exp_" + name, shape, dt))

        ident = sb("ident", [128, 128])
        b1rows = sb("b1rows", [DC, 2, 128])
        b1T = sb("b1T", [128, E0 * HJ])
        w1 = sb("w1", [DC, 2, 2, H0])
        w2 = sb("w2", [128, 2, HJ, D])
        b2 = sb("b2", [128, 2, D])
        hT = sb("hT", [128, 2, HJ, ROWS])
        eo = sb("eo", [128, 2, 4, D])
        s = phase_sems(ctx, nc, "exp", "consts_in b1_ps b1_ready w1_in0 w1_in1 w2_in0 w2_in1 h_ps h_ready o_ps o_ready0 o_ready1 stored0 stored1")
        block = ctx.enter_context(nc.Block())
        o_ready = (s["o_ready0"], s["o_ready1"])
        w1_in, w2_in, stored = (s["w1_in0"], s["w1_in1"]), (s["w2_in0"], s["w2_in1"]), (s["stored0"], s["stored1"])
        eo_view = t["eo_dram"].rearrange("(t q) k d -> q k t d", q=4)

        def run(eng, turn):
            turn(0, 0, 0, 0)
            with eng.Fori(0, E0 // 2 - 1) as pair:
                turn(pair * 2 + 1, 1, pair, pair)
                turn(pair * 2 + 2, 0, pair + 1, pair)
            turn(E0 - 1, 1, E0 // 2 - 1, E0 // 2 - 1)

        @block.sync
        def _(sp):
            sp.dma_start(ident[:, :], t["ident"]).then_inc(s["consts_in"], 16)
            sp.dma_start(b1rows[:, :, :], t["ffn_b1"].rearrange("(c e) (j p) -> (e j) c p", c=2, p=128)).then_inc(s["consts_in"], 16)

            def load_w1(e, u):
                sp.dma_start(w1[:, u, :, :], t["ffn_w1"][e, :, :].rearrange("(c p) h -> p c h", p=DC)).then_inc(w1_in[u], 16)

            def load_w2(e, u):
                sp.dma_start(w2[:, u, :, :], t["ffn_w2"][e, :, :].rearrange("(j p) d -> p j d", p=128)).then_inc(w2_in[u], 16)
                sp.dma_start(b2[:, u, :], row_bc(t["ffn_b2"][e, :], 128)).then_inc(w2_in[u], 16)

            for e in range(2):
                load_w1(e, e)
                load_w2(e, e)
            with sp.Fori(0, E0 // 2 - 1) as pair:
                for u in range(2):
                    e = pair * 2 + u
                    sp.wait_ge(s["h_ps"], HJ * e + HJ)
                    load_w1(e + 2, u)
                    sp.wait_ge(s["o_ready0"], e + 1)
                    sp.wait_ge(s["o_ready1"], e + 1)
                    load_w2(e + 2, u)

        @block.gpsimd
        def _(pool):
            def turn(e, u, k, before):
                pool.wait_ge(s["o_ready0"], e + 1)
                pool.wait_ge(s["o_ready1"], e + 1)
                for q in range(4):
                    pool.dma_start(eo_view[q, bass.ds(e * S0, S0), :, :], eo[S0 * q:S0 * q + S0, u, :, :]).then_inc(stored[u], 16)
            run(pool, turn)
            for u in range(2):
                pool.wait_ge(stored[u], 64 * (E0 // 2))

        @block.scalar
        def _(act):
            act.wait_ge(s["b1_ps"], 1)
            nc.scalar.copy(b1T[:, :], psum[:, 0, 0:E0 * HJ]).then_inc(s["b1_ready"], 1)
            act.wait_ge(s["b1_ready"], 1)

            def turn(e, u, k, before):
                if not (isinstance(e, int) and e < 2):
                    act.wait_ge(s["o_ps"], 2 * e - 2)
                for j in range(HJ):
                    act.wait_ge(s["h_ps"], HJ * e + j + 1)
                    nc.scalar.activation(hT[:, u, j, :], psum[:, j, :], ACT.Gelu,
                                         bias=b1T[:, bass.ds(e * HJ + j, 1)]).then_inc(s["h_ready"], 1)
            run(act, turn)

        @block.vector
        def _(dve):
            def turn(e, u, k, before):
                dve.wait_ge(w2_in[u], 32 * k + 32)
                dve.wait_ge(stored[u], 64 * k)
                for n in range(2):
                    dve.wait_ge(s["o_ps"], 2 * e + n + 1)
                    nc.vector.tensor_tensor(eo[:, u, 2 * n:2 * n + 2, :],
                                            psum[:, 6 + n, 0:2 * D].rearrange("p (a d) -> p a d", a=2),
                                            b2[:, u, :].unsqueeze(1).to_broadcast([128, 2, D]), ALU.add).then_inc(o_ready[n], 1)
            run(dve, turn)

        @block.tensor
        def _(pe):
            pe.wait_ge(s["consts_in"], 32)
            for c in range(2):
                mm = nc.tensor.transpose(psum[:, 0, c * DC:c * DC + DC], b1rows[:, c, :], ident[0:DC, 0:DC])
            mm.then_inc(s["b1_ps"], 1)
            pe.wait_ge(s["b1_ready"], 1)

            def hidden(e, u, k):
                pe.wait_ge(w1_in[u], 16 * k + 16)
                for j in range(HJ):
                    if not (isinstance(e, int) and e == 0):
                        pe.wait_ge(s["h_ready"], HJ * (e - 1) + j + 1)
                    for c in range(2):
                        mm = nc.tensor.matmul(psum[:, j, :], w1[:, u, c, 128 * j:128 * j + 128], slotsT[:, c, e, :, :],
                                              start=(c == 0), stop=(c == 1))
                    mm.then_inc(s["h_ps"], 1)

            def output(e, u, k):
                pe.wait_ge(w2_in[u], 32 * k + 32)
                pe.wait_ge(s["h_ready"], HJ * e + HJ)
                for n in range(2):
                    pe.wait_ge(o_ready[n], e)
                    for a in range(2):
                        for j in range(HJ):
                            at = 128 * (2 * n + a)
                            mm = nc.tensor.matmul(psum[:, 6 + n, a * D:a * D + D], hT[:, u, j, at:at + 128], w2[:, u, j, :],
                                                  start=(j == 0), stop=(j == HJ - 1))
                    mm.then_inc(s["o_ps"], 1)

            def turn(e, u, k, before):
                hidden(e, u, k)
                if not (isinstance(e, int) and e == 0):
                    output(e - 1, 1 - u, before)
            run(pe, turn)
            output(E0 - 1, 1, E0 // 2 - 1)


def soft_mixture(nc, t, psum):
    with nc.sbuf_tensor("slotsT", [DC, 2, E0, B, S0], FP32) as slotsT:
        dispatch(nc, t, psum, slotsT)
        soft_experts(nc, t, psum, slotsT)


def combine(nc, t, psum, th):
    RESO = 4 * HEADS
    with ExitStack() as ctx:
        def sb(name, shape, dt=FP32):
            return ctx.enter_context(nc.sbuf_tensor("cmb_" + name, shape, dt))

        ident = sb("ident", [128, 128])
        half = sb("half", [128, 2])
        lnw = sb("lnw", [DC, 2])
        wcomp = sb("wcomp", [DC, 2, 128])
        wreso = sb("wreso", [128, RESO])
        cw = sb("cw", [128, 2, NG, N])
        eo = sb("eo", [128, 2, NG, D])
        h1 = sb("h1", [128, 2, 2, D])
        h2 = sb("h2", [128, 2, D])
        stats = sb("stats", [128, 2, 6])
        mv = sb("mv", [128, 2, 2])
        g = sb("g", [128, 3, 2])
        r = sb("r", [128, 2, 2])
        y = sb("y", [128, 2, D])
        xr = sb("xr", [128, 2, D])
        xrT = sb("xrT", [DC, 2, N])
        lth = sb("lth", [128, N])
        lat = sb("lat", [128, N])
        s = phase_sems(ctx, nc, "cmb", "consts_in wcomp_ready half_ready in0 in1 comb_ps h2_ready var_ready r_ready y_ready y_stored h2_stored xr_ready "
                 "xrT_ps xrT_ready lat_ps lth_ready lat_ready lat_stored reso_ps th_ready chain passed")
        block = ctx.enter_context(nc.Block())
        s_in = (s["in0"], s["in1"])
        LOADS = 4 * 16

        def run(eng, turn):
            turn(0, 0, 0)
            with eng.Fori(0, B // 2 - 1) as pair:
                turn(pair * 2 + 1, 1, pair)
                turn(pair * 2 + 2, 0, pair + 1)
            turn(B - 1, 1, B // 2 - 1)

        @block.sync
        def _(sp):
            sp.dma_start(ident[:, :], t["ident"]).then_inc(s["consts_in"], 16)
            sp.dma_start(lnw[:, :], t["attn_ln_w"].rearrange("(c p) -> p c", p=DC), allow_slow_non_contiguous=True).then_inc(s["consts_in"], 16)
            sp.dma_start(wcomp[:, :, :], t["attn_w_comp"].rearrange("(c p) k -> p c k", p=DC)).then_inc(s["consts_in"], 16)
            sp.dma_start(wreso[:, :], t["attn_w_reso"]).then_inc(s["consts_in"], 16)

            def load(b, u):
                sp.dma_start(cw[:, u, :, :], t["cwT_dram"][b, :, :, :].rearrange("g p n -> p g n")).then_inc(s_in[u], 16)
                sp.dma_start(eo[:, u, :, :], t["eo_dram"][b, :, :].rearrange("(g p) d -> p g d", p=128)).then_inc(s_in[u], 16)
                for tile in range(2):
                    sp.dma_start(h1[:, u, tile, :], t["h1_dram"][b, TILE_AT[tile]:TILE_AT[tile] + 128, :]).then_inc(s_in[u], 16)

            def store(b):
                sp.wait_ge(s["h2_ready"], b + 1)
                sp.dma_start(t["h2_dram"][b, NPATCH:N, :], h2[:, 0, :]).then_inc(s["h2_stored"], 16)
                sp.dma_start(t["h2_dram"][b, 0:NPATCH, :], h2[0:NPATCH, 1, :]).then_inc(s["h2_stored"], 16)
                sp.wait_ge(s["y_ready"], b + 1)
                sp.dma_start(t["y3_dram"][b, NPATCH:N, :], y[:, 0, :]).then_inc(s["y_stored"], 16)
                sp.dma_start(t["y3_dram"][b, 0:NPATCH, :], y[0:NPATCH, 1, :]).then_inc(s["y_stored"], 16)
                sp.wait_ge(s["lat_ready"], b + 1)
                sp.dma_start(t["lat_dram"][b, :, :], lat[:, :]).then_inc(s["lat_stored"], 16)

            load(0, 0)
            load(1, 1)
            with sp.Fori(0, B // 2 - 1) as pair:
                for u in range(2):
                    b = pair * 2 + u
                    sp.wait_ge(s["h2_ready"], b + 1)
                    load(b + 2, u)
                    store(b)
            store(B - 2)
            store(B - 1)
            sp.wait_ge(s["h2_stored"], 32 * B)
            sp.wait_ge(s["y_stored"], 32 * B)
            sp.wait_ge(s["lat_stored"], 16 * B)

        @block.gpsimd
        def _(pool):
            nc.gpsimd.memset(half[:, :], -0.5).then_inc(s["half_ready"], 1)
            pool.wait_ge(s["half_ready"], 1)

            def turn(b, u, k):
                pool.wait_ge(s["var_ready"], b + 1)
                nc.gpsimd.tensor_tensor(r[:, :, :], g[:, 0:2, :], half[:, :].unsqueeze(1).to_broadcast([128, 2, 2]),
                                        ALU.pow).then_inc(s["r_ready"], 1)
            run(pool, turn)

        @block.vector
        def _(dve):
            ch = Chain(dve, s["chain"], s["passed"])
            dve.wait_ge(s["consts_in"], 64)
            nc.vector.tensor_tensor(wcomp[:, :, :], wcomp[:, :, :], lnw[:, :].unsqueeze(2).to_broadcast([DC, 2, 128]),
                                    ALU.mult).then_inc(s["wcomp_ready"], 1)
            LINKS = 5

            def turn(b, u, k):
                ch.base, ch.n = b * LINKS, 0
                dve.wait_ge(s_in[u], LOADS * k + LOADS)
                dve.wait_ge(s["comb_ps"], b + 1)
                dve.wait_ge(s["h2_stored"], 32 * b)
                nc.vector.tensor_tensor(h2[:, :, :], psum[:, 0:2, 0:D], h1[:, u, :, :], ALU.add).then_inc(s["h2_ready"], 1)
                dve.wait_ge(s["h2_ready"], b + 1)
                for j in range(2):
                    st = nc.vector.bn_stats(stats[:, j, :], h2[:, j, :])
                ch.link(st, apart=True)
                for j in range(2):
                    st = nc.vector.bn_aggr(mv[:, j, :], stats[:, j, :])
                ch.link(st)
                dve.wait_ge(s["r_ready"], b)
                dve.wait_ge(s["xr_ready"], b)
                ch.link(nc.vector.tensor_scalar(g[:, 0, :], mv[:, :, 1], LN_EPS, None, ALU.add))
                ch.link(nc.vector.reciprocal(g[:, 2, :], g[:, 0, :]))
                ch.link(nc.vector.tensor_tensor(g[:, 2, :], g[:, 2, :], mv[:, :, 1], ALU.mult))
                nc.vector.tensor_scalar(g[:, 1, :], g[:, 2, :], RMS_EPS, None, ALU.add).then_inc(s["var_ready"], 1)
                dve.wait_ge(s["r_ready"], b + 1)
                dve.wait_ge(s["y_stored"], 32 * b)
                for j in range(2):
                    st = nc.vector.tensor_scalar(y[:, j, :], h2[:, j, :], mv[:, j, 0:1], r[:, 0, j:j + 1],
                                                 ALU.subtract, ALU.mult)
                st.then_inc(s["y_ready"], 1)
                dve.wait_ge(s["y_ready"], b + 1)
                dve.wait_ge(s["xrT_ps"], b)
                for j in range(2):
                    st = nc.vector.tensor_scalar(xr[:, j, :], y[:, j, :], r[:, 1, j:j + 1], None, ALU.mult)
                st.then_inc(s["xr_ready"], 1)
                dve.wait_ge(s["lth_ready"], b + 1)
                dve.wait_ge(s["lat_stored"], 16 * b)
                dve.wait_ge(s["reso_ps"], b)
                nc.vector.scalar_tensor_tensor(lat[:, :], lth[:, :], 1.0, psum[:, 4, 0:N], ALU.add, ALU.mult).then_inc(s["lat_ready"], 1)
            run(dve, turn)

        @block.scalar
        def _(act):
            def turn(b, u, k):
                act.wait_ge(s["xrT_ps"], b + 1)
                act.wait_ge(s["lat_ps"], b)
                nc.scalar.copy(xrT[:, :, :], psum[0:DC, 2:4, 0:N]).then_inc(s["xrT_ready"], 1)
                act.wait_ge(s["lat_ps"], b + 1)
                act.wait_ge(s["lat_ready"], b)
                nc.scalar.activation(lth[:, :], psum[:, 4, 0:N], ACT.Tanh, scale=0.5).then_inc(s["lth_ready"], 1)
                act.wait_ge(s["reso_ps"], b + 1)
                nc.scalar.activation(th[:, b, :, :], psum[:, 5, 0:2 * RESO].rearrange("p (t k) -> p t k", t=2),
                                     ACT.Tanh, scale=0.25).then_inc(s["th_ready"], 1)
            run(act, turn)

        @block.tensor
        def _(pe):
            pe.wait_ge(s["consts_in"], 64)

            def product(b, u, k):
                pe.wait_ge(s_in[u], LOADS * k + LOADS)
                pe.wait_ge(s["h2_ready"], b)
                for tile in range(2):
                    at = TILE_AT[tile]
                    for n in range(NG):
                        mm = nc.tensor.matmul(psum[:, tile, 0:D], cw[:, u, n, at:at + 128], eo[:, u, n, :],
                                              start=(n == 0), stop=(n == NG - 1))
                mm.then_inc(s["comb_ps"], 1)

            def latent(b):
                pe.wait_ge(s["xr_ready"], b + 1)
                pe.wait_ge(s["xrT_ready"], b)
                for c in range(2):
                    for tile in range(2):
                        rows, at = TILE_ROWS[tile], TILE_AT[tile]
                        mm = nc.tensor.transpose(psum[0:DC, 2 + c, at:at + rows], xr[0:rows, tile, c * DC:c * DC + DC],
                                                 ident[0:rows, 0:rows])
                mm.then_inc(s["xrT_ps"], 1)
                pe.wait_ge(s["xrT_ready"], b + 1)
                pe.wait_ge(s["lat_ready"], b)
                pe.wait_ge(s["wcomp_ready"], 1)
                for c in range(2):
                    mm = nc.tensor.matmul(psum[:, 4, 0:N], wcomp[:, c, :], xrT[:, c, :], start=(c == 0), stop=(c == 1))
                mm.then_inc(s["lat_ps"], 1)
                pe.wait_ge(s["lat_ready"], b + 1)
                pe.wait_ge(s["th_ready"], b)
                for tile in range(2):
                    at = TILE_AT[tile]
                    mm = nc.tensor.matmul(psum[:, 5, tile * RESO:tile * RESO + RESO], lat[:, at:at + 128], wreso[:, :],
                                          start=True, stop=True)
                mm.then_inc(s["reso_ps"], 1)

            def turn(b, u, k):
                product(b, u, k)
                if not (isinstance(b, int) and b == 0):
                    latent(b - 1)
            run(pe, turn)
            latent(B - 1)


def gates(nc, t, psum, th, vgate, decay):
    A = 2 * B
    PI = 3.141592653589793
    with ExitStack() as ctx:
        def sb(name, shape, dt=FP32):
            return ctx.enter_context(nc.sbuf_tensor("gat_" + name, shape, dt))

        hd = sb("hd", [128, HEADS])
        temp = sb("temp", [128, 1])
        pos = sb("pos", [128, 2])
        rate = sb("rate", [128, HEADS])
        ln = sb("ln", [128, HEADS])
        dt = sb("dt", [128, HEADS])
        rdf = sb("rdf", [128, 2, HEADS])
        z = sb("z", [128, A, HEADS])
        w = sb("w", [128, A, HEADS])
        p = sb("p", [128, A, HEADS])
        s = phase_sems(ctx, nc, "gat", "in_ sig ln_ready rate_ready df_arg df_ready arg arg_th chain")
        block = ctx.enter_context(nc.Block())
        q4 = th[:, :, :, :].rearrange("p b t (h k) -> p (b t) h k", k=4)

        @block.sync
        def _(sp):
            sp.dma_start(hd[:, :], row_bc(t["attn_head_decay"], 128)).then_inc(s["in_"], 16)
            sp.dma_start(temp[:, :], row_bc(t["attn_temperature"], 128)).then_inc(s["in_"], 16)
            sp.dma_start(pos[:, :], t["pos"]).then_inc(s["in_"], 16)

        @block.scalar
        def _(act):
            act.wait_ge(s["in_"], 48)
            nc.scalar.activation(rate[:, :], hd[:, :], ACT.Tanh, scale=0.5).then_inc(s["sig"], 1)
            act.wait_ge(s["rate_ready"], 1)
            nc.scalar.activation(ln[:, :], rate[:, :], ACT.Ln).then_inc(s["ln_ready"], 1)
            act.wait_ge(s["df_arg"], 1)
            nc.scalar.activation(decay[:, :, :], decay[:, :, :], ACT.Exp).then_inc(s["df_ready"], 1)
            act.wait_ge(s["arg"], 1)
            nc.scalar.activation(p[:, :, :], p[:, :, :], ACT.Tanh, scale=0.5).then_inc(s["arg_th"], 1)

        @block.vector
        def _(dve):
            ch = Chain(dve, s["chain"])
            dve.wait_ge(s["in_"], 48)
            dve.wait_ge(s["sig"], 1)
            ch.link(nc.vector.tensor_scalar(rate[:, :], rate[:, :], 0.65 / 2, 0.3 + 0.65 / 2, ALU.mult, ALU.add))
            nc.vector.tensor_scalar(rate[:, :], rate[:, :], 1e-5, 0.999, ALU.max, ALU.min).then_inc(s["rate_ready"], 1)
            dve.wait_ge(s["rate_ready"], 1)
            ch.link(nc.vector.tensor_scalar(dt[:, :], rate[:, :], -1.0, 1.0, ALU.mult, ALU.add))
            dve.wait_ge(s["ln_ready"], 1)
            for tile in range(2):
                st = nc.vector.tensor_scalar(decay[:, tile, :], ln[:, :], pos[:, tile:tile + 1], None, ALU.mult)
            st.then_inc(s["df_arg"], 1)
            ch.link(nc.vector.tensor_tensor(z[:, :, :], q4[:, :, :, 1], q4[:, :, :, 3], ALU.subtract))
            ch.link(nc.vector.tensor_scalar(z[:, :, :], z[:, :, :], PI / 4, None, ALU.mult))
            ch.link(nc.vector.tensor_tensor(w[:, :, :], z[:, :, :], z[:, :, :], ALU.mult))
            ch.link(nc.vector.tensor_scalar(p[:, :, :], w[:, :, :], 1 / 6227020800.0, None, ALU.mult))
            for c in (-1 / 39916800.0, 1 / 362880.0, -1 / 5040.0, 1 / 120.0, -1 / 6.0):
                ch.link(nc.vector.scalar_tensor_tensor(p[:, :, :], p[:, :, :], c, w[:, :, :], ALU.add, ALU.mult))
            ch.link(nc.vector.scalar_tensor_tensor(p[:, :, :], p[:, :, :], 1.0, z[:, :, :], ALU.add, ALU.mult))
            ch.link(nc.vector.tensor_tensor(p[:, :, :], p[:, :, :], p[:, :, :], ALU.mult))
            ch.link(nc.vector.tensor_scalar(p[:, :, :], p[:, :, :], -2.0, 1.0, ALU.mult, ALU.add))
            for k in (0, 2):
                ch.link(nc.vector.tensor_scalar(w[:, :, :], q4[:, :, :, k], 0.5, 0.5, ALU.mult, ALU.add))
                ch.link(nc.vector.tensor_tensor(p[:, :, :], p[:, :, :], w[:, :, :], ALU.mult))
            nc.vector.tensor_scalar(p[:, :, :], p[:, :, :], temp[:, :], None, ALU.mult).then_inc(s["arg"], 1)
            dve.wait_ge(s["df_ready"], 1)
            ch.link(nc.vector.tensor_scalar(rdf[:, :, :], decay[:, :, :], 1e-8, None, ALU.add))
            ch.link(nc.vector.reciprocal(rdf[:, :, :], rdf[:, :, :]))
            ch.link(nc.vector.tensor_tensor(rdf[:, :, :], rdf[:, :, :], dt[:, :].unsqueeze(1).to_broadcast([128, 2, HEADS]), ALU.mult))
            dve.wait_ge(s["arg_th"], 1)
            ch.link(nc.vector.tensor_scalar(p[:, :, :], p[:, :, :], 0.6, 0.5, ALU.mult, ALU.add))
            ch.link(nc.vector.tensor_scalar(p[:, :, :], p[:, :, :], 0.05, 0.95, ALU.max, ALU.min))
            for tile in range(2):
                ch.link(nc.vector.tensor_tensor(vgate[:, 0:B, tile, :],
                                                p[:, :, :].rearrange("p (b t) h -> p b t h", t=2)[:, :, tile, :],
                                                rdf[:, tile, :].unsqueeze(1).to_broadcast([128, B, HEADS]), ALU.mult))
            ch.link(nc.vector.tensor_copy(vgate[:, B, :, :], rdf[:, :, :]))


def decay_attention(nc, t, psum, vgate, decay):
    NHG = HEADS // 4
    QK = 2 * D
    with ExitStack() as ctx:
        def sb(name, shape, dt=FP32):
            return ctx.enter_context(nc.sbuf_tensor("dec_" + name, shape, dt))

        ident = sb("ident", [128, 128])
        half = sb("half", [128, 2])
        ones = sb("ones", [128, 1])
        causal = sb("causal", [128, 128])
        causal_b = sb("causal_b", [128, N])
        cosw = sb("cosw", [128, 2, 2, DH])
        sinw = sb("sinw", [128, 2, 2, DH])
        nw = sb("nw", [128, 2, DH])
        nwx = sb("nwx", [128, 2, DH])
        wqkv = sb("wqkv", [128, 3 * D])
        wog = sb("wog", [128, D])
        memn = sb("memn", [128, NHG])
        wproj = sb("wproj", [128, NHG, D])
        lat = sb("lat", [128, 2, N])
        y3 = sb("y3", [128, 2, 2, D])
        qk = sb("qk", [128, 2, QK])
        vo = sb("vo", [128, 2, 2 * D])
        sq = sb("sq", [128, 2, QK])
        ms = sb("ms", [128, 4 * HEADS])
        rt = sb("rt", [128, 4 * HEADS])
        rq = sb("rq", [128, 4 * HEADS])
        qa = sb("qa", [128, 2, QK])
        qb = sb("qb", [128, 2, QK])
        qe = sb("qe", [128, 2, QK])
        qp = sb("qp", [128, 2, D])
        qkf = sb("qkf", [128, 2, 2 * HEADS, 32])
        kr = sb("kr", [128, 2, D])
        qc = sb("qc", [128, 2, D])
        den = sb("den", [128, 2, HEADS])
        qkT = sb("qkT", [128, 2, NHG, N])
        kbd = sb("kbd", [128, NHG, 4, 32])
        ogt = sb("ogt", [128, 2, D])
        og = sb("og", [128, 2, 2, D])
        vg = sb("vg", [128, 2, HEADS, DH])
        vgb = sb("vgb", [128, 2, NHG, 4, 32])
        at_ = sb("at", [128, 4, NHG, 128])
        ap_ = sb("ap", [128, NHG, N])
        oT = sb("oT", [128, NHG, N])
        osq = sb("osq", [128, NHG, N])
        oss = sb("oss", [128, 2])
        ro = sb("ro", [128, 2])
        x2 = sb("x2", [128, 2, D])
        s = phase_sems(ctx, nc, "dec", "consts_in half_ready padded wproj_ready tables_ready zeroed in0 in1 y_in0 y_in1 wl_ps qk_out vo_out "
                       "sq_ready ms_ready rt_ready qb_ready qm_ready qe_ready kr_ready kc_ps qc_ready qkf_ready turned qkT_ready kbd_ready "
                       "ogt_ready og_ready vg_ready sc_ps scp_ps masked masked_p ov_ps oT_ready ss_ps mso_ready ro_ready pr_ps x2_ready "
                       "x2_stored chain")
        block = ctx.enter_context(nc.Block())
        s_in, y_in = (s["in0"], s["in1"]), (s["y_in0"], s["y_in1"])
        CONSTS = 9 + 6 + 4 + HEADS

        def run(eng, turn):
            turn(0, 0, 0, 0)
            with eng.Fori(0, B // 2 - 1) as pair:
                turn(pair * 2 + 1, 1, pair, pair)
                turn(pair * 2 + 2, 0, pair + 1, pair)
            turn(B - 1, 1, B // 2 - 1, B // 2 - 1)

        def first(b):
            return isinstance(b, int) and b == 0

        def last(b):
            return isinstance(b, int) and b == B - 1

        @block.sync
        def _(sp):
            for dst, src in ((ident[:, :], t["ident"]), (causal[:, :], t["causal"]), (causal_b[:, :], t["causal_b"]),
                             (cosw[:, :, 0, :], t["cos"]), (cosw[:, :, 1, :], t["cos"]), (sinw[:, :, 0, :], t["sin"]), (sinw[:, :, 1, :], t["sin"]),
                             (wqkv[:, :], t["attn_w_qkv"]), (wog[:, :], t["attn_w_outgate"])):
                sp.dma_start(dst, src).then_inc(s["consts_in"], 16)
            for n, wn in enumerate((t["attn_qn_w"], t["attn_kn_w"])):
                sp.dma_start(nw[:, n, :], row_bc(wn, 128)).then_inc(s["consts_in"], 16)
                for k in range(2):
                    sp.dma_start(nwx[:, n, 8 * k:8 * k + 8], row_bc(wn[8 - 8 * k:16 - 8 * k], 128)).then_inc(s["consts_in"], 16)
            sp.wait_ge(s["padded"], 2)
            for r in range(4):
                lo = 32 * r
                sp.dma_start(wproj[lo:lo + DH, :, :], t["attn_w_proj"].rearrange("(g r d) k -> r d g k", r=4, d=DH)[r]).then_inc(s["consts_in"], 16)
            for g in range(NHG):
                for r in range(4):
                    at = (4 * g + r) * DH
                    sp.dma_start(memn[32 * r:32 * r + DH, g:g + 1], t["attn_memn_w"][at:at + DH].unsqueeze(1),
                                 allow_slow_non_contiguous=True).then_inc(s["consts_in"], 16)

            def load_lat(b, u):
                sp.dma_start(lat[:, u, :], t["lat_dram"][b, :, :]).then_inc(s_in[u], 16)

            def load_y(b, u):
                for tile in range(2):
                    sp.dma_start(y3[:, u, tile, :], t["y3_dram"][b, TILE_AT[tile]:TILE_AT[tile] + 128, :]).then_inc(y_in[u], 16)

            def store(b):
                sp.wait_ge(s["x2_ready"], b + 1)
                sp.dma_start(t["x2_dram"][b, NPATCH:N, :], x2[:, 0, :]).then_inc(s["x2_stored"], 16)
                sp.dma_start(t["x2_dram"][b, 0:NPATCH, :], x2[0:NPATCH, 1, :]).then_inc(s["x2_stored"], 16)

            for u in range(2):
                load_lat(u, u)
                load_y(u, u)
            with sp.Fori(0, B // 2 - 1) as pair:
                for u in range(2):
                    b = pair * 2 + u
                    sp.wait_ge(s["wl_ps"], 2 * b + 2)
                    load_lat(b + 2, u)
                    store(b)
                    load_y(b + 2, u)
            store(B - 2)
            store(B - 1)
            sp.wait_ge(s["x2_stored"], 32 * B)

        @block.gpsimd
        def _(pool):
            nc.gpsimd.memset(wproj[:, :, :], 0.0).then_inc(s["padded"], 1)
            nc.gpsimd.memset(memn[:, :], 0.0).then_inc(s["padded"], 1)
            nc.gpsimd.memset(ones[:, :], 1.0)
            nc.gpsimd.memset(half[:, :], -0.5).then_inc(s["half_ready"], 1)
            pool.wait_ge(s["half_ready"], 1)
            pool.wait_ge(s["tables_ready"], 1)

            def front(b):
                pool.wait_ge(s["qk_out"], 2 * b + 2)
                pool.wait_ge(s["qm_ready"], b)
                for tile in range(2):
                    for k in range(2):
                        src = qk[:, tile, :].rearrange("p (a h d) -> p a h d", a=2, d=DH)[:, :, :, 8 - 8 * k:16 - 8 * k]
                        dst = qb[:, tile, :].rearrange("p (a h d) -> p a h d", a=2, d=DH)[:, :, :, 8 * k:8 * k + 8]
                        for a in range(2):
                            st = nc.gpsimd.tensor_tensor(dst[:, a, :, :], src[:, a, :, :],
                                                         sinw[:, tile, a, 8 * k:8 * k + 8].unsqueeze(1).to_broadcast([128, HEADS, 8]), ALU.mult)
                st.then_inc(s["qb_ready"], 1)

            def back(b):
                pool.wait_ge(s["mso_ready"], b + 1)
                pool.wait_ge(s["x2_ready"], b)
                nc.gpsimd.tensor_tensor(ro[:, :], oss[:, :], half[:, :], ALU.pow).then_inc(s["ro_ready"], 1)

            def turn(b, u, k, before):
                front(b)
                if not first(b):
                    back(b - 1)
            run(pool, turn)
            back(B - 1)

        @block.vector
        def _(dve):
            ch = Chain(dve, s["chain"])
            for x in (qkf[:, :, :, :], kbd[:, :, :, :], vgb[:, :, :, :, :]):
                nc.vector.memset(x, 0.0).then_inc(s["zeroed"], 1)
            dve.wait_ge(s["consts_in"], CONSTS * 16)
            nc.vector.tensor_tensor(wproj[:, :, :], wproj[:, :, :], memn[:, :].unsqueeze(2).to_broadcast([128, NHG, D]),
                                    ALU.mult).then_inc(s["wproj_ready"], 1)
            for tile in range(2):
                nc.vector.tensor_tensor(cosw[:, tile, :, :], cosw[:, tile, :, :], nw[:, :, :], ALU.mult)
                st = nc.vector.tensor_tensor(sinw[:, tile, :, :], sinw[:, tile, :, :], nwx[:, :, :], ALU.mult)
            st.then_inc(s["tables_ready"], 1)
            dve.wait_ge(s["tables_ready"], 1)
            dve.wait_ge(s["zeroed"], 3)
            LINKS = 11

            def heads(x):
                return x.rearrange("p t (h d) -> p (t h) d", d=DH)

            def by_head(x):
                return x.rearrange("p (h d) -> p h d", d=DH)

            def front1(b, u):
                dve.wait_ge(s["qk_out"], 2 * b + 2)
                for tile in range(2):
                    for a in range(2):
                        st = nc.vector.tensor_tensor(by_head(qa[:, tile, a * D:a * D + D]), by_head(qk[:, tile, a * D:a * D + D]),
                                                     cosw[:, tile, a, :].unsqueeze(1).to_broadcast([128, HEADS, DH]), ALU.mult)
                ch.link(st)
                dve.wait_ge(s["sq_ready"], b + 1)
                dve.wait_ge(s["rt_ready"], b)
                ch.link(nc.vector.tensor_reduce(ms[:, :], heads(sq[:, :, :]), AXX, ALU.add))
                nc.vector.tensor_scalar(ms[:, :], ms[:, :], 1.0 / DH, RMS_EPS, ALU.mult, ALU.add).then_inc(s["ms_ready"], 1)
                dve.wait_ge(s["vo_out"], 2 * b + 2)
                if not (isinstance(b, int) and b < 2):
                    dve.wait_ge(s["ov_ps"], b - 1)
                nc.vector.tensor_tensor(vg[:, u, :, :], by_head(vo[:, 0, 0:D]), vgate[:, b, 0, :].unsqueeze(2).to_broadcast([128, HEADS, DH]), ALU.mult)
                for r in range(4):
                    st = nc.vector.tensor_tensor(vgb[32 * r:32 * r + NPATCH, u, :, r, 0:DH],
                                                 vo[0:NPATCH, 1, 0:D].rearrange("p (g r d) -> p g r d", r=4, d=DH)[:, :, r, :],
                                                 vgate[0:NPATCH, b, 1, r:HEADS:4].unsqueeze(2).to_broadcast([NPATCH, NHG, DH]), ALU.mult)
                st.then_inc(s["vg_ready"], 1)
                dve.wait_ge(s["qb_ready"], b + 1)
                ch.link(nc.vector.tensor_tensor(qa[:, :, :], qa[:, :, :], qb[:, :, :], ALU.add))

            def front2(b):
                dve.wait_ge(s["rt_ready"], b + 1)
                ch.link(nc.vector.reciprocal(rq[:, :], rt[:, :]))
                ch.link(nc.vector.tensor_tensor(heads(qa[:, :, :]), heads(qa[:, :, :]),
                                                rq[:, :].unsqueeze(2).to_broadcast([128, 4 * HEADS, DH]), ALU.mult))
                nc.vector.tensor_scalar(qe[:, :, :], qa[:, :, :], 0.0, None, ALU.min).then_inc(s["qm_ready"], 1)

            def front3(b, u):
                dve.wait_ge(s["qe_ready"], b + 1)
                dve.wait_ge(s["turned"], b)
                nc.vector.scalar_tensor_tensor(qp[:, :, :], qa[:, :, 0:D], 0.0, qe[:, :, 0:D], ALU.max, ALU.add)
                for tile in range(2):
                    st = nc.vector.scalar_tensor_tensor(qkf[:, tile, HEADS:2 * HEADS, 0:DH], by_head(qa[:, tile, D:QK]), 0.0,
                                                        by_head(qe[:, tile, D:QK]), ALU.max, ALU.add)
                ch.link(st)
                dve.wait_ge(s["kc_ps"], b)
                for tile in range(2):
                    st = nc.vector.tensor_tensor(by_head(kr[:, tile, :]), qkf[:, tile, HEADS:2 * HEADS, 0:DH],
                                                 vgate[:, B, tile, :].unsqueeze(2).to_broadcast([128, HEADS, DH]), ALU.mult)
                st.then_inc(s["kr_ready"], 1)
                dve.wait_ge(s["ogt_ready"], b + 1)
                nc.vector.scalar_tensor_tensor(og[:, u, :, :], ogt[:, :, :], 1.0, vo[:, :, D:2 * D], ALU.add, ALU.mult).then_inc(s["og_ready"], 1)

            def front4(b):
                dve.wait_ge(s["kc_ps"], b + 1)
                nc.vector.tensor_tensor(qc[:, :, :], psum[:, 2, 0:2 * D].rearrange("p (t d) -> p t d", t=2), qp[:, :, :],
                                        ALU.mult).then_inc(s["qc_ready"], 1)
                dve.wait_ge(s["qc_ready"], b + 1)
                ch.link(nc.vector.tensor_reduce(den[:, :, :].rearrange("p t h -> p (t h)"), heads(qc[:, :, :]), AXX, ALU.add))

            def front5(b):
                ch.link(nc.vector.tensor_tensor(den[:, :, :], den[:, :, :], decay[:, :, :], ALU.mult))
                ch.link(nc.vector.tensor_scalar(den[:, :, :], den[:, :, :], 1e-5, None, ALU.max))
                ch.link(nc.vector.reciprocal(den[:, :, :], den[:, :, :]))
                ch.link(nc.vector.tensor_tensor(den[:, :, :], den[:, :, :], decay[:, :, :], ALU.mult))
                for tile in range(2):
                    st = nc.vector.tensor_tensor(qkf[:, tile, 0:HEADS, 0:DH], by_head(qp[:, tile, :]),
                                                 den[:, tile, :].unsqueeze(2).to_broadcast([128, HEADS, DH]), ALU.mult)
                st.then_inc(s["qkf_ready"], 1)

            def mask(b, half_):
                dve.wait_ge(s["sc_ps"], 2 * b + half_ + 1)
                dve.wait_ge(s["ov_ps"], b)
                for r in (2 * half_, 2 * half_ + 1):
                    st = nc.vector.tensor_tensor(at_[:, r, :, :], psum[:, 4 + r, 0:NHG * 128].rearrange("p (g n) -> p g n", g=NHG),
                                                 causal[:, :].unsqueeze(1).to_broadcast([128, NHG, 128]), ALU.mult)
                st.then_inc(s["masked"], 1)

            def mask_patches(b):
                dve.wait_ge(s["scp_ps"], b + 1)
                nc.vector.tensor_tensor(ap_[:, :, :], psum[:, 1, 0:NHG * N].rearrange("p (g n) -> p g n", g=NHG),
                                        causal_b[:, :].unsqueeze(1).to_broadcast([128, NHG, N]), ALU.mult).then_inc(s["masked_p"], 1)

            def post1(b):
                dve.wait_ge(s["ss_ps"], b + 1)
                dve.wait_ge(s["ro_ready"], b)
                nc.vector.tensor_scalar(oss[:, :], psum[:, 1, 0:2], 4.0 / D, 4.0 * RMS_EPS, ALU.mult, ALU.add).then_inc(s["mso_ready"], 1)

            def post2(b, u, k):
                dve.wait_ge(s["pr_ps"], b + 1)
                dve.wait_ge(s["ro_ready"], b + 1)
                dve.wait_ge(y_in[u], 32 * k + 32)
                dve.wait_ge(s["x2_stored"], 32 * b)
                dve.wait_ge(s["og_ready"], b + 1)
                for tile in range(2):
                    st = nc.vector.scalar_tensor_tensor(x2[:, tile, :], psum[:, 3, tile * D:tile * D + D], ro[:, tile:tile + 1],
                                                        og[:, u, tile, :], ALU.mult, ALU.mult)
                ch.link(st)
                nc.vector.tensor_tensor(x2[:, :, :], x2[:, :, :], y3[:, u, :, :], ALU.add).then_inc(s["x2_ready"], 1)

            def turn(b, u, k, before):
                if first(b):
                    ch.base, ch.n = 0, 0
                else:
                    ch.base, ch.n = LINKS + (b - 1) * (LINKS + 1), 0
                front1(b, u)
                if not first(b):
                    mask(b - 1, 0)
                front2(b)
                if not first(b):
                    mask(b - 1, 1)
                    mask_patches(b - 1)
                front3(b, u)
                front4(b)
                if not first(b):
                    post1(b - 1)
                front5(b)
                assert ch.n == LINKS, ch.n
                if not first(b):
                    post2(b - 1, 1 - u, before)
            run(dve, turn)
            ch.base, ch.n = LINKS + (B - 1) * (LINKS + 1), 0
            mask(B - 1, 0)
            mask(B - 1, 1)
            mask_patches(B - 1)
            post1(B - 1)
            post2(B - 1, 1, B // 2 - 1)

        @block.scalar
        def _(act):
            act.wait_ge(s["zeroed"], 3)

            def evacuate(b):
                for tile in range(2):
                    act.wait_ge(s["wl_ps"], 2 * b + tile + 1)
                    act.wait_ge(s["qb_ready"], b)
                    act.wait_ge(s["ms_ready"], b)
                    act.wait_ge(s["vg_ready"], b)
                    act.wait_ge(s["og_ready"], b)
                    nc.scalar.mul(qk[:, tile, :], psum[:, 2 * tile, 0:QK], 0.5).then_inc(s["qk_out"], 1)
                    nc.scalar.mul(vo[:, tile, :], psum[:, 2 * tile + 1, 0:2 * D], 0.5).then_inc(s["vo_out"], 1)
                act.wait_ge(s["qk_out"], 2 * b + 2)
                nc.scalar.activation(sq[:, :, :], qk[:, :, :], ACT.Square).then_inc(s["sq_ready"], 1)

            def turned(b):
                act.wait_ge(s["turned"], b + 1)
                act.wait_ge(s["scp_ps"], b)
                nc.scalar.copy(qkT[:, :, :, :], psum[:, 0:3:2, 0:NHG * N].rearrange("p a (g n) -> p a g n", g=NHG)).then_inc(s["qkT_ready"], 1)
                for r in range(4):
                    lo = 32 * r
                    st = nc.scalar.copy(kbd[lo:lo + DH, :, r, 0:NPATCH],
                                        psum[lo:lo + DH, 2, 0:NHG * N].rearrange("p (g n) -> p g n", g=NHG)[:, :, 0:NPATCH])
                st.then_inc(s["kbd_ready"], 1)

            def root(b):
                act.wait_ge(s["ms_ready"], b + 1)
                act.wait_ge(s["qm_ready"], b)
                nc.scalar.activation(rt[:, :], ms[:, :], ACT.Sqrt).then_inc(s["rt_ready"], 1)

            def tanh_exp(b):
                act.wait_ge(s["vo_out"], 2 * b + 2)
                nc.scalar.activation(ogt[:, :, :], vo[:, :, D:2 * D], ACT.Tanh, scale=0.5).then_inc(s["ogt_ready"], 1)
                act.wait_ge(s["qm_ready"], b + 1)
                nc.scalar.activation(qe[:, :, :], qe[:, :, :], ACT.Exp).then_inc(s["qe_ready"], 1)

            def output(b):
                act.wait_ge(s["ov_ps"], b + 1)
                act.wait_ge(s["pr_ps"], b)
                ov = psum[:, 3, 0:NHG * N].rearrange("p (g n) -> p g n", g=NHG)
                nc.scalar.copy(oT[:, :, :], ov).then_inc(s["oT_ready"], 1)
                nc.scalar.activation(osq[:, :, :], ov, ACT.Square).then_inc(s["oT_ready"], 1)

            def turn(b, u, k, before):
                evacuate(b)
                if not first(b):
                    turned(b - 1)
                root(b)
                tanh_exp(b)
                if not first(b):
                    output(b - 1)
            run(act, turn)
            turned(B - 1)
            output(B - 1)

        @block.tensor
        def _(pe):
            pe.wait_ge(s["consts_in"], CONSTS * 16)
            pe.wait_ge(s["wproj_ready"], 1)
            pe.wait_ge(s["half_ready"], 1)

            def project(b, u, k):
                pe.wait_ge(s_in[u], 16 * k + 16)
                if not first(b):
                    pe.wait_ge(s["qk_out"], 2 * b)
                    pe.wait_ge(s["vo_out"], 2 * b)
                    pe.wait_ge(s["mso_ready"], b - 1)
                for tile in range(2):
                    at = TILE_AT[tile]
                    lhs = lat[:, u, at:at + 128]
                    if tile and not first(b):
                        pe.wait_ge(s["qc_ready"], b)
                    nc.tensor.matmul(psum[:, 2 * tile, 0:QK], lhs, wqkv[:, 0:QK], start=True, stop=True)
                    if tile and not first(b):
                        pe.wait_ge(s["x2_ready"], b - 1)
                    nc.tensor.matmul(psum[:, 2 * tile + 1, 0:D], lhs, wqkv[:, QK:3 * D], start=True, stop=True)
                    nc.tensor.matmul(psum[:, 2 * tile + 1, D:2 * D], lhs, wog[:, :], start=True, stop=True).then_inc(s["wl_ps"], 1)

            def turn_qk(b):
                pe.wait_ge(s["qkf_ready"], b + 1)
                pe.wait_ge(s["qk_out"], 2 * B if last(b) else 2 * b + 4)
                for a in range(2):
                    for g in range(NHG):
                        for tile in range(2):
                            rows, at = TILE_ROWS[tile], g * N + TILE_AT[tile]
                            mm = nc.tensor.transpose(psum[:, 2 * a, at:at + rows],
                                                     qkf[0:rows, tile, 12 * a + 4 * g:12 * a + 4 * g + 4, :].rearrange("p h d -> p (h d)"),
                                                     ident[0:rows, 0:rows])
                mm.then_inc(s["turned"], 1)

            def scores(b):
                pe.wait_ge(s["qkT_ready"], b + 1)
                pe.wait_ge(s["masked"], 2 * b)
                for half_ in range(2):
                    for g in range(NHG):
                        for r in (2 * half_, 2 * half_ + 1):
                            lo = 32 * r
                            mm = nc.tensor.matmul(psum[:, 4 + r, 128 * g:128 * g + 128], qkT[lo:lo + DH, 1, g, NPATCH:N],
                                                  qkT[lo:lo + DH, 0, g, NPATCH:N], start=True, stop=True)
                    mm.then_inc(s["sc_ps"], 1)
                pe.wait_ge(s["kbd_ready"], b + 1)
                pe.wait_ge(s["vo_out"], 2 * B if last(b) else 2 * b + 4)
                pe.wait_ge(s["mso_ready"], b)
                for g in range(NHG):
                    mm = nc.tensor.matmul(psum[:, 1, g * N:g * N + N], kbd[:, g, :, :].rearrange("p r m -> p (r m)"),
                                          qkT[:, 0, g, :], start=True, stop=True)
                mm.then_inc(s["scp_ps"], 1)

            def values(b, u):
                pe.wait_ge(s["masked_p"], b + 1)
                pe.wait_ge(s["masked"], 2 * b + 2)
                pe.wait_ge(s["vg_ready"], b + 1)
                pe.wait_ge(s["x2_ready"], b)
                for g in range(NHG):
                    nc.tensor.matmul(psum[:, 3, g * N:g * N + N], vgb[:, u, g, :, :].rearrange("p r d -> p (r d)"), ap_[:, g, :],
                                     start=True, stop=False, skip_group_check=True)
                    for r in range(4):
                        lo = 32 * r
                        mm = nc.tensor.matmul(psum[lo:lo + DH, 3, g * N + NPATCH:g * N + N], vg[:, u, 4 * g + r, :], at_[:, r, g, :],
                                              start=False, stop=True, skip_group_check=True)
                mm.then_inc(s["ov_ps"], 1)

            def sums(b):
                pe.wait_ge(s["kr_ready"], b + 1)
                if not first(b):
                    pe.wait_ge(s["kbd_ready"], b)
                else:
                    pe.wait_ge(s["qk_out"], 2)
                nc.tensor.matmul(psum[:, 2, 0:D], causal[:, :], kr[:, 0, :], start=True, stop=False)
                nc.tensor.matmul(psum[:, 2, 0:D], causal_b[0:NPATCH, NPATCH:N], kr[0:NPATCH, 1, :], start=False, stop=True)
                nc.tensor.matmul(psum[:, 2, D:2 * D], causal_b[0:NPATCH, 0:128], kr[0:NPATCH, 1, :], start=True, stop=True).then_inc(s["kc_ps"], 1)

            def out(b):
                pe.wait_ge(s["oT_ready"], 2 * b + 2)
                for tile in range(2):
                    at = TILE_AT[tile]
                    for g in range(NHG):
                        mm = nc.tensor.matmul(psum[:, 1, tile:tile + 1], osq[:, g, at:at + 128], ones[:, :],
                                              start=(g == 0), stop=(g == NHG - 1))
                mm.then_inc(s["ss_ps"], 1)
                for tile in range(2):
                    at = TILE_AT[tile]
                    for g in range(NHG):
                        mm = nc.tensor.matmul(psum[:, 3, tile * D:tile * D + D], oT[:, g, at:at + 128], wproj[:, g, :],
                                              start=(g == 0), stop=(g == NHG - 1))
                mm.then_inc(s["pr_ps"], 1)

            def turn(b, u, k, before):
                project(b, u, k)
                if not first(b):
                    turn_qk(b - 1)
                    scores(b - 1)
                    values(b - 1, 1 - u)
                sums(b)
                if not first(b):
                    out(b - 1)
            run(pe, turn)
            turn_qk(B - 1)
            scores(B - 1)
            values(B - 1, 1)
            out(B - 1)


def gated_ffn(nc, t, psum):
    TURNS = B // 2
    HID = 512
    HJ = HID // 128
    with ExitStack() as ctx:
        def sb(name, shape, dt=FP32):
            return ctx.enter_context(nc.sbuf_tensor("ffn_" + name, shape, dt))

        ident = sb("ident", [128, 128])
        half = sb("half", [128, 4])
        nwt = sb("nwt", [DC, 2])
        w1 = sb("w1", [DC, 2, HID])
        w2 = sb("w2", [DC, 2, HID])
        w3 = sb("w3", [128, HJ, D])
        x2 = sb("x2", [128, 2, 4, D])
        h2 = sb("h2", [128, 2, 4, D])
        xsq = sb("xsq", [128, D])
        ss = sb("ss", [128, 4])
        r = sb("r", [128, 4])
        xr = sb("xr", [128, 4, D])
        xrT = sb("xrT", [DC, 2, 2, N])
        gth = sb("gth", [128, HJ, 2 * N])
        hid = sb("hid", [128, HJ, 2 * N])
        h3 = sb("h3", [128, 4, D])
        s = phase_sems(ctx, nc, "ffn", "consts_in half_ready w_ready in0 in1 ss_ready mss r_ready xr_ready xrT_ps xrT_ready g_ps gth_ready g2_ready "
                 "hid_ready o_ps sum_ready h3_ready h3_stored chain")
        block = ctx.enter_context(nc.Block())
        s_in = (s["in0"], s["in1"])

        def run(eng, turn):
            turn(0, 0, 0)
            with eng.Fori(0, TURNS // 2 - 1) as pair:
                turn(pair * 2 + 1, 1, pair)
                turn(pair * 2 + 2, 0, pair + 1)
            turn(TURNS - 1, 1, TURNS // 2 - 1)

        @block.sync
        def _(sp):
            for dst, src in ((ident[:, :], t["ident"]), (w1[:, :, :], t["attn_w1"].rearrange("(c p) k -> p c k", p=DC)),
                             (w2[:, :, :], t["attn_w2"].rearrange("(c p) k -> p c k", p=DC)),
                             (w3[:, :, :], t["attn_w3"].rearrange("(j p) k -> p j k", p=128))):
                sp.dma_start(dst, src).then_inc(s["consts_in"], 16)
            sp.dma_start(nwt[:, :], t["attn_ffn_ln_w"].rearrange("(c p) -> p c", p=DC), allow_slow_non_contiguous=True).then_inc(s["consts_in"], 16)

            def load(i, u):
                for j in range(4):
                    at = TILE_AT[j % 2]
                    sp.dma_start(x2[:, u, j, :], t["x2_dram"][2 * i + j // 2, at:at + 128, :]).then_inc(s_in[u], 16)
                    sp.dma_start(h2[:, u, j, :], t["h2_dram"][2 * i + j // 2, at:at + 128, :]).then_inc(s_in[u], 16)

            def store(i):
                sp.wait_ge(s["h3_ready"], i + 1)
                for b in range(2):
                    sp.dma_start(t["h3_dram"][2 * i + b, NPATCH:N, :], h3[:, 2 * b, :]).then_inc(s["h3_stored"], 16)
                    sp.dma_start(t["h3_dram"][2 * i + b, 0:NPATCH, :], h3[0:NPATCH, 2 * b + 1, :]).then_inc(s["h3_stored"], 16)

            load(0, 0)
            load(1, 1)
            with sp.Fori(0, TURNS // 2 - 1) as pair:
                for u in range(2):
                    store(pair * 2 + u)
                    load(pair * 2 + u + 2, u)
            store(TURNS - 2)
            store(TURNS - 1)
            sp.wait_ge(s["h3_stored"], 64 * TURNS)

        @block.gpsimd
        def _(pool):
            nc.gpsimd.memset(half[:, :], -0.5).then_inc(s["half_ready"], 1)
            pool.wait_ge(s["half_ready"], 1)

            def turn(i, u, k):
                pool.wait_ge(s["mss"], i + 1)
                pool.wait_ge(s["xr_ready"], i)
                nc.gpsimd.tensor_tensor(r[:, :], ss[:, :], half[:, :], ALU.pow).then_inc(s["r_ready"], 1)
            run(pool, turn)

        @block.vector
        def _(dve):
            dve.wait_ge(s["consts_in"], 5 * 16)
            for w in (w1, w2):
                nc.vector.tensor_tensor(w[:, :, :], w[:, :, :], nwt[:, :].unsqueeze(2).to_broadcast([DC, 2, HID]),
                                        ALU.mult).then_inc(s["w_ready"], 1)

            def front(i, u, k):
                dve.wait_ge(s["ss_ready"], 4 * i + 4)
                nc.vector.tensor_scalar(ss[:, :], ss[:, :], 1.0 / D, RMS_EPS, ALU.mult, ALU.add).then_inc(s["mss"], 1)
                dve.wait_ge(s_in[u], 128 * k + 128)
                dve.wait_ge(s["r_ready"], i + 1)
                dve.wait_ge(s["xrT_ps"], i)
                for j in range(4):
                    st = nc.vector.tensor_scalar(xr[:, j, :], x2[:, u, j, :], r[:, j:j + 1], None, ALU.mult)
                st.then_inc(s["xr_ready"], 1)

            def middle(i, u):
                for j in range(HJ):
                    dve.wait_ge(s["gth_ready"], HJ * i + j + 1)
                    nc.vector.scalar_tensor_tensor(gth[:, j, :], gth[:, j, :], 1.0, psum[:, 2 * j, 0:2 * N], ALU.add, ALU.mult).then_inc(s["g2_ready"], 1)
                    dve.wait_ge(s["g2_ready"], HJ * i + j + 1)
                    dve.wait_ge(s["o_ps"], 2 * i)
                    nc.vector.scalar_tensor_tensor(hid[:, j, :], gth[:, j, :], 0.5, psum[:, 2 * j + 1, 0:2 * N], ALU.mult, ALU.mult).then_inc(s["hid_ready"], 1)

            def last(i, u):
                dve.wait_ge(s["h3_stored"], 64 * i)
                dve.wait_ge(s["h3_ready"], i)
                nc.vector.tensor_tensor(h3[:, :, :], x2[:, u, :, :], h2[:, u, :, :], ALU.add).then_inc(s["sum_ready"], 1)
                dve.wait_ge(s["sum_ready"], i + 1)
                for b in range(2):
                    dve.wait_ge(s["o_ps"], 2 * i + b + 1)
                    st = nc.vector.tensor_tensor(h3[:, 2 * b:2 * b + 2, :], h3[:, 2 * b:2 * b + 2, :],
                                                 psum[:, b, 0:2 * D].rearrange("p (a d) -> p a d", a=2), ALU.add)
                st.then_inc(s["h3_ready"], 1)

            def turn(i, u, k):
                if isinstance(i, int) and i == 0:
                    front(0, 0, 0)
                else:
                    middle(i - 1, 1 - u)
                    front(i, u, k)
                    last(i - 1, 1 - u)
            run(dve, turn)
            middle(TURNS - 1, 1)
            last(TURNS - 1, 1)

        @block.scalar
        def _(act):
            def front(i, u, k):
                act.wait_ge(s_in[u], 128 * k + 128)
                act.wait_ge(s["r_ready"], i)
                for j in range(4):
                    act.wait_ge(s["ss_ready"], 4 * i + j)
                    nc.scalar.activation(xsq[:, :], x2[:, u, j, :], ACT.Square, accum_out=ss[:, j:j + 1]).then_inc(s["ss_ready"], 1)

            def copy(i):
                act.wait_ge(s["xrT_ps"], i + 1)
                act.wait_ge(s["g_ps"], 2 * HJ * i)
                nc.scalar.copy(xrT[:, :, :, :], psum[0:DC, 2:4, 0:2 * N].rearrange("p c (b n) -> p c b n", b=2)).then_inc(s["xrT_ready"], 1)

            def tanh(i):
                for j in range(HJ):
                    act.wait_ge(s["g_ps"], 2 * HJ * i + 2 * j + 2)
                    act.wait_ge(s["hid_ready"], HJ * i)
                    nc.scalar.activation(gth[:, j, :], psum[:, 2 * j, 0:2 * N], ACT.Tanh, scale=0.5).then_inc(s["gth_ready"], 1)

            def turn(i, u, k):
                front(i, u, k)
                if not (isinstance(i, int) and i == 0):
                    tanh(i - 1)
                copy(i)
            run(act, turn)
            tanh(TURNS - 1)

        @block.tensor
        def _(pe):
            pe.wait_ge(s["consts_in"], 5 * 16)
            pe.wait_ge(s["w_ready"], 2)

            def turned(i):
                pe.wait_ge(s["xr_ready"], i + 1)
                pe.wait_ge(s["hid_ready"], HJ * i)
                for c in range(2):
                    for j in range(4):
                        rows, at = TILE_ROWS[j % 2], (j // 2) * N + TILE_AT[j % 2]
                        mm = nc.tensor.transpose(psum[0:DC, 2 + c, at:at + rows], xr[0:rows, j, c * DC:c * DC + DC], ident[0:rows, 0:rows])
                mm.then_inc(s["xrT_ps"], 1)

            def hidden(i):
                pe.wait_ge(s["xrT_ready"], i + 1)
                pe.wait_ge(s["h3_ready"], i)
                for j in range(HJ):
                    for n, w in enumerate((w1, w2)):
                        for c in range(2):
                            mm = nc.tensor.matmul(psum[:, 2 * j + n, 0:2 * N], w[:, c, 128 * j:128 * j + 128],
                                                  xrT[:, c, :, :], start=(c == 0), stop=(c == 1))
                        mm.then_inc(s["g_ps"], 1)

            def output(i):
                pe.wait_ge(s["hid_ready"], HJ * i + HJ)
                for b in range(2):
                    for a in range(2):
                        at = b * N + TILE_AT[a]
                        for j in range(HJ):
                            mm = nc.tensor.matmul(psum[:, b, a * D:a * D + D], hid[:, j, at:at + 128], w3[:, j, :],
                                                  start=(j == 0), stop=(j == HJ - 1))
                    mm.then_inc(s["o_ps"], 1)

            turned(0)

            def turn(i, u, k):
                hidden(i)
                turned(i + 1)
                output(i)
            with pe.Fori(0, TURNS - 1) as i:
                turn(i, 0, 0)
            hidden(TURNS - 1)
            output(TURNS - 1)


def temporal_layer(nc, t, psum):
    with ExitStack() as ctx:
        def sb(name, shape):
            return ctx.enter_context(nc.sbuf_tensor("l1_" + name, shape, FP32))

        vgate = sb("vgate", [128, B + 1, 2, HEADS])
        decay = sb("decay", [128, 2, HEADS])
        with nc.sbuf_tensor("l1_th", [128, B, 2, 4 * HEADS], FP32) as th:
            combine(nc, t, psum, th)
            gates(nc, t, psum, th, vgate, decay)
        decay_attention(nc, t, psum, vgate, decay)
        gated_ffn(nc, t, psum)


def routed_mixture(nc, t, psum):
    TM = 102
    NT = B * N // TM
    PER = 4
    BLOCKS = NT // PER
    BT = PER * TM
    FJ = F1 // 128
    NE = E1 + 1
    ORDER = [E1] + list(range(E1))
    with ExitStack() as ctx:
        def sb(name, shape, dt=FP32):
            return ctx.enter_context(nc.sbuf_tensor("moe_" + name, shape, dt))

        ident = sb("ident", [128, 128])
        half = sb("half", [128, NT])
        before = sb("before", [128, E1, E1])
        ebias = sb("ebias", [128, E1])
        wr = sb("wr", [E1, D])
        wrT = sb("wrT", [DC, 2, E1])
        stage_gu = sb("stage_gu", [128, 2, 2, FJ, D])
        stage_d = sb("stage_d", [DC, 2, 2, F1])
        wguT = sb("wguT", [DC, NE, 2, 2, F1])
        wdT = sb("wdT", [128, NE, FJ, D])
        h3 = sb("h3", [TM, NT, D])
        y = sb("y", [TM, NT, D])
        stats = sb("stats", [TM, NT, 6])
        mv = sb("mv", [TM, NT, 2])
        rstd = sb("rstd", [TM, NT])
        yT = sb("yT", [DC, 2, B * N])
        lg = sb("lg", [TM, NT, E1])
        sel = sb("sel", [TM, NT, E1])
        v1 = sb("v1", [TM, NT])
        cmp = sb("cmp", [TM, NT, E1, E1])
        eq = sb("eq", [TM, NT, E1, E1])
        comb = sb("comb", [TM, NT, E1])
        cb = sb("cb", [TM, PER, E1])
        sg = sb("sg", [128, FJ, BT])
        hT = sb("hT", [128, 2, FJ, BT])
        acc = sb("acc", [TM, PER, D])
        s = phase_sems(ctx, nc, "moe", "consts_in h_in half_ready w_in0 w_in1 wt_ps wt_out stats_done mv_ready rstd_ready y_ready yT_ps yT_out wrT_ps wrT_out "
                 "lg_ps lg_ready lg_exp comb_ready cb_ready g_ps sg_ready h_ready o_ps o_used0 o_used1 acc_ready out_stored chain passed")
        block = ctx.enter_context(nc.Block())
        w_in, o_used = (s["w_in0"], s["w_in1"]), (s["o_used0"], s["o_used1"])
        out_v = t["out"].rearrange("b n d -> (b n) d").rearrange("(k p) d -> p k d", p=TM)
        h3_v = t["h3_dram"].rearrange("b n d -> (b n) d").rearrange("(k p) d -> p k d", p=TM)

        def experts(eng, turn):
            with eng.Fori(0, E1 // 2) as pair:
                turn(pair * 2, 0, pair)
                turn(pair * 2 + 1, 1, pair)
            turn(E1, 0, E1 // 2)

        @block.sync
        def _(sp):
            for dst, src in ((ident[:, :], t["ident"]), (before[:, :, :], t["before"].unsqueeze(0).to_broadcast([128, E1, E1])),
                             (ebias[:, :], row_bc(t["ffn_expert_bias"], 128)), (wr[:, :], t["ffn_w_router"])):
                sp.dma_start(dst, src).then_inc(s["consts_in"], 16)
            sp.dma_start(h3[:, :, :], h3_v).then_inc(s["h_in"], 16)

            def load(e, u, gate, up, down):
                sp.dma_start(stage_gu[:, u, 0, :, :], gate.rearrange("(j p) d -> p j d", p=128)).then_inc(w_in[u], 16)
                sp.dma_start(stage_gu[:, u, 1, :, :], up.rearrange("(j p) d -> p j d", p=128)).then_inc(w_in[u], 16)
                sp.dma_start(stage_d[:, u, :, :], down.rearrange("(c p) f -> p c f", p=DC)).then_inc(w_in[u], 16)

            def turn(e, u, k):
                if isinstance(e, int):
                    sp.wait_ge(s["wt_ps"], 3 * (e - 1))
                    load(e, u, t["ffn_sg"], t["ffn_su"], t["ffn_sd"])
                else:
                    sp.wait_ge(s["wt_ps"], 6 * k)
                    load(e, u, t["ffn_Wg"][e, :, :], t["ffn_Wu"][e, :, :], t["ffn_Wd"][e, :, :])
            experts(sp, turn)
            with sp.Fori(0, BLOCKS) as k:
                sp.wait_ge(s["acc_ready"], k + 1)
                sp.dma_start(out_v[:, bass.ds(k * PER, PER), :], acc[:, :, :]).then_inc(s["out_stored"], 16)
            sp.wait_ge(s["out_stored"], 16 * BLOCKS)

        @block.gpsimd
        def _(pool):
            nc.gpsimd.memset(half[:, :], -0.5).then_inc(s["half_ready"], 1)
            pool.wait_ge(s["half_ready"], 1)
            pool.wait_ge(s["mv_ready"], 1)
            nc.gpsimd.tensor_tensor(rstd[:, :], mv[:, :, 1], half[0:TM, :], ALU.pow).then_inc(s["rstd_ready"], 1)

        @block.vector
        def _(dve):
            ch = Chain(dve, s["chain"])
            dve.wait_ge(s["h_in"], 16)
            for k in range(NT):
                st = nc.vector.bn_stats(stats[:, k, :], h3[:, k, :])
            ch.link(st)
            for k in range(NT):
                st = nc.vector.bn_aggr(mv[:, k, :], stats[:, k, :])
            ch.link(st)
            nc.vector.tensor_scalar(mv[:, :, 1], mv[:, :, 1], LN_EPS, None, ALU.add).then_inc(s["mv_ready"], 1)
            dve.wait_ge(s["rstd_ready"], 1)
            for k in range(NT):
                nc.vector.tensor_scalar(y[:, k, :], h3[:, k, :], mv[:, k, 0:1], rstd[:, k:k + 1],
                                        ALU.subtract, ALU.mult).then_inc(s["y_ready"], 1)
            dve.wait_ge(s["consts_in"], 64)
            dve.wait_ge(s["lg_ps"], 1)
            lps = psum[0:TM, 0, 0:NT * E1].rearrange("p (k e) -> p k e", e=E1)

            def over_experts(x):
                return x.unsqueeze(2).to_broadcast([TM, NT, E1])

            ch.link(nc.vector.tensor_reduce(v1[:, :], lps, AXX, ALU.max))
            nc.vector.tensor_tensor(lg[:, :, :], lps, over_experts(v1[:, :]), ALU.subtract).then_inc(s["lg_ready"], 1)
            dve.wait_ge(s["lg_exp"], 1)
            ch.link(nc.vector.tensor_reduce(v1[:, :], lg[:, :, :], AXX, ALU.add))
            ch.link(nc.vector.reciprocal(v1[:, :], v1[:, :]))
            ch.link(nc.vector.tensor_tensor(lg[:, :, :], lg[:, :, :], over_experts(v1[:, :]), ALU.mult))
            ch.link(nc.vector.tensor_tensor(sel[:, :, :], lg[:, :, :], ebias[0:TM, :].unsqueeze(1).to_broadcast([TM, NT, E1]), ALU.add))
            for k in range(NT):
                mine = sel[:, k, :].unsqueeze(2).to_broadcast([TM, E1, E1])
                other = sel[:, k, :].unsqueeze(1).to_broadcast([TM, E1, E1])
                nc.vector.tensor_tensor(cmp[:, k, :, :], other, mine, ALU.is_gt)
                st = nc.vector.tensor_tensor(eq[:, k, :, :], other, mine, ALU.is_equal)
            ch.link(st)
            ch.link(nc.vector.tensor_tensor(eq[:, :, :, :].rearrange("p k a b -> p k (a b)"), eq[:, :, :, :].rearrange("p k a b -> p k (a b)"),
                                            before[0:TM, :, :].rearrange("p a b -> p (a b)").unsqueeze(1).to_broadcast([TM, NT, E1 * E1]), ALU.mult))
            ch.link(nc.vector.tensor_tensor(cmp[:, :, :, :], cmp[:, :, :, :], eq[:, :, :, :], ALU.add))
            ch.link(nc.vector.tensor_reduce(sel[:, :, :].rearrange("p k e -> p (k e)"), cmp[:, :, :, :].rearrange("p k a b -> p (k a) b"), AXX, ALU.add))
            ch.link(nc.vector.tensor_scalar(sel[:, :, :], sel[:, :, :], 2.0, None, ALU.is_lt))
            ch.link(nc.vector.tensor_tensor(comb[:, :, :], sel[:, :, :], lg[:, :, :], ALU.mult))
            ch.link(nc.vector.tensor_reduce(v1[:, :], comb[:, :, :], AXX, ALU.add))
            ch.link(nc.vector.tensor_scalar(v1[:, :], v1[:, :], 1e-9, None, ALU.add))
            ch.link(nc.vector.reciprocal(v1[:, :], v1[:, :]))
            nc.vector.tensor_tensor(comb[:, :, :], comb[:, :, :], over_experts(v1[:, :]), ALU.mult).then_inc(s["comb_ready"], 1)
            dve.wait_ge(s["comb_ready"], 1)
            SETUP = ch.n
            ADDS = 2 * NE

            def hidden(k, n):
                for j in range(FJ):
                    dve.wait_ge(s["sg_ready"], (k * NE + n) * FJ + j + 1)
                    if n >= 2:
                        dve.wait_ge(s["o_ps"], (k * NE + n - 2) * 2 + 2)
                    else:
                        dve.wait_ge(s["o_ps"], k * NE * 2)
                    nc.vector.tensor_tensor(hT[:, n % 2, j, :], sg[:, j, :], psum[:, 2 * j + 1, 0:BT], ALU.mult).then_inc(s["h_ready"], 1)

            def add(k, n):
                for m in range(2):
                    dve.wait_ge(s["o_ps"], (k * NE + n) * 2 + m + 1)
                    part = psum[0:TM, 6 + m, 0:2 * D].rearrange("p (a d) -> p a d", a=2)
                    if n == 0:
                        nc.vector.tensor_tensor(acc[:, 2 * m:2 * m + 2, :], part, h3[:, bass.ds(k * PER + 2 * m, 2), :],
                                                ALU.add).then_inc(o_used[m], 1)
                    else:
                        dve.wait_ge(o_used[m], k * NE + n)
                        for a in range(2):
                            st = nc.vector.scalar_tensor_tensor(acc[:, 2 * m + a, :], part[:, a, :], cb[:, 2 * m + a, ORDER[n]:ORDER[n] + 1],
                                                                acc[:, 2 * m + a, :], ALU.mult, ALU.add)
                        st.then_inc(o_used[m], 1)

            with dve.Fori(0, BLOCKS) as k:
                nc.vector.tensor_copy(cb[:, :, :], comb[:, bass.ds(k * PER, PER), :]).then_inc(s["cb_ready"], 1)
                dve.wait_ge(s["cb_ready"], k + 1)
                dve.wait_ge(s["out_stored"], 16 * k)
                for n in range(NE):
                    hidden(k, n)
                    if n:
                        add(k, n - 1)
                add(k, NE - 1)
                for m in range(2):
                    dve.wait_ge(o_used[m], k * NE + NE)
                nc.vector.tensor_copy(acc[:, 0, 0:2], acc[:, 0, 0:2]).then_inc(s["acc_ready"], 1)

        @block.scalar
        def _(act):
            act.wait_ge(s["wrT_ps"], 1)
            nc.scalar.copy(wrT[:, :, :], psum[0:DC, 6, 0:2 * E1].rearrange("p (c e) -> p c e", c=2)).then_inc(s["wrT_out"], 1)

            def turn(e, u, k):
                for n in range(2):
                    act.wait_ge(s["wt_ps"], 3 * e + n + 1)
                    nc.scalar.copy(wguT[:, e, n, :, :], psum[0:DC, 2 * n:2 * n + 2, 0:F1]).then_inc(s["wt_out"], 1)
                act.wait_ge(s["wt_ps"], 3 * e + 3)
                nc.scalar.copy(wdT[:, e, 0:2, :], psum[:, 4, 0:2 * D].rearrange("p (j d) -> p j d", j=2)).then_inc(s["wt_out"], 1)
                nc.scalar.copy(wdT[:, e, 2, :], psum[:, 5, 0:D]).then_inc(s["wt_out"], 1)
            experts(act, turn)
            for k in range(BLOCKS):
                act.wait_ge(s["yT_ps"], k + 1)
                b0 = 2 * (k % 2)
                nc.scalar.copy(yT[:, :, k * BT:k * BT + BT], psum[0:DC, b0:b0 + 2, 0:BT]).then_inc(s["yT_out"], 1)
            act.wait_ge(s["lg_ready"], 1)
            nc.scalar.activation(lg[:, :, :], lg[:, :, :], ACT.Exp).then_inc(s["lg_exp"], 1)
            with act.Fori(0, BLOCKS) as k:
                for n in range(NE):
                    for j in range(FJ):
                        act.wait_ge(s["g_ps"], (k * NE + n) * FJ + j + 1)
                        if n == 0:
                            act.wait_ge(s["h_ready"], k * NE * FJ)
                        else:
                            act.wait_ge(s["h_ready"], (k * NE + n - 1) * FJ + j + 1)
                        nc.scalar.activation(sg[:, j, :], psum[:, 2 * j, 0:BT], ACT.Silu).then_inc(s["sg_ready"], 1)

        @block.tensor
        def _(pe):
            pe.wait_ge(s["consts_in"], 64)
            for c in range(2):
                mm = nc.tensor.transpose(psum[0:DC, 6, c * E1:c * E1 + E1], wr[:, c * DC:c * DC + DC], ident[0:E1, 0:E1])
            mm.then_inc(s["wrT_ps"], 1)

            def turn(e, u, k):
                pe.wait_ge(w_in[u], 48 * k + 48)
                pe.wait_ge(s["wt_out"], 4 * e)
                for n in range(2):
                    for c in range(2):
                        for j in range(FJ):
                            mm = nc.tensor.transpose(psum[0:DC, 2 * n + c, 128 * j:128 * j + 128],
                                                     stage_gu[:, u, n, j, c * DC:c * DC + DC], ident[:, :])
                    mm.then_inc(s["wt_ps"], 1)
                for j in range(FJ):
                    for c in range(2):
                        at = (j % 2) * D + c * DC
                        mm = nc.tensor.transpose(psum[:, 4 + j // 2, at:at + DC], stage_d[:, u, c, 128 * j:128 * j + 128],
                                                 ident[0:DC, 0:DC])
                mm.then_inc(s["wt_ps"], 1)
            experts(pe, turn)
            pe.wait_ge(s["wt_out"], 4 * NE)
            for k in range(BLOCKS):
                pe.wait_ge(s["y_ready"], PER * k + PER)
                if k >= 2:
                    pe.wait_ge(s["yT_out"], k - 1)
                for c in range(2):
                    for a in range(PER):
                        mm = nc.tensor.transpose(psum[0:DC, 2 * (k % 2) + c, a * TM:a * TM + TM],
                                                 y[:, PER * k + a, c * DC:c * DC + DC], ident[0:TM, 0:TM])
                mm.then_inc(s["yT_ps"], 1)
            pe.wait_ge(s["yT_out"], BLOCKS)
            pe.wait_ge(s["wrT_out"], 1)
            for k in range(NT):
                for c in range(2):
                    mm = nc.tensor.matmul(psum[0:TM, 0, k * E1:k * E1 + E1], yT[:, c, k * TM:k * TM + TM], wrT[:, c, :],
                                          start=(c == 0), stop=(c == 1))
            mm.then_inc(s["lg_ps"], 1)
            pe.wait_ge(s["lg_ready"], 1)

            def hidden(k, n):
                for j in range(FJ):
                    if n == 0:
                        pe.wait_ge(s["h_ready"], k * NE * FJ)
                    else:
                        pe.wait_ge(s["h_ready"], (k * NE + n - 1) * FJ + j + 1)
                    for a in range(2):
                        for c in range(2):
                            mm = nc.tensor.matmul(psum[:, 2 * j + a, 0:BT], wguT[:, ORDER[n], a, c, 128 * j:128 * j + 128],
                                                  yT[:, c, bass.ds(k * BT, BT)], start=(c == 0), stop=(c == 1))
                    mm.then_inc(s["g_ps"], 1)

            def output(k, n):
                pe.wait_ge(s["h_ready"], (k * NE + n) * FJ + FJ)
                for m in range(2):
                    pe.wait_ge(o_used[m], k * NE + n)
                    for a in range(2):
                        at = (2 * m + a) * TM
                        for j in range(FJ):
                            mm = nc.tensor.matmul(psum[0:TM, 6 + m, a * D:a * D + D], hT[:, n % 2, j, at:at + TM],
                                                  wdT[:, ORDER[n], j, :], start=(j == 0), stop=(j == FJ - 1))
                    mm.then_inc(s["o_ps"], 1)

            with pe.Fori(0, BLOCKS) as k:
                for n in range(NE):
                    hidden(k, n)
                    if n:
                        output(k, n - 1)
                output(k, NE - 1)


def build(nc, ins, outs, consts, scratch):
    t = {"x": ins["x"], "txt": ins["txt"], "tok_W": ins["L0_tok_W"], "tok_b": ins["L0_tok_b"],
         "tok_alpha_w": ins["L0_tok_alpha_w"], "tok_alpha_a": ins["L0_tok_alpha_a"], "attn_W": ins["L0_attn_W"],
         "attn_params": [ins["L0_attn_" + n] for n in ("b", "bn_gamma", "bn_beta", "bn_mean", "bn_var")],
         "out": outs[0], **consts, **scratch}
    t.update({n.split("_", 1)[1]: a for n, a in ins.items() if n.startswith(("L0_ffn", "L1_"))})
    with nc.psum_tensor("banks", [128, 8, 512], FP32) as psum:
        for phase in (patches, spiking_attention, soft_mixture, temporal_layer, routed_mixture):
            phase(nc, t, psum)


_SCRATCH = {"h_dram": (B, N, D), "h1_dram": (B, N, D), "xn_dram": (B, N, D), "xnT_dram": (B, 2, DC, N),
            "cwT_dram": (B, NG, 128, N), "eo_dram": (B, SLOTS, D), "h2_dram": (B, N, D), "y3_dram": (B, N, D),
            "lat_dram": (B, 128, N), "x2_dram": (B, N, D), "h3_dram": (B, N, D)}


def _constants():
    import numpy as np
    f32 = np.float32
    token = np.stack([np.arange(128) + NPATCH, np.arange(128)], 1)
    freq = (f32(1.0) / f32(10000.0) ** (np.arange(0, DH, 2, dtype=f32) / f32(DH))).astype(f32)
    angle = token[:, :, None].astype(f32) * np.concatenate([freq, freq])
    sign = np.concatenate([-np.ones(DH // 2), np.ones(DH // 2)])
    tokens = np.arange(N)
    return {"ident": np.eye(128, dtype=f32),
            "heads_mask": np.kron(np.eye(DC // DH), np.ones((DH, DH))).astype(f32),
            "cos": np.cos(angle).astype(f32), "sin": (np.sin(angle) * sign).astype(f32),
            "pos": (token + 1).astype(f32),
            "causal": np.triu(np.ones((128, 128), f32)),
            "causal_b": ((tokens[:128, None] % 32 < NPATCH) & (tokens[:128, None] % 32 <= tokens[None, :])).astype(f32),
            "before": np.tril(np.ones((E1, E1), f32), -1)}


def kernel(**inputs):
    import numpy as _np
    import concourse.bacc as _bacc
    from concourse import mybir as _mybir
    from concourse.bass_utils import run_bass_kernel_spmd as _run

    nc = _bacc.Bacc("TRN2", target_bir_lowering=False, num_devices=1)
    arrays, ins, consts, scratch = {}, {}, {}, {}
    for name, value in inputs.items():
        a = _np.ascontiguousarray(value)
        if a.ndim == 0:
            a = a.reshape(1)
        arrays[f"in_{name}_dram"] = a
        ins[name] = nc.dram_tensor(f"in_{name}_dram", a.shape, _mybir.dt.from_np(a.dtype), kind="ExternalInput").ap()
    for name, a in _constants().items():
        arrays[f"const_{name}_dram"] = a
        consts[name] = nc.dram_tensor(f"const_{name}_dram", a.shape, _mybir.dt.from_np(a.dtype), kind="ExternalInput").ap()
    for name, shape in _SCRATCH.items():
        scratch[name] = nc.dram_tensor(name, shape, _mybir.dt.float32, kind="Internal").ap()
    outs = [nc.dram_tensor("out_0_dram", (B, N, D), _mybir.dt.float32, kind="ExternalOutput").ap()]
    build(nc, ins, outs, consts, scratch)
    r = _run(nc, [arrays], core_ids=[0])
    return r.results[0]["out_0_dram"]
```

```python
import concourse.bass as bass
from concourse import mybir
from contextlib import ExitStack

FP32 = mybir.dt.float32
F32R = mybir.dt.float32r
BF16 = mybir.dt.bfloat16
ALU = mybir.AluOpType
ACT = mybir.ActivationFunctionType
AXX = mybir.AxisListType.X

B = 16
D = 192
DC = 96
NPATCH = 25
NTXT = 128
N = NPATCH + NTXT
PATCH = 16
KPATCH = 3 * PATCH * PATCH
LN_EPS = 1e-5
RMS_EPS = 1e-6
E0, S0, H0 = 32, 32, 768
SLOTS = E0 * S0
NG = SLOTS // 128
HEADS, DH = 12, 16
E1, F1 = 8, 384
ROUND = 1.5 * 2.0 ** 23

TILE_AT = (NPATCH, 0)
TILE_ROWS = (NTXT, NPATCH)


class Chain:

    def __init__(self, eng, sem, passed=None):
        self.eng, self.sem, self.base, self.n, self.passed = eng, sem, 0, 0, passed

    def link(self, ins, apart=False):
        self.n += 1
        ins.then_inc(self.sem, 1)
        self.eng.wait_ge(self.sem, self.base + self.n)
        if apart:
            self.eng.sem_inc(self.passed, 1)


def phase_sems(ctx, nc, phase, names):
    sems = {name: nc.alloc_semaphore(name=f"{phase}_{name}") for name in names.split()}

    def clear():
        nc.clear_and_free_semaphores(list(sems.values()))
        nc.all_engine_barrier()
    ctx.callback(clear)
    return sems


def row_bc(ap, parts):
    return ap.unsqueeze(0).to_broadcast([parts] + list(ap.shape))


def patches(nc, t, psum):
    KC = KPATCH // 128
    with ExitStack() as ctx:
        def sb(name, shape, dt=FP32):
            return ctx.enter_context(nc.sbuf_tensor("tok_" + name, shape, dt))

        img = sb("img", [B * 5, 3, PATCH, 80])
        imgq = sb("imgq", [B * 5, 5, 3 * PATCH, PATCH], BF16)
        w = sb("w", [DC, 2, KPATCH])
        wq = sb("wq", [DC, 2, KPATCH], BF16)
        alpha = sb("alpha", [128, 2])
        ralpha = sb("ralpha", [128, 2])
        yscale = sb("yscale", [128, 1])
        bias = sb("bias", [128, D])
        ident = sb("ident", [128, 128])
        identb = sb("identb", [128, 128], BF16)
        imgT = sb("imgT", [128, KC, B, 5, 5], BF16)
        wT = sb("wT", [128, KC, D], BF16)
        emb = sb("emb", [100, 4, D])
        s = phase_sems(ctx, nc, "tok", "consts_in img_in txt_copied img_q w_q identb_ready turned evacuated "
                 "product scaled stored chain")
        block = ctx.enter_context(nc.Block())
        turn_ps = [psum[:, k, :].bitcast(BF16) for k in range(2)]

        @block.sync
        def _(sp):
            sp.dma_start(ident[:, :], t["ident"]).then_inc(s["consts_in"], 16)
            sp.dma_start(w[:, :, :], t["tok_W"].rearrange("(c o) i a b -> o c (i a b)", o=DC)).then_inc(s["consts_in"], 16)
            sp.dma_start(alpha[:, 0:1], row_bc(t["tok_alpha_a"], 128)).then_inc(s["consts_in"], 16)
            sp.dma_start(alpha[:, 1:2], row_bc(t["tok_alpha_w"], 128)).then_inc(s["consts_in"], 16)
            sp.dma_start(bias[:, :], row_bc(t["tok_b"], 128)).then_inc(s["consts_in"], 16)
            for c in range(3):
                for py in range(5):
                    sp.dma_start(img[py:B * 5:5, c, :, :],
                                 t["x"][:, c, PATCH * py:PATCH * py + PATCH, 0:80]).then_inc(s["img_in"], 16)
            sp.dma_start(t["h_dram"][:, NPATCH:N, :], t["txt"]).then_inc(s["txt_copied"], 16)
            for q in range(4):
                sp.wait_ge(s["scaled"], q + 1)
                for k in range(4):
                    sp.dma_start(t["h_dram"][4 * q + k, 0:NPATCH, :],
                                 emb[NPATCH * k:NPATCH * k + NPATCH, q, :]).then_inc(s["stored"], 16)
            sp.wait_ge(s["stored"], 16 * 16)
            sp.wait_ge(s["txt_copied"], 16)

        @block.vector
        def _(dve):
            ch = Chain(dve, s["chain"])
            dve.wait_ge(s["consts_in"], 5 * 16)
            nc.vector.tensor_copy(identb[:, :], ident[:, :]).then_inc(s["identb_ready"], 1)
            ch.link(nc.vector.reciprocal(ralpha[:, :], alpha[:, :]))

            def quantise(src, dst, ra, out_sem):
                ch.link(nc.vector.tensor_scalar(src, src, ra, -128.0, ALU.mult, ALU.max))
                ch.link(nc.vector.tensor_scalar(src, src, 127.0, ROUND, ALU.min, ALU.add))
                nc.vector.tensor_scalar(dst, src, -ROUND, None, ALU.add).then_inc(out_sem, 1)

            quantise(w[:, :, :], wq[:, :, :], ralpha[0:DC, 1:2], s["w_q"])
            dve.wait_ge(s["img_in"], 16 * 15)
            quantise(img[:, :, :, :].rearrange("p c i (x j) -> p (c i) x j", j=PATCH),
                     imgq[:, :, :, :].rearrange("p x r j -> p r x j"), ralpha[0:80, 0:1], s["img_q"])
            ch.link(nc.vector.tensor_tensor(yscale[:, :], alpha[:, 0:1], alpha[:, 1:2], ALU.mult))
            for q in range(4):
                dve.wait_ge(s["product"], q + 1)
                nc.vector.scalar_tensor_tensor(emb[:, q, :], psum[0:100, 2 + q, 0:D], yscale[0:100, :],
                                               bias[0:100, :], ALU.mult, ALU.add).then_inc(s["scaled"], 1)

        @block.tensor
        def _(pe):
            pe.wait_ge(s["identb_ready"], 1)
            pe.wait_ge(s["w_q"], 1)
            for k in range(KC):
                if k >= 2:
                    pe.wait_ge(s["evacuated"], k - 1)
                for c in range(2):
                    mm = nc.tensor.transpose(turn_ps[k % 2][:, c * DC:c * DC + DC], wq[:, c, 128 * k:128 * k + 128],
                                             identb[0:DC, 0:DC])
                mm.then_inc(s["turned"], 1)
            pe.wait_ge(s["img_q"], 1)
            for k in range(KC):
                pe.wait_ge(s["evacuated"], KC + k - 1)
                for px in range(5):
                    src = imgq[:, px, 8 * k:8 * k + 8, :].rearrange("p r j -> p (r j)")
                    mm = nc.tensor.transpose(turn_ps[k % 2][:, px * 80:px * 80 + 80], src, identb[0:80, 0:80])
                mm.then_inc(s["turned"], 1)
            pe.wait_ge(s["evacuated"], 2 * KC)
            for q in range(4):
                for k in range(KC):
                    mm = nc.tensor.matmul(psum[0:100, 2 + q, 0:D],
                                          imgT[:, k, 4 * q:4 * q + 4, :, :].rearrange("p b y x -> p (b y x)"), wT[:, k, :],
                                          start=(k == 0), stop=(k == KC - 1))
                mm.then_inc(s["product"], 1)

        @block.scalar
        def _(act):
            for k in range(KC):
                act.wait_ge(s["turned"], k + 1)
                nc.scalar.copy(wT[:, k, :], turn_ps[k % 2][:, 0:D]).then_inc(s["evacuated"], 1)
            for k in range(KC):
                act.wait_ge(s["turned"], KC + k + 1)
                nc.scalar.copy(imgT[:, k, :, :, :].rearrange("p b y x -> p (b y) x"),
                               turn_ps[k % 2][:, 0:400].rearrange("p (x a) -> p a x", x=5)).then_inc(s["evacuated"], 1)


def spiking_attention(nc, t, psum):
    TURNS = B // 2
    with ExitStack() as ctx:
        def sb(name, shape, dt=FP32):
            return ctx.enter_context(nc.sbuf_tensor("spk_" + name, shape, dt))

        ident = sb("ident", [128, 128])
        heads_mask = sb("heads_mask", [DC, DC])
        wrow = sb("wrow", [DC, 8, D])
        prm_c = sb("prm_c", [DC, 5, 8])
        inv_c = sb("inv_c", [DC, 8])
        thr_c = sb("thr_c", [DC, 8])
        ones = sb("ones", [DC, 128])
        thr_d = sb("thr_d", [DC, 6, DC])
        thr_r = sb("thr_r", [128, 6 * DC])
        wT = sb("wT", [DC, 2, 4 * D])
        half = sb("half", [128, 8])
        h = sb("h", [128, 2, 4, D])
        stats = sb("stats", [128, 4, 6])
        mv = sb("mv", [128, 4, 2])
        rstd = sb("rstd", [128, 4])
        y = sb("y", [128, 4, D])
        yT = sb("yT", [DC, 2, 2, N])
        q = sb("q", [DC, 2, 2, N], BF16)
        kv = sb("kv", [128, 4, 2 * D], BF16)
        kvh = sb("kvh", [DC, 2, 2, DC], BF16)
        xs = sb("xs", [DC, 2, 2, N])
        spike = sb("spike", [128, 4, D])
        hr = sb("hr", [128, 2, 4, D])
        h1 = sb("h1", [128, 4, D])
        stats1 = sb("stats1", [128, 4, 6])
        mv1 = sb("mv1", [128, 4, 2])
        g = sb("g", [128, 5, 4])
        xn = sb("xn", [128, 4, D])
        xnT = sb("xnT", [DC, 2, 2, N])
        s = phase_sems(ctx, nc, "spk", "consts_in w_turned w_out wrow_ready thr_ready ones_ready var_ready thr_ps thr_out in0 in1 res_in0 res_in1 bn rstd_ready y_ready yT_ps yT_ready "
                 "q_ps q_ready kv_ps kv_ready kvh_ps kvh_ready xa_ps xs_ready sp_ps spike_ready h1_ready mv1_ready norm_ready "
                 "xn_ready xnT_ps xnT_ready h1_out xn_out xnT_out half_ready chain passed root")
        block = ctx.enter_context(nc.Block())
        s_in, res_in = (s["in0"], s["in1"]), (s["res_in0"], s["res_in1"])

        def turns(eng, turn):
            turn(0, 0, 0, False, False)
            turn(1, 1, 0, True, False)
            with eng.Fori(0, TURNS // 2 - 2) as pair:
                turn(pair * 2 + 2, 0, pair + 1, True, True)
                turn(pair * 2 + 3, 1, pair + 1, True, True)
            turn(TURNS - 2, 0, TURNS // 2 - 1, True, True)
            turn(TURNS - 1, 1, TURNS // 2 - 1, True, True)

        @block.sync
        def _(sp):
            sp.dma_start(ident[:, :], t["ident"]).then_inc(s["consts_in"], 16)
            sp.dma_start(heads_mask[:, :], t["heads_mask"]).then_inc(s["consts_in"], 16)
            sp.dma_start(wrow[:, :, :], t["attn_W"].rearrange("l (c o) d -> o (l c) d", o=DC)).then_inc(s["consts_in"], 16)
            for n, p in enumerate(t["attn_params"]):
                sp.dma_start(prm_c[:, n, :], p.rearrange("l (c o) -> o (l c)", o=DC), allow_slow_non_contiguous=True).then_inc(s["consts_in"], 16)

            def load(dst, sem, i, u):
                for b in range(2):
                    for tile in range(2):
                        sp.dma_start(dst[:, u, 2 * b + tile, :],
                                     t["h_dram"][2 * i + b, TILE_AT[tile]:TILE_AT[tile] + 128, :]).then_inc(sem[u], 16)

            def store_h1(i):
                sp.wait_ge(s["h1_ready"], i + 1)
                for b in range(2):
                    sp.dma_start(t["h1_dram"][2 * i + b, NPATCH:N, :], h1[:, 2 * b, :]).then_inc(s["h1_out"], 16)
                    sp.dma_start(t["h1_dram"][2 * i + b, 0:NPATCH, :], h1[0:NPATCH, 2 * b + 1, :]).then_inc(s["h1_out"], 16)

            def store_xn(i):
                sp.wait_ge(s["xn_ready"], i + 1)
                for b in range(2):
                    sp.dma_start(t["xn_dram"][2 * i + b, NPATCH:N, :], xn[:, 2 * b, :]).then_inc(s["xn_out"], 16)
                    sp.dma_start(t["xn_dram"][2 * i + b, 0:NPATCH, :], xn[0:NPATCH, 2 * b + 1, :]).then_inc(s["xn_out"], 16)
                sp.wait_ge(s["xnT_ready"], i + 1)
                for b in range(2):
                    sp.dma_start(t["xnT_dram"][2 * i + b, :, :, :].rearrange("c p n -> p c n"),
                                 xnT[:, :, b, :]).then_inc(s["xnT_out"], 16)

            for u in range(2):
                load(h, s_in, u, u)
            for u in range(2):
                load(hr, res_in, u, u)

            def step(i, u):
                sp.wait_ge(s["y_ready"], i + 1)
                load(h, s_in, i + 2, u)

            def stores(i, u):
                store_xn(i - 2)
                store_h1(i - 1)
                load(hr, res_in, i + 1, 1 - u)

            step(0, 0)
            step(1, 1)
            store_h1(0)
            load(hr, res_in, 2, 0)
            with sp.Fori(0, TURNS // 2 - 2) as pair:
                for u in range(2):
                    step(pair * 2 + 2 + u, u)
                    stores(pair * 2 + 2 + u, u)
            stores(TURNS - 2, 0)
            store_xn(TURNS - 3)
            store_h1(TURNS - 2)
            store_xn(TURNS - 2)
            store_h1(TURNS - 1)
            store_xn(TURNS - 1)
            sp.wait_ge(s["h1_out"], 64 * TURNS)
            sp.wait_ge(s["xn_out"], 64 * TURNS)
            sp.wait_ge(s["xnT_out"], 32 * TURNS)

        @block.gpsimd
        def _(pool):
            nc.gpsimd.memset(half[:, :], -0.5).then_inc(s["half_ready"], 1)
            pool.wait_ge(s["half_ready"], 1)

            def factor(i):
                pool.wait_ge(s["bn"], i + 1)
                pool.wait_ge(s["y_ready"], i)
                nc.gpsimd.tensor_tensor(rstd[:, :], mv[:, :, 1], half[:, 0:4], ALU.pow).then_inc(s["rstd_ready"], 1)

            def norm(i):
                pool.wait_ge(s["mv1_ready"], i + 1)
                nc.gpsimd.tensor_tensor(g[:, 2:4, :], g[:, 0:2, :],
                                        half[:, :].rearrange("p (a j) -> p a j", a=2), ALU.pow).then_inc(s["norm_ready"], 1)

            factor(0)
            factor(1)
            with pool.Fori(0, TURNS - 2) as i:
                factor(i + 2)
                norm(i)
            norm(TURNS - 2)
            norm(TURNS - 1)

        @block.vector
        def _(dve):
            ch = Chain(dve, s["chain"], s["passed"])
            nc.vector.memset(ones[:, :], 1.0).then_inc(s["ones_ready"], 1)
            dve.wait_ge(s["consts_in"], 8 * 16)
            nc.vector.tensor_scalar(prm_c[:, 4, :], prm_c[:, 4, :], LN_EPS, None, ALU.add).then_inc(s["var_ready"], 1)
            dve.wait_ge(s["root"], 1)
            ch.link(nc.vector.reciprocal(inv_c[:, :], prm_c[:, 4, :]))
            ch.link(nc.vector.tensor_tensor(inv_c[:, :], inv_c[:, :], prm_c[:, 1, :], ALU.mult))
            ch.link(nc.vector.tensor_tensor(thr_c[:, :], prm_c[:, 0, :], prm_c[:, 3, :], ALU.subtract))
            ch.link(nc.vector.tensor_tensor(thr_c[:, :], thr_c[:, :], inv_c[:, :], ALU.mult))
            ch.link(nc.vector.tensor_tensor(thr_c[:, :], thr_c[:, :], prm_c[:, 2, :], ALU.add))
            ch.link(nc.vector.tensor_scalar(thr_c[:, :], thr_c[:, :], -1.0, 2.0, ALU.mult, ALU.add))
            nc.vector.tensor_tensor(thr_d[:, :, :], ident[0:DC, 0:DC].unsqueeze(1).to_broadcast([DC, 6, DC]),
                                    thr_c[:, 2:8].unsqueeze(2).to_broadcast([DC, 6, DC]), ALU.mult).then_inc(s["thr_ready"], 1)
            nc.vector.tensor_tensor(wrow[:, :, :], wrow[:, :, :],
                                    inv_c[:, :].unsqueeze(2).to_broadcast([DC, 8, D]), ALU.mult).then_inc(s["wrow_ready"], 1)
            SETUP = ch.n
            ALL = 2 + 5 + 1
            FIRST = SETUP + 2 + 2 + 2 + 5

            def normed(i, u, k):
                dve.wait_ge(s_in[u], k * 64 + 64)
                dve.wait_ge(s["rstd_ready"], i)
                for j in range(4):
                    st = nc.vector.bn_stats(stats[:, j, :], h[:, u, j, :])
                ch.link(st, apart=True)
                for j in range(4):
                    st = nc.vector.bn_aggr(mv[:, j, :], stats[:, j, :])
                ch.link(st)
                nc.vector.tensor_scalar(mv[:, :, 1], mv[:, :, 1], LN_EPS, None, ALU.add).then_inc(s["bn"], 1)

            def make_y(i, u):
                dve.wait_ge(s["rstd_ready"], i + 1)
                dve.wait_ge(s["yT_ps"], i)
                for j in range(4):
                    st = nc.vector.tensor_scalar(y[:, j, :], h[:, u, j, :], mv[:, j, 0:1], rstd[:, j:j + 1],
                                                 ALU.subtract, ALU.mult)
                st.then_inc(s["y_ready"], 1)

            def mask_kv(i):
                dve.wait_ge(s["kvh_ps"], i + 1)
                for b in range(2):
                    st = nc.vector.tensor_tensor(kvh[:, b, :, :],
                                                 psum[0:DC, 4, b * D:b * D + D].rearrange("p (c e) -> p c e", c=2),
                                                 heads_mask[:, :].unsqueeze(1).to_broadcast([DC, 2, DC]), ALU.mult)
                st.then_inc(s["kvh_ready"], 1)

            def make_xn(i):
                dve.wait_ge(s["norm_ready"], i + 1)
                ch.link(nc.vector.tensor_tensor(g[:, 4, :], g[:, 2, :], g[:, 3, :], ALU.mult))
                dve.wait_ge(s["xn_out"], i * 64)
                dve.wait_ge(s["xnT_ps"], i)
                for j in range(4):
                    st = nc.vector.tensor_scalar(xn[:, j, :], h1[:, j, :], mv1[:, j, 0:1], g[:, 4, j:j + 1],
                                                 ALU.subtract, ALU.mult)
                st.then_inc(s["xn_ready"], 1)

            def make_xs(i):
                dve.wait_ge(s["xa_ps"], i + 1)
                dve.wait_ge(s["sp_ps"], i)
                for c in range(2):
                    st = nc.vector.tensor_scalar(xs[:, c, :, :], psum[0:DC, 5 + c, 0:2 * N].rearrange("p (b n) -> p b n", b=2),
                                                 float(DH) ** -0.125, 1.0, ALU.mult, ALU.is_ge)
                st.then_inc(s["xs_ready"], 1)

            def make_q(i):
                dve.wait_ge(s["q_ps"], i + 1)
                dve.wait_ge(s["xa_ps"], i)
                for c in range(2):
                    st = nc.vector.tensor_scalar(q[:, c, :, :], psum[0:DC, 2 + c, 0:2 * N].rearrange("p (b n) -> p b n", b=2),
                                                 thr_c[:, c:c + 1], None, ALU.is_ge)
                st.then_inc(s["q_ready"], 1)

            def make_kv(i):
                dve.wait_ge(s["kv_ps"], i + 1)
                dve.wait_ge(s["kvh_ps"], i)
                nc.vector.tensor_tensor(kv[:, :, :], psum[:, 4:8, 0:2 * D],
                                        thr_r[:, 0:2 * D].unsqueeze(1).to_broadcast([128, 4, 2 * D]),
                                        ALU.is_ge).then_inc(s["kv_ready"], 1)

            def residual(i, u, k):
                dve.wait_ge(s["sp_ps"], i + 1)
                nc.vector.tensor_tensor(spike[:, :, :], psum[:, 0:2, 0:2 * D].rearrange("p k (a d) -> p k a d", a=2),
                                        thr_r[:, 2 * D:3 * D].unsqueeze(1).unsqueeze(1).to_broadcast([128, 2, 2, D]),
                                        ALU.is_ge).then_inc(s["spike_ready"], 1)
                dve.wait_ge(s["spike_ready"], i + 1)
                dve.wait_ge(res_in[u], k * 64 + 64)
                dve.wait_ge(s["h1_out"], i * 64)
                nc.vector.tensor_tensor(h1[:, :, :], hr[:, u, :, :], spike[:, :, :], ALU.add).then_inc(s["h1_ready"], 1)
                dve.wait_ge(s["h1_ready"], i + 1)
                for j in range(4):
                    st = nc.vector.bn_stats(stats1[:, j, :], h1[:, j, :])
                ch.link(st, apart=True)
                for j in range(4):
                    st = nc.vector.bn_aggr(mv1[:, j, :], stats1[:, j, :])
                ch.link(st)
                ch.link(nc.vector.tensor_scalar(g[:, 0, :], mv1[:, :, 1], LN_EPS, None, ALU.add))
                ch.link(nc.vector.reciprocal(g[:, 1, :], g[:, 0, :]))
                ch.link(nc.vector.tensor_tensor(g[:, 1, :], g[:, 1, :], mv1[:, :, 1], ALU.mult))
                nc.vector.tensor_scalar(g[:, 1, :], g[:, 1, :], float(D), 1e-24, ALU.mult, ALU.max).then_inc(s["mv1_ready"], 1)

            normed(0, 0, 0)
            make_y(0, 0)
            dve.wait_ge(s["thr_out"], 1)

            def turn(i, u, k, middle, last):
                following = not (isinstance(i, int) and i == TURNS - 1)
                before = k if u else k - 1
                if last:
                    ch.base, ch.n = FIRST + (i - 2) * ALL, 0
                if middle:
                    mask_kv(i - 1)
                if last:
                    make_xn(i - 2)
                if following:
                    normed(i + 1, 1 - u, k if not u else k + 1)
                if middle:
                    make_xs(i - 1)
                make_q(i)
                if following:
                    make_y(i + 1, 1 - u)
                make_kv(i)
                if middle:
                    residual(i - 1, 1 - u, before)
            turns(dve, turn)
            mask_kv(TURNS - 1)
            make_xn(TURNS - 2)
            make_xs(TURNS - 1)
            residual(TURNS - 1, 1, TURNS // 2 - 1)
            make_xn(TURNS - 1)

        @block.scalar
        def _(act):
            act.wait_ge(s["var_ready"], 1)
            nc.scalar.activation(prm_c[:, 4, :], prm_c[:, 4, :], ACT.Sqrt).then_inc(s["root"], 1)
            act.wait_ge(s["thr_ps"], 1)
            nc.scalar.copy(thr_r[:, :].rearrange("p (k n) -> p k n", k=2), psum[:, 4:6, 0:3 * DC]).then_inc(s["thr_out"], 1)
            for c in range(2):
                act.wait_ge(s["w_turned"], c + 1)
                nc.scalar.copy(wT[:, c, :].rearrange("p (k o) -> p k o", k=2),
                               psum[0:DC, 2 * c:2 * c + 2, 0:4 * DC]).then_inc(s["w_out"], 1)

            def copy_yT(i):
                act.wait_ge(s["yT_ps"], i + 1)
                act.wait_ge(s["kv_ps"], i)
                nc.scalar.copy(yT[:, :, :, :], psum[0:DC, 0:2, 0:2 * N].rearrange("p c (b n) -> p c b n", b=2)).then_inc(s["yT_ready"], 1)

            def copy_xnT(i):
                act.wait_ge(s["xnT_ps"], i + 1)
                act.wait_ge(s["xnT_out"], i * 32)
                nc.scalar.copy(xnT[:, :, :, :], psum[0:DC, 2:4, 0:2 * N].rearrange("p c (b n) -> p c b n", b=2)).then_inc(s["xnT_ready"], 1)

            def turn(i, u, k, middle, last):
                copy_yT(i)
                if last:
                    copy_xnT(i - 2)
            turns(act, turn)
            copy_xnT(TURNS - 2)
            copy_xnT(TURNS - 1)

        @block.tensor
        def _(pe):
            pe.wait_ge(s["ones_ready"], 1)
            pe.wait_ge(s["thr_ready"], 1)
            for k in range(2):
                mm = nc.tensor.matmul(psum[:, 4 + k, 0:3 * DC], ones[:, :], thr_d[:, 3 * k:3 * k + 3, :].rearrange("p a b -> p (a b)"),
                                      start=True, stop=True)
            mm.then_inc(s["thr_ps"], 1)
            pe.wait_ge(s["wrow_ready"], 1)
            for c in range(2):
                for k in range(8):
                    mm = nc.tensor.transpose(psum[0:DC, 2 * c + k // 4, (k % 4) * DC:(k % 4) * DC + DC],
                                             wrow[:, k, c * DC:c * DC + DC], ident[0:DC, 0:DC])
                mm.then_inc(s["w_turned"], 1)
            pe.wait_ge(s["w_out"], 2)
            pe.wait_ge(s["thr_out"], 1)

            def turned(src, bank):
                for c in range(2):
                    for b in range(2):
                        for tile in range(2):
                            rows, at = TILE_ROWS[tile], b * N + TILE_AT[tile]
                            mm = nc.tensor.transpose(psum[0:DC, bank + c, at:at + rows],
                                                     src[0:rows, 2 * b + tile, c * DC:c * DC + DC], ident[0:rows, 0:rows])
                return mm

            def turn_y(i):
                pe.wait_ge(s["y_ready"], i + 1)
                if not (isinstance(i, int) and i < 2):
                    pe.wait_ge(s["spike_ready"], i - 1)
                turned(y, 0).then_inc(s["yT_ps"], 1)

            def product_kv(i):
                pe.wait_ge(s["kv_ready"], i + 1)
                for b in range(2):
                    for c in range(2):
                        for tile in range(2):
                            rows = TILE_ROWS[tile]
                            mm = nc.tensor.matmul(psum[0:DC, 4, b * D + c * DC:b * D + c * DC + DC],
                                                  kv[0:rows, 2 * b + tile, c * DC:c * DC + DC],
                                                  kv[0:rows, 2 * b + tile, D + c * DC:D + c * DC + DC],
                                                  start=(tile == 0), stop=(tile == 1))
                mm.then_inc(s["kvh_ps"], 1)

            def project_q(i):
                pe.wait_ge(s["yT_ready"], i + 1)
                if not (isinstance(i, int) and i < 3):
                    pe.wait_ge(s["xnT_ready"], i - 2)
                pe.wait_ge(s["q_ready"], i)
                for m in range(2):
                    for c in range(2):
                        mm = nc.tensor.matmul(psum[0:DC, 2 + m, 0:2 * N], wT[:, c, m * DC:m * DC + DC],
                                              yT[:, c, :, :], start=(c == 0), stop=(c == 1))
                mm.then_inc(s["q_ps"], 1)

            def attend(i):
                pe.wait_ge(s["kvh_ready"], i + 1)
                pe.wait_ge(s["q_ready"], i + 1)
                pe.wait_ge(s["kv_ready"], i + 1)
                for b in range(2):
                    for c in range(2):
                        mm = nc.tensor.matmul(psum[0:DC, 5 + c, b * N:b * N + N], kvh[:, b, c, :], q[:, c, b, :],
                                              start=True, stop=True)
                mm.then_inc(s["xa_ps"], 1)

            def project_kv(i, middle):
                pe.wait_ge(s["kv_ready"], i)
                for n, j in enumerate((3, 0, 1, 2)):
                    if n == 1 and middle:
                        pe.wait_ge(s["kvh_ready"], i)
                    if n == 2 and middle:
                        pe.wait_ge(s["xs_ready"], i)
                    at = TILE_AT[j % 2]
                    for c in range(2):
                        mm = nc.tensor.matmul(psum[:, 4 + j, 0:2 * D], yT[:, c, j // 2, at:at + 128],
                                              wT[:, c, D:3 * D], start=(c == 0), stop=(c == 1))
                mm.then_inc(s["kv_ps"], 1)

            def turn_xn(i, latest):
                pe.wait_ge(s["xn_ready"], i + 1)
                pe.wait_ge(s["q_ready"], latest)
                pe.wait_ge(s["xnT_ready"], i)
                turned(xn, 2).then_inc(s["xnT_ps"], 1)

            def spikes(i, latest):
                pe.wait_ge(s["xs_ready"], i + 1)
                pe.wait_ge(s["yT_ready"], latest)
                for j in range(4):
                    at = TILE_AT[j % 2]
                    for c in range(2):
                        mm = nc.tensor.matmul(psum[:, j // 2, (j % 2) * D:(j % 2) * D + D], xs[:, c, j // 2, at:at + 128],
                                              wT[:, c, 3 * D:4 * D], start=(c == 0), stop=(c == 1))
                mm.then_inc(s["sp_ps"], 1)

            def turn(i, u, k, middle, last):
                turn_y(i)
                if middle:
                    product_kv(i - 1)
                project_q(i)
                if middle:
                    attend(i - 1)
                project_kv(i, middle)
                if last:
                    turn_xn(i - 2, i + 1)
                if middle:
                    spikes(i - 1, i + 1)
            turns(pe, turn)
            product_kv(TURNS - 1)
            attend(TURNS - 1)
            turn_xn(TURNS - 2, TURNS)
            pe.wait_ge(s["spike_ready"], TURNS - 1)
            spikes(TURNS - 1, TURNS)
            turn_xn(TURNS - 1, TURNS)


def dispatch(nc, t, psum, slotsT):
    HALF = 512
    with ExitStack() as ctx:
        def sb(name, shape, dt=FP32):
            return ctx.enter_context(nc.sbuf_tensor("dsp_" + name, shape, dt))

        ident = sb("ident", [128, 128])
        ones = sb("ones", [DC, DC])
        phin = sb("phin", [DC, 2, SLOTS])
        phins = sb("phins", [DC, 2, 2, SLOTS], F32R)
        scale = sb("scale", [DC, 1])
        xn = sb("xn", [128, 2, 2, D])
        xnT = sb("xnT", [DC, 2, 2, N])
        xnTs = sb("xnTs", [DC, 2, 2, N], F32R)
        e = sb("e", [128, 2, 2, SLOTS])
        dw = sb("dw", [128, 2, 2, SLOTS])
        m = sb("m", [128, 2, E0])
        top = sb("top", [128, 2])
        mg = sb("mg", [128, 2, E0])
        se = sb("se", [128, 2, E0])
        rse = sb("rse", [128, 2, E0])
        sg = sb("sg", [128, 2, E0])
        z = sb("z", [128, 2])
        kc = sb("kc", [128, 2, 2, E0])
        cwT = sb("cwT", [128, NG, N])
        s = phase_sems(ctx, nc, "dsp", "consts_in ones_ready sq_ready norm_ps norm2 root phin_ready in0 in1 logits shifted mg_ready exped gexped "
                 "dw_ready kc_ready cw_ready slots_ps slots_out cwT_ps cwT_out cwT_stored chain "
                 "phin_hi xn_hi xn_lo t_in0 t_in1")
        block = ctx.enter_context(nc.Block())
        s_in, t_in = (s["in0"], s["in1"]), (s["t_in0"], s["t_in1"])
        sq = dw[0:DC, 0, :, :]
        nrm = dw[0:DC, 1, 0, :]

        def run(eng, turn):
            turn(0, 0, 0)
            with eng.Fori(0, B // 2 - 1) as pair:
                turn(pair * 2 + 1, 1, pair)
                turn(pair * 2 + 2, 0, pair + 1)
            turn(B - 1, 1, B // 2 - 1)

        @block.sync
        def _(sp):
            sp.dma_start(ident[:, :], t["ident"]).then_inc(s["consts_in"], 16)
            sp.dma_start(phin[:, :, :], t["ffn_phi"].rearrange("(c p) e s -> p c (e s)", p=DC)).then_inc(s["consts_in"], 16)
            sp.dma_start(scale[:, :], row_bc(t["ffn_scale"], DC)).then_inc(s["consts_in"], 16)

            def load(b, u):
                sp.dma_start(xn[:, u, 0, :], t["xn_dram"][b, NPATCH:N, :]).then_inc(s_in[u], 16)
                sp.dma_start(xn[0:NPATCH, u, 1, :], t["xn_dram"][b, 0:NPATCH, :]).then_inc(s_in[u], 16)

            def load_turned(b, u):
                sp.dma_start(xnT[:, u, :, :], t["xnT_dram"][b, :, :, :].rearrange("c p n -> p c n")).then_inc(t_in[u], 16)

            def store(b):
                sp.wait_ge(s["cwT_out"], 3 * b + 3)
                sp.dma_start(t["cwT_dram"][b, :, :, :].rearrange("g p n -> p g n"), cwT[:, :, :]).then_inc(s["cwT_stored"], 16)

            for u in range(2):
                load_turned(u, u)
                load(u, u)
            with sp.Fori(0, B // 2 - 1) as pair:
                for u in range(2):
                    b = pair * 2 + u
                    sp.wait_ge(s["xn_lo"], b + 1)
                    load_turned(b + 2, u)
                    sp.wait_ge(s["slots_ps"], 2 * b + 2)
                    load(b + 2, u)
                    store(b)
            store(B - 2)
            store(B - 1)
            sp.wait_ge(s["cwT_stored"], 16 * B)

        @block.vector
        def _(dve):
            ch = Chain(dve, s["chain"])
            nc.vector.memset(ones[:, :], 1.0).then_inc(s["ones_ready"], 1)
            dve.wait_ge(s["consts_in"], 48)
            nc.vector.tensor_tensor(sq, phin[:, :, :], phin[:, :, :], ALU.mult).then_inc(s["sq_ready"], 1)
            dve.wait_ge(s["norm_ps"], 1)
            nc.vector.tensor_scalar(nrm, psum[0:DC, 0:2, :].rearrange("p a b -> p (a b)"), 1e-24, None, ALU.max).then_inc(s["norm2"], 1)
            dve.wait_ge(s["root"], 1)
            ch.link(nc.vector.reciprocal(nrm, nrm))
            ch.link(nc.vector.tensor_scalar(nrm, nrm, scale[:, :], None, ALU.mult))
            ch.link(nc.vector.tensor_tensor(phin[:, :, :], phin[:, :, :], nrm.unsqueeze(1).to_broadcast([DC, 2, SLOTS]), ALU.mult))
            nc.vector.tensor_copy(phins[:, 0, :, :], phin[:, :, :]).then_inc(s["phin_hi"], 1)
            dve.wait_ge(s["phin_hi"], 1)
            nc.vector.tensor_tensor(phins[:, 1, :, :], phin[:, :, :], phins[:, 0, :, :].bitcast(FP32), ALU.subtract).then_inc(s["phin_ready"], 1)

            def rest(b, u):
                dve.wait_ge(s["xn_hi"], b + 1)
                nc.vector.tensor_tensor(xnTs[:, 1, :, :], xnT[:, u, :, :], xnTs[:, 0, :, :].bitcast(FP32), ALU.subtract).then_inc(s["xn_lo"], 1)

            rest(0, 0)
            LINKS = 6

            def turn(b, u, k):
                ch.base, ch.n = 3 + b * LINKS, 0
                lg = psum[:, 0:4, :].rearrange("p k (e s) -> p (k e) s", s=S0)
                dve.wait_ge(s["logits"], b + 1)
                ch.link(nc.vector.tensor_reduce(m[:, :, :].rearrange("p t e -> p (t e)"), lg, AXX, ALU.max))
                dve.wait_ge(s["gexped"], b)
                if not (isinstance(b, int) and b < 2):
                    dve.wait_ge(s["cwT_ps"], b - 1)
                nc.vector.tensor_tensor(e[:, u, :, :].rearrange("p t (e s) -> p (t e) s", s=S0), lg,
                                        m[:, :, :].rearrange("p t e -> p (t e)").unsqueeze(2).to_broadcast([128, 2 * E0, S0]),
                                        ALU.subtract).then_inc(s["shifted"], 1)
                ch.link(nc.vector.tensor_reduce(top[:, :], m[:, :, :], AXX, ALU.max))
                nc.vector.tensor_tensor(mg[:, :, :], m[:, :, :], top[:, :].unsqueeze(2).to_broadcast([128, 2, E0]),
                                        ALU.subtract).then_inc(s["mg_ready"], 1)
                if not (isinstance(b, int) and b == B - 1):
                    rest(b + 1, 1 - u)
                dve.wait_ge(s["exped"], b + 1)
                ch.link(nc.vector.tensor_reduce(se[:, :, :].rearrange("p t e -> p (t e)"),
                                                e[:, u, :, :].rearrange("p t (e s) -> p (t e) s", s=S0), AXX, ALU.add))
                dve.wait_ge(s["gexped"], b + 1)
                nc.vector.reciprocal(rse[:, :, :], se[:, :, :])
                ch.link(nc.vector.tensor_tensor(sg[:, :, :], se[:, :, :], mg[:, :, :], ALU.mult))
                ch.link(nc.vector.tensor_reduce(z[:, :], sg[:, :, :], AXX, ALU.add))
                ch.link(nc.vector.reciprocal(z[:, :], z[:, :]))
                nc.vector.tensor_tensor(kc[:, u, :, :], mg[:, :, :], z[:, :].unsqueeze(2).to_broadcast([128, 2, E0]),
                                        ALU.mult).then_inc(s["kc_ready"], 1)
                if not (isinstance(b, int) and b < 2):
                    dve.wait_ge(s["slots_ps"], 2 * b - 2)
                nc.vector.tensor_tensor(dw[:, u, :, :].rearrange("p t (e s) -> p (t e) s", s=S0),
                                        e[:, u, :, :].rearrange("p t (e s) -> p (t e) s", s=S0),
                                        rse[:, :, :].rearrange("p t e -> p (t e)").unsqueeze(2).to_broadcast([128, 2 * E0, S0]),
                                        ALU.mult).then_inc(s["dw_ready"], 1)
                dve.wait_ge(s["dw_ready"], b + 1)
            run(dve, turn)

        @block.gpsimd
        def _(pool):
            def turn(b, u, k):
                pool.wait_ge(s["kc_ready"], b + 1)
                pool.wait_ge(s["dw_ready"], b + 1)
                for tile in range(2):
                    ev = e[:, u, tile, :].rearrange("p (e s) -> p e s", s=S0)
                    nc.gpsimd.tensor_tensor(ev, ev, kc[:, u, tile, :].unsqueeze(2).to_broadcast([128, E0, S0]),
                                            ALU.mult).then_inc(s["cw_ready"], 1)
            run(pool, turn)

        @block.scalar
        def _(act):
            act.wait_ge(s["norm2"], 1)
            nc.scalar.activation(nrm, nrm, ACT.Sqrt).then_inc(s["root"], 1)

            def round_off(b, u, k):
                act.wait_ge(t_in[u], 16 * k + 16)
                act.wait_ge(s["logits"], b)
                nc.scalar.copy(xnTs[:, 0, :, :], xnT[:, u, :, :]).then_inc(s["xn_hi"], 1)

            round_off(0, 0, 0)

            def softmax(b, u):
                act.wait_ge(s["shifted"], b + 1)
                nc.scalar.activation(e[:, u, :, :], e[:, u, :, :], ACT.Exp).then_inc(s["exped"], 1)
                act.wait_ge(s["mg_ready"], b + 1)
                nc.scalar.activation(mg[:, :, :], mg[:, :, :], ACT.Exp).then_inc(s["gexped"], 1)

            def copy_slots(b, c):
                act.wait_ge(s["slots_ps"], 2 * b + c + 1)
                nc.scalar.copy(slotsT[:, c, :, b, :],
                               psum[0:DC, 4 + 2 * c:6 + 2 * c, :].rearrange("p k (e s) -> p (k e) s", s=S0)).then_inc(s["slots_out"], 1)

            def copy_cwT(b):
                act.wait_ge(s["cwT_ps"], b + 1)
                act.wait_ge(s["cwT_stored"], b * 16)
                for k in range(3):
                    n = min(3, NG - 3 * k)
                    nc.scalar.copy(cwT[:, 3 * k:3 * k + n, :],
                                   psum[:, 4 + k, 0:n * N].rearrange("p (g n) -> p g n", g=n)).then_inc(s["cwT_out"], 1)

            def turn(b, u, k):
                following = not isinstance(b, int) or b
                if not (isinstance(b, int) and b == B - 1):
                    round_off(b + 1, 1 - u, k + u)
                if following:
                    copy_slots(b - 1, 0)
                softmax(b, u)
                if following:
                    copy_slots(b - 1, 1)
                    copy_cwT(b - 1)
            run(act, turn)
            for c in range(2):
                copy_slots(B - 1, c)
            copy_cwT(B - 1)

        @block.tensor
        def _(pe):
            pe.wait_ge(s["ones_ready"], 1)
            pe.wait_ge(s["sq_ready"], 1)
            for k in range(2):
                for c in range(2):
                    mm = nc.tensor.matmul(psum[0:DC, k, :], ones[:, :], sq[:, c, k * HALF:k * HALF + HALF],
                                          start=(c == 0), stop=(c == 1))
            mm.then_inc(s["norm_ps"], 1)
            pe.wait_ge(s["phin_ready"], 1)

            def logits(b, u, k):
                pe.wait_ge(s["xn_lo"], b + 1)
                pe.wait_ge(s["shifted"], b)
                for tile in range(2):
                    at = TILE_AT[tile]
                    for k in range(2):
                        parts = [(c, xp, fp) for xp, fp in ((0, 1), (1, 0), (0, 0)) for c in range(2)]
                        for n, (c, xp, fp) in enumerate(parts):
                            mm = nc.tensor.matmul(psum[:, 2 * tile + k, :], xnTs[:, xp, c, at:at + 128],
                                                  phins[:, fp, c, k * HALF:k * HALF + HALF], start=(n == 0), stop=(n == len(parts) - 1))
                mm.then_inc(s["logits"], 1)

            def slots(b, u, k):
                pe.wait_ge(s_in[u], 32 * k + 32)
                pe.wait_ge(s["dw_ready"], b + 1)
                pe.wait_ge(s["cwT_out"], 3 * b)
                pe.wait_ge(s["slots_out"], 2 * b)
                for c in range(2):
                    for k in range(2):
                        for tile in range(2):
                            rows = TILE_ROWS[tile]
                            mm = nc.tensor.matmul(psum[0:DC, 4 + 2 * c + k, :], xn[0:rows, u, tile, c * DC:c * DC + DC],
                                                  dw[0:rows, u, tile, k * HALF:k * HALF + HALF],
                                                  start=(tile == 0), stop=(tile == 1))
                    mm.then_inc(s["slots_ps"], 1)
                pe.wait_ge(s["cw_ready"], 2 * b + 2)
                pe.wait_ge(s["slots_out"], 2 * b + 1)
                for g in range(NG):
                    if g == 6:
                        pe.wait_ge(s["slots_out"], 2 * b + 2)
                    for tile in range(2):
                        rows, at = TILE_ROWS[tile], (g % 3) * N + TILE_AT[tile]
                        mm = nc.tensor.transpose(psum[:, 4 + g // 3, at:at + rows],
                                                 e[0:rows, u, tile, 128 * g:128 * g + 128], ident[0:rows, 0:rows])
                mm.then_inc(s["cwT_ps"], 1)

            def turn(b, u, k):
                logits(b, u, k)
                if not isinstance(b, int) or b:
                    slots(b - 1, 1 - u, k if u else k - 1)
            run(pe, turn)
            slots(B - 1, 1, B // 2 - 1)


def soft_experts(nc, t, psum, slotsT):
    HJ = H0 // 128
    ROWS = B * S0
    with ExitStack() as ctx:
        def sb(name, shape, dt=FP32):
            return ctx.enter_context(nc.sbuf_tensor("exp_" + name, shape, dt))

        ident = sb("ident", [128, 128])
        b1rows = sb("b1rows", [DC, 2, 128])
        b1T = sb("b1T", [128, E0 * HJ])
        w1 = sb("w1", [DC, 2, 2, H0])
        w1s = sb("w1s", [DC, 2, 2, H0], F32R)
        sls = sb("sls", [DC, 2, 2, ROWS], F32R)
        w2 = sb("w2", [128, 2, HJ, D])
        b2 = sb("b2", [128, 2, D])
        hT = sb("hT", [128, 2, HJ, ROWS])
        eo = sb("eo", [128, 2, 4, D])
        s = phase_sems(ctx, nc, "exp", "consts_in b1_ps b1_ready w1_in0 w1_in1 w2_in0 w2_in1 h_ps h_ready o_ps o_ready0 o_ready1 stored0 stored1 "
                       "hi_ready lo_ready")
        block = ctx.enter_context(nc.Block())
        o_ready = (s["o_ready0"], s["o_ready1"])
        w1_in, w2_in, stored = (s["w1_in0"], s["w1_in1"]), (s["w2_in0"], s["w2_in1"]), (s["stored0"], s["stored1"])
        eo_view = t["eo_dram"].rearrange("(t q) k d -> q k t d", q=4)

        def run(eng, turn):
            turn(0, 0, 0, 0)
            with eng.Fori(0, E0 // 2 - 1) as pair:
                turn(pair * 2 + 1, 1, pair, pair)
                turn(pair * 2 + 2, 0, pair + 1, pair)
            turn(E0 - 1, 1, E0 // 2 - 1, E0 // 2 - 1)

        @block.sync
        def _(sp):
            sp.dma_start(ident[:, :], t["ident"]).then_inc(s["consts_in"], 16)
            sp.dma_start(b1rows[:, :, :], t["ffn_b1"].rearrange("(c e) (j p) -> (e j) c p", c=2, p=128)).then_inc(s["consts_in"], 16)

            def load_w1(e, u):
                sp.dma_start(w1[:, u, :, :], t["ffn_w1"][e, :, :].rearrange("(c p) h -> p c h", p=DC)).then_inc(w1_in[u], 16)

            def load_w2(e, u):
                sp.dma_start(w2[:, u, :, :], t["ffn_w2"][e, :, :].rearrange("(j p) d -> p j d", p=128)).then_inc(w2_in[u], 16)
                sp.dma_start(b2[:, u, :], row_bc(t["ffn_b2"][e, :], 128)).then_inc(w2_in[u], 16)

            for e in range(2):
                load_w1(e, e)
                load_w2(e, e)
            with sp.Fori(0, E0 // 2 - 1) as pair:
                for u in range(2):
                    e = pair * 2 + u
                    sp.wait_ge(s["lo_ready"], 2 * e + 2)
                    load_w1(e + 2, u)
                    sp.wait_ge(s["o_ready0"], e + 1)
                    sp.wait_ge(s["o_ready1"], e + 1)
                    load_w2(e + 2, u)

        @block.gpsimd
        def _(pool):
            def turn(e, u, k, before):
                pool.wait_ge(s["o_ready0"], e + 1)
                pool.wait_ge(s["o_ready1"], e + 1)
                for q in range(4):
                    pool.dma_start(eo_view[q, bass.ds(e * S0, S0), :, :], eo[S0 * q:S0 * q + S0, u, :, :]).then_inc(stored[u], 16)
            run(pool, turn)
            for u in range(2):
                pool.wait_ge(stored[u], 64 * (E0 // 2))

        @block.scalar
        def _(act):
            act.wait_ge(s["b1_ps"], 1)
            nc.scalar.copy(b1T[:, :], psum[:, 0, 0:E0 * HJ]).then_inc(s["b1_ready"], 1)
            act.wait_ge(s["b1_ready"], 1)

            def round_off(e, u, k):
                act.wait_ge(w1_in[u], 16 * k + 16)
                act.wait_ge(s["h_ps"], HJ * e)
                nc.scalar.copy(w1s[:, 0, :, :], w1[:, u, :, :]).then_inc(s["hi_ready"], 1)
                nc.scalar.copy(sls[:, 0, :, :], slotsT[:, :, e, :, :].rearrange("p c b s -> p c (b s)")).then_inc(s["hi_ready"], 1)

            round_off(0, 0, 0)

            def turn(e, u, k, before):
                if not (isinstance(e, int) and e < 2):
                    act.wait_ge(s["o_ps"], 2 * e - 2)
                for j in range(HJ):
                    act.wait_ge(s["h_ps"], HJ * e + j + 1)
                    nc.scalar.activation(hT[:, u, j, :], psum[:, j, :], ACT.Gelu,
                                         bias=b1T[:, bass.ds(e * HJ + j, 1)]).then_inc(s["h_ready"], 1)
                if not (isinstance(e, int) and e == E0 - 1):
                    round_off(e + 1, 1 - u, k + u)
            run(act, turn)

        @block.vector
        def _(dve):
            def rest(e, u):
                dve.wait_ge(s["hi_ready"], 2 * e + 1)
                nc.vector.tensor_tensor(w1s[:, 1, :, :], w1[:, u, :, :], w1s[:, 0, :, :].bitcast(FP32),
                                        ALU.subtract).then_inc(s["lo_ready"], 1)
                dve.wait_ge(s["hi_ready"], 2 * e + 2)
                nc.vector.tensor_tensor(sls[:, 1, :, :], slotsT[:, :, e, :, :].rearrange("p c b s -> p c (b s)"),
                                        sls[:, 0, :, :].bitcast(FP32), ALU.subtract).then_inc(s["lo_ready"], 1)

            rest(0, 0)

            def outputs(e, u, k):
                dve.wait_ge(w2_in[u], 32 * k + 32)
                dve.wait_ge(stored[u], 64 * k)
                for n in range(2):
                    dve.wait_ge(s["o_ps"], 2 * e + n + 1)
                    nc.vector.tensor_tensor(eo[:, u, 2 * n:2 * n + 2, :],
                                            psum[:, 6 + n, 0:2 * D].rearrange("p (a d) -> p a d", a=2),
                                            b2[:, u, :].unsqueeze(1).to_broadcast([128, 2, D]), ALU.add).then_inc(o_ready[n], 1)

            def turn(e, u, k, before):
                if not (isinstance(e, int) and e == E0 - 1):
                    rest(e + 1, 1 - u)
                if not (isinstance(e, int) and e == 0):
                    outputs(e - 1, 1 - u, before)
            run(dve, turn)
            outputs(E0 - 1, 1, E0 // 2 - 1)

        @block.tensor
        def _(pe):
            pe.wait_ge(s["consts_in"], 32)
            for c in range(2):
                mm = nc.tensor.transpose(psum[:, 0, c * DC:c * DC + DC], b1rows[:, c, :], ident[0:DC, 0:DC])
            mm.then_inc(s["b1_ps"], 1)
            pe.wait_ge(s["b1_ready"], 1)

            def hidden(e, u, k):
                pe.wait_ge(s["lo_ready"], 2 * e + 2)
                for j in range(HJ):
                    if not (isinstance(e, int) and e == 0):
                        pe.wait_ge(s["h_ready"], HJ * (e - 1) + j + 1)
                    parts = [(c, wp, xp) for wp, xp in ((0, 1), (1, 0), (0, 0)) for c in range(2)]
                    for n, (c, wp, xp) in enumerate(parts):
                        mm = nc.tensor.matmul(psum[:, j, :], w1s[:, wp, c, 128 * j:128 * j + 128], sls[:, xp, c, :],
                                              start=(n == 0), stop=(n == len(parts) - 1))
                    mm.then_inc(s["h_ps"], 1)

            def output(e, u, k):
                pe.wait_ge(w2_in[u], 32 * k + 32)
                pe.wait_ge(s["h_ready"], HJ * e + HJ)
                for n in range(2):
                    pe.wait_ge(o_ready[n], e)
                    for a in range(2):
                        for j in range(HJ):
                            at = 128 * (2 * n + a)
                            mm = nc.tensor.matmul(psum[:, 6 + n, a * D:a * D + D], hT[:, u, j, at:at + 128], w2[:, u, j, :],
                                                  start=(j == 0), stop=(j == HJ - 1))
                    mm.then_inc(s["o_ps"], 1)

            def turn(e, u, k, before):
                hidden(e, u, k)
                if not (isinstance(e, int) and e == 0):
                    output(e - 1, 1 - u, before)
            run(pe, turn)
            output(E0 - 1, 1, E0 // 2 - 1)


def soft_mixture(nc, t, psum):
    with nc.sbuf_tensor("slotsT", [DC, 2, E0, B, S0], FP32) as slotsT:
        dispatch(nc, t, psum, slotsT)
        soft_experts(nc, t, psum, slotsT)


def combine(nc, t, psum, th):
    RESO = 4 * HEADS
    with ExitStack() as ctx:
        def sb(name, shape, dt=FP32):
            return ctx.enter_context(nc.sbuf_tensor("cmb_" + name, shape, dt))

        ident = sb("ident", [128, 128])
        half = sb("half", [128, 2])
        lnw = sb("lnw", [DC, 2])
        wcomp = sb("wcomp", [DC, 2, 128])
        wreso = sb("wreso", [128, RESO])
        cw = sb("cw", [128, 2, NG, N])
        eo = sb("eo", [128, 2, NG, D])
        h1 = sb("h1", [128, 2, 2, D])
        h2 = sb("h2", [128, 2, D])
        stats = sb("stats", [128, 2, 6])
        mv = sb("mv", [128, 2, 2])
        g = sb("g", [128, 3, 2])
        r = sb("r", [128, 2, 2])
        y = sb("y", [128, 2, D])
        xr = sb("xr", [128, 2, D])
        xrT = sb("xrT", [DC, 2, N])
        lth = sb("lth", [128, N])
        lat = sb("lat", [128, N])
        s = phase_sems(ctx, nc, "cmb", "consts_in wcomp_ready half_ready in0 in1 comb_ps h2_ready var_ready r_ready y_ready y_stored h2_stored xr_ready "
                 "xrT_ps xrT_ready lat_ps lth_ready lat_ready lat_stored reso_ps th_ready chain passed")
        block = ctx.enter_context(nc.Block())
        s_in = (s["in0"], s["in1"])
        LOADS = 4 * 16

        def run(eng, turn):
            turn(0, 0, 0)
            with eng.Fori(0, B // 2 - 1) as pair:
                turn(pair * 2 + 1, 1, pair)
                turn(pair * 2 + 2, 0, pair + 1)
            turn(B - 1, 1, B // 2 - 1)

        @block.sync
        def _(sp):
            def load(b, u):
                sp.dma_start(cw[:, u, :, :], t["cwT_dram"][b, :, :, :].rearrange("g p n -> p g n")).then_inc(s_in[u], 16)
                sp.dma_start(eo[:, u, :, :], t["eo_dram"][b, :, :].rearrange("(g p) d -> p g d", p=128)).then_inc(s_in[u], 16)
                for tile in range(2):
                    sp.dma_start(h1[:, u, tile, :], t["h1_dram"][b, TILE_AT[tile]:TILE_AT[tile] + 128, :]).then_inc(s_in[u], 16)

            def store(b):
                sp.wait_ge(s["h2_ready"], b + 1)
                sp.dma_start(t["h2_dram"][b, NPATCH:N, :], h2[:, 0, :]).then_inc(s["h2_stored"], 16)
                sp.dma_start(t["h2_dram"][b, 0:NPATCH, :], h2[0:NPATCH, 1, :]).then_inc(s["h2_stored"], 16)
                sp.wait_ge(s["y_ready"], b + 1)
                sp.dma_start(t["y3_dram"][b, NPATCH:N, :], y[:, 0, :]).then_inc(s["y_stored"], 16)
                sp.dma_start(t["y3_dram"][b, 0:NPATCH, :], y[0:NPATCH, 1, :]).then_inc(s["y_stored"], 16)
                sp.wait_ge(s["lat_ready"], b + 1)
                sp.dma_start(t["lat_dram"][b, :, :], lat[:, :]).then_inc(s["lat_stored"], 16)

            load(0, 0)
            sp.dma_start(ident[:, :], t["ident"]).then_inc(s["consts_in"], 16)
            sp.dma_start(lnw[:, :], t["attn_ln_w"].rearrange("(c p) -> p c", p=DC), allow_slow_non_contiguous=True).then_inc(s["consts_in"], 16)
            sp.dma_start(wcomp[:, :, :], t["attn_w_comp"].rearrange("(c p) k -> p c k", p=DC)).then_inc(s["consts_in"], 16)
            sp.dma_start(wreso[:, :], t["attn_w_reso"]).then_inc(s["consts_in"], 16)
            load(1, 1)
            with sp.Fori(0, B // 2 - 1) as pair:
                for u in range(2):
                    b = pair * 2 + u
                    sp.wait_ge(s["h2_ready"], b + 1)
                    load(b + 2, u)
                    store(b)
            store(B - 2)
            store(B - 1)
            sp.wait_ge(s["h2_stored"], 32 * B)
            sp.wait_ge(s["y_stored"], 32 * B)
            sp.wait_ge(s["lat_stored"], 16 * B)

        @block.gpsimd
        def _(pool):
            nc.gpsimd.memset(half[:, :], -0.5).then_inc(s["half_ready"], 1)
            pool.wait_ge(s["half_ready"], 1)

            def turn(b, u, k):
                pool.wait_ge(s["var_ready"], b + 1)
                nc.gpsimd.tensor_tensor(r[:, :, :], g[:, 0:2, :], half[:, :].unsqueeze(1).to_broadcast([128, 2, 2]),
                                        ALU.pow).then_inc(s["r_ready"], 1)
            run(pool, turn)

        @block.vector
        def _(dve):
            ch = Chain(dve, s["chain"], s["passed"])
            dve.wait_ge(s["consts_in"], 64)
            nc.vector.tensor_tensor(wcomp[:, :, :], wcomp[:, :, :], lnw[:, :].unsqueeze(2).to_broadcast([DC, 2, 128]),
                                    ALU.mult).then_inc(s["wcomp_ready"], 1)
            LINKS = 5

            def turn(b, u, k):
                ch.base, ch.n = b * LINKS, 0
                dve.wait_ge(s_in[u], LOADS * k + LOADS)
                dve.wait_ge(s["comb_ps"], b + 1)
                dve.wait_ge(s["h2_stored"], 32 * b)
                nc.vector.tensor_tensor(h2[:, :, :], psum[:, 0:2, 0:D], h1[:, u, :, :], ALU.add).then_inc(s["h2_ready"], 1)
                dve.wait_ge(s["h2_ready"], b + 1)
                for j in range(2):
                    st = nc.vector.bn_stats(stats[:, j, :], h2[:, j, :])
                ch.link(st, apart=True)
                for j in range(2):
                    st = nc.vector.bn_aggr(mv[:, j, :], stats[:, j, :])
                ch.link(st)
                dve.wait_ge(s["r_ready"], b)
                dve.wait_ge(s["xr_ready"], b)
                ch.link(nc.vector.tensor_scalar(g[:, 0, :], mv[:, :, 1], LN_EPS, None, ALU.add))
                ch.link(nc.vector.reciprocal(g[:, 2, :], g[:, 0, :]))
                ch.link(nc.vector.tensor_tensor(g[:, 2, :], g[:, 2, :], mv[:, :, 1], ALU.mult))
                nc.vector.tensor_scalar(g[:, 1, :], g[:, 2, :], RMS_EPS, None, ALU.add).then_inc(s["var_ready"], 1)
                dve.wait_ge(s["r_ready"], b + 1)
                dve.wait_ge(s["y_stored"], 32 * b)
                for j in range(2):
                    st = nc.vector.tensor_scalar(y[:, j, :], h2[:, j, :], mv[:, j, 0:1], r[:, 0, j:j + 1],
                                                 ALU.subtract, ALU.mult)
                st.then_inc(s["y_ready"], 1)
                dve.wait_ge(s["y_ready"], b + 1)
                dve.wait_ge(s["xrT_ps"], b)
                for j in range(2):
                    st = nc.vector.tensor_scalar(xr[:, j, :], y[:, j, :], r[:, 1, j:j + 1], None, ALU.mult)
                st.then_inc(s["xr_ready"], 1)
                dve.wait_ge(s["lth_ready"], b + 1)
                dve.wait_ge(s["lat_stored"], 16 * b)
                dve.wait_ge(s["reso_ps"], b)
                nc.vector.scalar_tensor_tensor(lat[:, :], lth[:, :], 1.0, psum[:, 4, 0:N], ALU.add, ALU.mult).then_inc(s["lat_ready"], 1)
            run(dve, turn)

        @block.scalar
        def _(act):
            def turn(b, u, k):
                act.wait_ge(s["xrT_ps"], b + 1)
                act.wait_ge(s["lat_ps"], b)
                nc.scalar.copy(xrT[:, :, :], psum[0:DC, 2:4, 0:N]).then_inc(s["xrT_ready"], 1)
                act.wait_ge(s["lat_ps"], b + 1)
                act.wait_ge(s["lat_ready"], b)
                nc.scalar.activation(lth[:, :], psum[:, 4, 0:N], ACT.Tanh, scale=0.5).then_inc(s["lth_ready"], 1)
                act.wait_ge(s["reso_ps"], b + 1)
                nc.scalar.activation(th[:, b, :, :], psum[:, 5, 0:2 * RESO].rearrange("p (t k) -> p t k", t=2),
                                     ACT.Tanh, scale=0.25).then_inc(s["th_ready"], 1)
            run(act, turn)

        @block.tensor
        def _(pe):
            def product(b, u, k, tile, groups):
                if tile == 0 and groups[0] == 0:
                    pe.wait_ge(s_in[u], LOADS * k + LOADS)
                    pe.wait_ge(s["h2_ready"], b)
                at = TILE_AT[tile]
                for n in range(*groups):
                    mm = nc.tensor.matmul(psum[:, tile, 0:D], cw[:, u, n, at:at + 128], eo[:, u, n, :],
                                          start=(n == 0), stop=(n == NG - 1))
                if tile == 1 and groups[1] == NG:
                    mm.then_inc(s["comb_ps"], 1)

            def turned(b):
                pe.wait_ge(s["xr_ready"], b + 1)
                pe.wait_ge(s["xrT_ready"], b)
                for c in range(2):
                    for tile in range(2):
                        rows, at = TILE_ROWS[tile], TILE_AT[tile]
                        mm = nc.tensor.transpose(psum[0:DC, 2 + c, at:at + rows], xr[0:rows, tile, c * DC:c * DC + DC],
                                                 ident[0:rows, 0:rows])
                mm.then_inc(s["xrT_ps"], 1)

            def latent(b):
                pe.wait_ge(s["xrT_ready"], b + 1)
                pe.wait_ge(s["lat_ready"], b)
                pe.wait_ge(s["wcomp_ready"], 1)
                for c in range(2):
                    mm = nc.tensor.matmul(psum[:, 4, 0:N], wcomp[:, c, :], xrT[:, c, :], start=(c == 0), stop=(c == 1))
                mm.then_inc(s["lat_ps"], 1)

            def resonance(b):
                pe.wait_ge(s["lat_ready"], b + 1)
                pe.wait_ge(s["th_ready"], b)
                for tile in range(2):
                    at = TILE_AT[tile]
                    mm = nc.tensor.matmul(psum[:, 5, tile * RESO:tile * RESO + RESO], lat[:, at:at + 128], wreso[:, :],
                                          start=True, stop=True)
                mm.then_inc(s["reso_ps"], 1)

            def turn(b, u, k):
                following = not (isinstance(b, int) and b == 0)
                product(b, u, k, 0, (0, NG))
                if not following:
                    pe.wait_ge(s["consts_in"], 64)
                if following:
                    turned(b - 1)
                product(b, u, k, 1, (0, NG // 2))
                if following:
                    latent(b - 1)
                product(b, u, k, 1, (NG // 2, NG))
                if following:
                    resonance(b - 1)
            run(pe, turn)
            turned(B - 1)
            latent(B - 1)
            resonance(B - 1)


def gates(nc, t, ctx, th, vgate, decay):
    A = 2 * B
    PI = 3.141592653589793
    def sb(name, shape, dt=FP32):
        return ctx.enter_context(nc.sbuf_tensor("gat_" + name, shape, dt))

    hd = sb("hd", [128, HEADS])
    temp = sb("temp", [128, 1])
    pos = sb("pos", [128, 2])
    rate = sb("rate", [128, HEADS])
    ln = sb("ln", [128, HEADS])
    dt = sb("dt", [128, HEADS])
    rdf = sb("rdf", [128, 2, HEADS])
    z = sb("z", [128, A, HEADS])
    w = sb("w", [128, A, HEADS])
    p = sb("p", [128, A, HEADS])
    s = phase_sems(ctx, nc, "gat", "in_ sig ln_ready rate_ready df_arg df_ready arg arg_th chain")
    q4 = th[:, :, :, :].rearrange("p b t (h k) -> p (b t) h k", k=4)

    def load(sp):
        sp.dma_start(hd[:, :], row_bc(t["attn_head_decay"], 128)).then_inc(s["in_"], 16)
        sp.dma_start(temp[:, :], row_bc(t["attn_temperature"], 128)).then_inc(s["in_"], 16)
        sp.dma_start(pos[:, :], t["pos"]).then_inc(s["in_"], 16)

    def scalar(act):
        act.wait_ge(s["in_"], 48)
        nc.scalar.activation(rate[:, :], hd[:, :], ACT.Tanh, scale=0.5).then_inc(s["sig"], 1)
        act.wait_ge(s["rate_ready"], 1)
        nc.scalar.activation(ln[:, :], rate[:, :], ACT.Ln).then_inc(s["ln_ready"], 1)
        act.wait_ge(s["df_arg"], 1)
        nc.scalar.activation(decay[:, :, :], decay[:, :, :], ACT.Exp).then_inc(s["df_ready"], 1)
        act.wait_ge(s["arg"], 1)
        nc.scalar.activation(p[:, :, :], p[:, :, :], ACT.Tanh, scale=0.5).then_inc(s["arg_th"], 1)

    def vector(dve):
        ch = Chain(dve, s["chain"])
        dve.wait_ge(s["in_"], 48)
        dve.wait_ge(s["sig"], 1)
        ch.link(nc.vector.tensor_scalar(rate[:, :], rate[:, :], 0.65 / 2, 0.3 + 0.65 / 2, ALU.mult, ALU.add))
        nc.vector.tensor_scalar(rate[:, :], rate[:, :], 1e-5, 0.999, ALU.max, ALU.min).then_inc(s["rate_ready"], 1)
        dve.wait_ge(s["rate_ready"], 1)
        ch.link(nc.vector.tensor_scalar(dt[:, :], rate[:, :], -1.0, 1.0, ALU.mult, ALU.add))
        dve.wait_ge(s["ln_ready"], 1)
        for tile in range(2):
            st = nc.vector.tensor_scalar(decay[:, tile, :], ln[:, :], pos[:, tile:tile + 1], None, ALU.mult)
        st.then_inc(s["df_arg"], 1)
        ch.link(nc.vector.tensor_tensor(z[:, :, :], q4[:, :, :, 1], q4[:, :, :, 3], ALU.subtract))
        ch.link(nc.vector.tensor_scalar(z[:, :, :], z[:, :, :], PI / 4, None, ALU.mult))
        ch.link(nc.vector.tensor_tensor(w[:, :, :], z[:, :, :], z[:, :, :], ALU.mult))
        ch.link(nc.vector.tensor_scalar(p[:, :, :], w[:, :, :], 1 / 6227020800.0, None, ALU.mult))
        for c in (-1 / 39916800.0, 1 / 362880.0, -1 / 5040.0, 1 / 120.0, -1 / 6.0):
            ch.link(nc.vector.scalar_tensor_tensor(p[:, :, :], p[:, :, :], c, w[:, :, :], ALU.add, ALU.mult))
        ch.link(nc.vector.scalar_tensor_tensor(p[:, :, :], p[:, :, :], 1.0, z[:, :, :], ALU.add, ALU.mult))
        ch.link(nc.vector.tensor_tensor(p[:, :, :], p[:, :, :], p[:, :, :], ALU.mult))
        ch.link(nc.vector.tensor_scalar(p[:, :, :], p[:, :, :], -2.0, 1.0, ALU.mult, ALU.add))
        for k in (0, 2):
            ch.link(nc.vector.tensor_scalar(w[:, :, :], q4[:, :, :, k], 0.5, 0.5, ALU.mult, ALU.add))
            ch.link(nc.vector.tensor_tensor(p[:, :, :], p[:, :, :], w[:, :, :], ALU.mult))
        nc.vector.tensor_scalar(p[:, :, :], p[:, :, :], temp[:, :], None, ALU.mult).then_inc(s["arg"], 1)
        dve.wait_ge(s["df_ready"], 1)
        ch.link(nc.vector.tensor_scalar(rdf[:, :, :], decay[:, :, :], 1e-8, None, ALU.add))
        ch.link(nc.vector.reciprocal(rdf[:, :, :], rdf[:, :, :]))
        ch.link(nc.vector.tensor_tensor(rdf[:, :, :], rdf[:, :, :], dt[:, :].unsqueeze(1).to_broadcast([128, 2, HEADS]), ALU.mult))
        dve.wait_ge(s["arg_th"], 1)
        ch.link(nc.vector.tensor_scalar(p[:, :, :], p[:, :, :], 0.6, 0.5, ALU.mult, ALU.add))
        ch.link(nc.vector.tensor_scalar(p[:, :, :], p[:, :, :], 0.05, 0.95, ALU.max, ALU.min))
        for tile in range(2):
            ch.link(nc.vector.tensor_tensor(vgate[:, 0:B, tile, :],
                                            p[:, :, :].rearrange("p (b t) h -> p b t h", t=2)[:, :, tile, :],
                                            rdf[:, tile, :].unsqueeze(1).to_broadcast([128, B, HEADS]), ALU.mult))
        ch.link(nc.vector.tensor_copy(vgate[:, B, :, :], rdf[:, :, :]))
    return load, scalar, vector


def decay_attention(nc, t, psum, th, vgate, decay):
    NHG = HEADS // 4
    QK = 2 * D
    with ExitStack() as ctx:
        def sb(name, shape, dt=FP32):
            return ctx.enter_context(nc.sbuf_tensor("dec_" + name, shape, dt))

        ident = sb("ident", [128, 128])
        half = sb("half", [128, 2])
        ones = sb("ones", [128, 1])
        causal = sb("causal", [128, 128])
        causal_b = sb("causal_b", [128, N])
        cosw = sb("cosw", [128, 2, 2, DH])
        sinw = sb("sinw", [128, 2, 2, DH])
        nw = sb("nw", [128, 2, DH])
        nwx = sb("nwx", [128, 2, DH])
        wqkv = sb("wqkv", [128, 3 * D])
        wog = sb("wog", [128, D])
        memn = sb("memn", [128, NHG])
        wproj = sb("wproj", [128, NHG, D])
        lat = sb("lat", [128, 2, N])
        y3 = sb("y3", [128, 2, 2, D])
        qk = sb("qk", [128, 2, QK])
        vo = sb("vo", [128, 2, 2 * D])
        sq = sb("sq", [128, 2, QK])
        ms = sb("ms", [128, 4 * HEADS])
        rt = sb("rt", [128, 4 * HEADS])
        rq = sb("rq", [128, 4 * HEADS])
        qa = sb("qa", [128, 2, QK])
        qb = sb("qb", [128, 2, QK])
        qe = sb("qe", [128, 2, QK])
        qp = sb("qp", [128, 2, D])
        qkf = sb("qkf", [128, 2, 2 * HEADS, 32])
        kr = sb("kr", [128, 2, D])
        qc = sb("qc", [128, 2, D])
        den = sb("den", [128, 2, HEADS])
        qkT = sb("qkT", [128, 2, NHG, N])
        kbd = sb("kbd", [128, NHG, 4, 32])
        ogt = sb("ogt", [128, 2, D])
        og = sb("og", [128, 2, 2, D])
        vg = sb("vg", [128, 2, HEADS, DH])
        vgb = sb("vgb", [128, 2, NHG, 4, 32])
        at_ = sb("at", [128, 4, NHG, 128])
        ap_ = sb("ap", [128, NHG, N])
        oT = sb("oT", [128, NHG, N])
        osq = sb("osq", [128, NHG, N])
        oss = sb("oss", [128, 2])
        ro = sb("ro", [128, 2])
        x2 = sb("x2", [128, 2, D])
        s = phase_sems(ctx, nc, "dec", "consts_in half_ready padded wproj_ready tables_ready zeroed in0 in1 y_in0 y_in1 wl_ps qk_out vo_out "
                       "sq_ready ms_ready rt_ready qb_ready qm_ready qe_ready kr_ready kc_ps qc_ready qkf_ready turned qkT_ready kbd_ready "
                       "ogt_ready og_ready vg_ready sc_ps scp_ps masked masked_p ov_ps oT_ready ss_ps mso_ready ro_ready pr_ps x2_ready "
                       "x2_stored chain")
        gates_load, gates_scalar, gates_vector = gates(nc, t, ctx, th, vgate, decay)
        block = ctx.enter_context(nc.Block())
        s_in, y_in = (s["in0"], s["in1"]), (s["y_in0"], s["y_in1"])
        CONSTS = 9 + 6 + 4 + HEADS

        def run(eng, turn):
            turn(0, 0, 0, 0)
            with eng.Fori(0, B // 2 - 1) as pair:
                turn(pair * 2 + 1, 1, pair, pair)
                turn(pair * 2 + 2, 0, pair + 1, pair)
            turn(B - 1, 1, B // 2 - 1, B // 2 - 1)

        def first(b):
            return isinstance(b, int) and b == 0

        def last(b):
            return isinstance(b, int) and b == B - 1

        @block.sync
        def _(sp):
            gates_load(sp)
            for dst, src in ((ident[:, :], t["ident"]), (causal[:, :], t["causal"]), (causal_b[:, :], t["causal_b"]),
                             (cosw[:, :, 0, :], t["cos"]), (cosw[:, :, 1, :], t["cos"]), (sinw[:, :, 0, :], t["sin"]), (sinw[:, :, 1, :], t["sin"]),
                             (wqkv[:, :], t["attn_w_qkv"]), (wog[:, :], t["attn_w_outgate"])):
                sp.dma_start(dst, src).then_inc(s["consts_in"], 16)
            for n, wn in enumerate((t["attn_qn_w"], t["attn_kn_w"])):
                sp.dma_start(nw[:, n, :], row_bc(wn, 128)).then_inc(s["consts_in"], 16)
                for k in range(2):
                    sp.dma_start(nwx[:, n, 8 * k:8 * k + 8], row_bc(wn[8 - 8 * k:16 - 8 * k], 128)).then_inc(s["consts_in"], 16)
            sp.wait_ge(s["padded"], 2)
            for r in range(4):
                lo = 32 * r
                sp.dma_start(wproj[lo:lo + DH, :, :], t["attn_w_proj"].rearrange("(g r d) k -> r d g k", r=4, d=DH)[r]).then_inc(s["consts_in"], 16)
            for g in range(NHG):
                for r in range(4):
                    at = (4 * g + r) * DH
                    sp.dma_start(memn[32 * r:32 * r + DH, g:g + 1], t["attn_memn_w"][at:at + DH].unsqueeze(1),
                                 allow_slow_non_contiguous=True).then_inc(s["consts_in"], 16)

            def load_lat(b, u):
                sp.dma_start(lat[:, u, :], t["lat_dram"][b, :, :]).then_inc(s_in[u], 16)

            def load_y(b, u):
                for tile in range(2):
                    sp.dma_start(y3[:, u, tile, :], t["y3_dram"][b, TILE_AT[tile]:TILE_AT[tile] + 128, :]).then_inc(y_in[u], 16)

            def store(b):
                sp.wait_ge(s["x2_ready"], b + 1)
                sp.dma_start(t["x2_dram"][b, NPATCH:N, :], x2[:, 0, :]).then_inc(s["x2_stored"], 16)
                sp.dma_start(t["x2_dram"][b, 0:NPATCH, :], x2[0:NPATCH, 1, :]).then_inc(s["x2_stored"], 16)

            for u in range(2):
                load_lat(u, u)
                load_y(u, u)
            with sp.Fori(0, B // 2 - 1) as pair:
                for u in range(2):
                    b = pair * 2 + u
                    sp.wait_ge(s["wl_ps"], 2 * b + 2)
                    load_lat(b + 2, u)
                    store(b)
                    load_y(b + 2, u)
            store(B - 2)
            store(B - 1)
            sp.wait_ge(s["x2_stored"], 32 * B)

        @block.gpsimd
        def _(pool):
            nc.gpsimd.memset(wproj[:, :, :], 0.0).then_inc(s["padded"], 1)
            nc.gpsimd.memset(memn[:, :], 0.0).then_inc(s["padded"], 1)
            nc.gpsimd.memset(ones[:, :], 1.0)
            nc.gpsimd.memset(half[:, :], -0.5).then_inc(s["half_ready"], 1)
            pool.wait_ge(s["half_ready"], 1)
            pool.wait_ge(s["tables_ready"], 1)

            def front(b):
                pool.wait_ge(s["qk_out"], 2 * b + 2)
                pool.wait_ge(s["qm_ready"], b)
                for tile in range(2):
                    for k in range(2):
                        src = qk[:, tile, :].rearrange("p (a h d) -> p a h d", a=2, d=DH)[:, :, :, 8 - 8 * k:16 - 8 * k]
                        dst = qb[:, tile, :].rearrange("p (a h d) -> p a h d", a=2, d=DH)[:, :, :, 8 * k:8 * k + 8]
                        for a in range(2):
                            st = nc.gpsimd.tensor_tensor(dst[:, a, :, :], src[:, a, :, :],
                                                         sinw[:, tile, a, 8 * k:8 * k + 8].unsqueeze(1).to_broadcast([128, HEADS, 8]), ALU.mult)
                st.then_inc(s["qb_ready"], 1)

            def back(b):
                pool.wait_ge(s["mso_ready"], b + 1)
                pool.wait_ge(s["x2_ready"], b)
                nc.gpsimd.tensor_tensor(ro[:, :], oss[:, :], half[:, :], ALU.pow).then_inc(s["ro_ready"], 1)

            def turn(b, u, k, before):
                front(b)
                if not first(b):
                    back(b - 1)
            run(pool, turn)
            back(B - 1)

        @block.vector
        def _(dve):
            gates_vector(dve)
            ch = Chain(dve, s["chain"])
            for x in (qkf[:, :, :, :], kbd[:, :, :, :], vgb[:, :, :, :, :]):
                nc.vector.memset(x, 0.0).then_inc(s["zeroed"], 1)
            dve.wait_ge(s["consts_in"], CONSTS * 16)
            nc.vector.tensor_tensor(wproj[:, :, :], wproj[:, :, :], memn[:, :].unsqueeze(2).to_broadcast([128, NHG, D]),
                                    ALU.mult).then_inc(s["wproj_ready"], 1)
            for tile in range(2):
                nc.vector.tensor_tensor(cosw[:, tile, :, :], cosw[:, tile, :, :], nw[:, :, :], ALU.mult)
                st = nc.vector.tensor_tensor(sinw[:, tile, :, :], sinw[:, tile, :, :], nwx[:, :, :], ALU.mult)
            st.then_inc(s["tables_ready"], 1)
            dve.wait_ge(s["tables_ready"], 1)
            dve.wait_ge(s["zeroed"], 3)
            LINKS = 11

            def heads(x):
                return x.rearrange("p t (h d) -> p (t h) d", d=DH)

            def by_head(x):
                return x.rearrange("p (h d) -> p h d", d=DH)

            def front1(b, u):
                dve.wait_ge(s["qk_out"], 2 * b + 2)
                for tile in range(2):
                    for a in range(2):
                        st = nc.vector.tensor_tensor(by_head(qa[:, tile, a * D:a * D + D]), by_head(qk[:, tile, a * D:a * D + D]),
                                                     cosw[:, tile, a, :].unsqueeze(1).to_broadcast([128, HEADS, DH]), ALU.mult)
                ch.link(st)
                dve.wait_ge(s["sq_ready"], b + 1)
                dve.wait_ge(s["rt_ready"], b)
                ch.link(nc.vector.tensor_reduce(ms[:, :], heads(sq[:, :, :]), AXX, ALU.add))
                nc.vector.tensor_scalar(ms[:, :], ms[:, :], 1.0 / DH, RMS_EPS, ALU.mult, ALU.add).then_inc(s["ms_ready"], 1)
                dve.wait_ge(s["vo_out"], 2 * b + 2)
                if not (isinstance(b, int) and b < 2):
                    dve.wait_ge(s["ov_ps"], b - 1)
                nc.vector.tensor_tensor(vg[:, u, :, :], by_head(vo[:, 0, 0:D]), vgate[:, b, 0, :].unsqueeze(2).to_broadcast([128, HEADS, DH]), ALU.mult)
                for r in range(4):
                    st = nc.vector.tensor_tensor(vgb[32 * r:32 * r + NPATCH, u, :, r, 0:DH],
                                                 vo[0:NPATCH, 1, 0:D].rearrange("p (g r d) -> p g r d", r=4, d=DH)[:, :, r, :],
                                                 vgate[0:NPATCH, b, 1, r:HEADS:4].unsqueeze(2).to_broadcast([NPATCH, NHG, DH]), ALU.mult)
                st.then_inc(s["vg_ready"], 1)
                dve.wait_ge(s["qb_ready"], b + 1)
                ch.link(nc.vector.tensor_tensor(qa[:, :, :], qa[:, :, :], qb[:, :, :], ALU.add))

            def front2(b):
                dve.wait_ge(s["rt_ready"], b + 1)
                ch.link(nc.vector.reciprocal(rq[:, :], rt[:, :]))

            def front2b(b):
                ch.link(nc.vector.tensor_tensor(heads(qa[:, :, :]), heads(qa[:, :, :]),
                                                rq[:, :].unsqueeze(2).to_broadcast([128, 4 * HEADS, DH]), ALU.mult))
                nc.vector.tensor_scalar(qe[:, :, :], qa[:, :, :], 0.0, None, ALU.min).then_inc(s["qm_ready"], 1)

            def front3(b, u):
                dve.wait_ge(s["qe_ready"], b + 1)
                dve.wait_ge(s["turned"], b)
                nc.vector.scalar_tensor_tensor(qp[:, :, :], qa[:, :, 0:D], 0.0, qe[:, :, 0:D], ALU.max, ALU.add)
                for tile in range(2):
                    st = nc.vector.scalar_tensor_tensor(qkf[:, tile, HEADS:2 * HEADS, 0:DH], by_head(qa[:, tile, D:QK]), 0.0,
                                                        by_head(qe[:, tile, D:QK]), ALU.max, ALU.add)
                ch.link(st)
                dve.wait_ge(s["kc_ps"], b)
                for tile in range(2):
                    st = nc.vector.tensor_tensor(by_head(kr[:, tile, :]), qkf[:, tile, HEADS:2 * HEADS, 0:DH],
                                                 vgate[:, B, tile, :].unsqueeze(2).to_broadcast([128, HEADS, DH]), ALU.mult)
                st.then_inc(s["kr_ready"], 1)
                dve.wait_ge(s["ogt_ready"], b + 1)
                nc.vector.scalar_tensor_tensor(og[:, u, :, :], ogt[:, :, :], 1.0, vo[:, :, D:2 * D], ALU.add, ALU.mult).then_inc(s["og_ready"], 1)

            def front4(b):
                dve.wait_ge(s["kc_ps"], b + 1)
                nc.vector.tensor_tensor(qc[:, :, :], psum[:, 2, 0:2 * D].rearrange("p (t d) -> p t d", t=2), qp[:, :, :],
                                        ALU.mult).then_inc(s["qc_ready"], 1)
                dve.wait_ge(s["qc_ready"], b + 1)
                ch.link(nc.vector.tensor_reduce(den[:, :, :].rearrange("p t h -> p (t h)"), heads(qc[:, :, :]), AXX, ALU.add))

            def front5(b):
                ch.link(nc.vector.tensor_tensor(den[:, :, :], den[:, :, :], decay[:, :, :], ALU.mult))
                ch.link(nc.vector.tensor_scalar(den[:, :, :], den[:, :, :], 1e-5, None, ALU.max))
                ch.link(nc.vector.reciprocal(den[:, :, :], den[:, :, :]))
                ch.link(nc.vector.tensor_tensor(den[:, :, :], den[:, :, :], decay[:, :, :], ALU.mult))
                for tile in range(2):
                    st = nc.vector.tensor_tensor(qkf[:, tile, 0:HEADS, 0:DH], by_head(qp[:, tile, :]),
                                                 den[:, tile, :].unsqueeze(2).to_broadcast([128, HEADS, DH]), ALU.mult)
                st.then_inc(s["qkf_ready"], 1)

            def mask(b, half_):
                dve.wait_ge(s["sc_ps"], 2 * b + half_ + 1)
                dve.wait_ge(s["ov_ps"], b)
                for r in (2 * half_, 2 * half_ + 1):
                    st = nc.vector.tensor_tensor(at_[:, r, :, :], psum[:, 4 + r, 0:NHG * 128].rearrange("p (g n) -> p g n", g=NHG),
                                                 causal[:, :].unsqueeze(1).to_broadcast([128, NHG, 128]), ALU.mult)
                st.then_inc(s["masked"], 1)

            def mask_patches(b):
                dve.wait_ge(s["scp_ps"], b + 1)
                nc.vector.tensor_tensor(ap_[:, :, :], psum[:, 1, 0:NHG * N].rearrange("p (g n) -> p g n", g=NHG),
                                        causal_b[:, :].unsqueeze(1).to_broadcast([128, NHG, N]), ALU.mult).then_inc(s["masked_p"], 1)

            def post1(b):
                dve.wait_ge(s["ss_ps"], b + 1)
                dve.wait_ge(s["ro_ready"], b)
                nc.vector.tensor_scalar(oss[:, :], psum[:, 1, 0:2], 4.0 / D, 4.0 * RMS_EPS, ALU.mult, ALU.add).then_inc(s["mso_ready"], 1)

            def post2(b, u, k):
                dve.wait_ge(s["pr_ps"], b + 1)
                dve.wait_ge(s["ro_ready"], b + 1)
                dve.wait_ge(y_in[u], 32 * k + 32)
                dve.wait_ge(s["x2_stored"], 32 * b)
                dve.wait_ge(s["og_ready"], b + 1)
                for tile in range(2):
                    st = nc.vector.scalar_tensor_tensor(x2[:, tile, :], psum[:, 3, tile * D:tile * D + D], ro[:, tile:tile + 1],
                                                        og[:, u, tile, :], ALU.mult, ALU.mult)
                ch.link(st)
                nc.vector.tensor_tensor(x2[:, :, :], x2[:, :, :], y3[:, u, :, :], ALU.add).then_inc(s["x2_ready"], 1)

            def turn(b, u, k, before):
                if first(b):
                    ch.base, ch.n = 0, 0
                else:
                    ch.base, ch.n = LINKS + (b - 1) * (LINKS + 1), 0
                front1(b, u)
                if not first(b):
                    mask(b - 1, 0)
                front2(b)
                if not first(b):
                    mask(b - 1, 1)
                    mask_patches(b - 1)
                front2b(b)
                front3(b, u)
                front4(b)
                if not first(b):
                    post1(b - 1)
                front5(b)
                assert ch.n == LINKS, ch.n
                if not first(b):
                    post2(b - 1, 1 - u, before)
            run(dve, turn)
            ch.base, ch.n = LINKS + (B - 1) * (LINKS + 1), 0
            mask(B - 1, 0)
            mask(B - 1, 1)
            mask_patches(B - 1)
            post1(B - 1)
            post2(B - 1, 1, B // 2 - 1)

        @block.scalar
        def _(act):
            gates_scalar(act)
            act.wait_ge(s["zeroed"], 3)

            def evacuate(b):
                for tile in range(2):
                    act.wait_ge(s["wl_ps"], 2 * b + tile + 1)
                    act.wait_ge(s["qb_ready"], b)
                    act.wait_ge(s["ms_ready"], b)
                    act.wait_ge(s["vg_ready"], b)
                    act.wait_ge(s["og_ready"], b)
                    nc.scalar.mul(qk[:, tile, :], psum[:, 2 * tile, 0:QK], 0.5).then_inc(s["qk_out"], 1)
                    nc.scalar.mul(vo[:, tile, :], psum[:, 2 * tile + 1, 0:2 * D], 0.5).then_inc(s["vo_out"], 1)
                act.wait_ge(s["qk_out"], 2 * b + 2)
                nc.scalar.activation(sq[:, :, :], qk[:, :, :], ACT.Square).then_inc(s["sq_ready"], 1)

            def turned(b):
                act.wait_ge(s["turned"], b + 1)
                act.wait_ge(s["scp_ps"], b)
                nc.scalar.copy(qkT[:, :, :, :], psum[:, 0:3:2, 0:NHG * N].rearrange("p a (g n) -> p a g n", g=NHG)).then_inc(s["qkT_ready"], 1)
                for r in range(4):
                    lo = 32 * r
                    st = nc.scalar.copy(kbd[lo:lo + DH, :, r, 0:NPATCH],
                                        psum[lo:lo + DH, 2, 0:NHG * N].rearrange("p (g n) -> p g n", g=NHG)[:, :, 0:NPATCH])
                st.then_inc(s["kbd_ready"], 1)

            def root(b):
                act.wait_ge(s["ms_ready"], b + 1)
                act.wait_ge(s["qm_ready"], b)
                nc.scalar.activation(rt[:, :], ms[:, :], ACT.Sqrt).then_inc(s["rt_ready"], 1)

            def tanh_exp(b):
                act.wait_ge(s["vo_out"], 2 * b + 2)
                nc.scalar.activation(ogt[:, :, :], vo[:, :, D:2 * D], ACT.Tanh, scale=0.5).then_inc(s["ogt_ready"], 1)
                act.wait_ge(s["qm_ready"], b + 1)
                nc.scalar.activation(qe[:, :, :], qe[:, :, :], ACT.Exp).then_inc(s["qe_ready"], 1)

            def output(b):
                act.wait_ge(s["ov_ps"], b + 1)
                act.wait_ge(s["pr_ps"], b)
                ov = psum[:, 3, 0:NHG * N].rearrange("p (g n) -> p g n", g=NHG)
                nc.scalar.copy(oT[:, :, :], ov).then_inc(s["oT_ready"], 1)
                nc.scalar.activation(osq[:, :, :], ov, ACT.Square).then_inc(s["oT_ready"], 1)

            def turn(b, u, k, before):
                evacuate(b)
                if not first(b):
                    turned(b - 1)
                root(b)
                tanh_exp(b)
                if not first(b):
                    output(b - 1)
            run(act, turn)
            turned(B - 1)
            output(B - 1)

        @block.tensor
        def _(pe):
            pe.wait_ge(s["consts_in"], CONSTS * 16)
            pe.wait_ge(s["wproj_ready"], 1)
            pe.wait_ge(s["half_ready"], 1)

            def project(b, u, k):
                pe.wait_ge(s_in[u], 16 * k + 16)
                if not first(b):
                    pe.wait_ge(s["qk_out"], 2 * b)
                    pe.wait_ge(s["vo_out"], 2 * b)
                    pe.wait_ge(s["mso_ready"], b - 1)
                for tile in range(2):
                    at = TILE_AT[tile]
                    lhs = lat[:, u, at:at + 128]
                    if tile and not first(b):
                        pe.wait_ge(s["qc_ready"], b)
                    nc.tensor.matmul(psum[:, 2 * tile, 0:QK], lhs, wqkv[:, 0:QK], start=True, stop=True)
                    if tile and not first(b):
                        pe.wait_ge(s["x2_ready"], b - 1)
                    nc.tensor.matmul(psum[:, 2 * tile + 1, 0:D], lhs, wqkv[:, QK:3 * D], start=True, stop=True)
                    nc.tensor.matmul(psum[:, 2 * tile + 1, D:2 * D], lhs, wog[:, :], start=True, stop=True).then_inc(s["wl_ps"], 1)

            def turn_qk(b):
                pe.wait_ge(s["qkf_ready"], b + 1)
                pe.wait_ge(s["qk_out"], 2 * B if last(b) else 2 * b + 4)
                for a in range(2):
                    for g in range(NHG):
                        for tile in range(2):
                            rows, at = TILE_ROWS[tile], g * N + TILE_AT[tile]
                            mm = nc.tensor.transpose(psum[:, 2 * a, at:at + rows],
                                                     qkf[0:rows, tile, 12 * a + 4 * g:12 * a + 4 * g + 4, :].rearrange("p h d -> p (h d)"),
                                                     ident[0:rows, 0:rows])
                mm.then_inc(s["turned"], 1)

            def scores(b):
                pe.wait_ge(s["qkT_ready"], b + 1)
                pe.wait_ge(s["masked"], 2 * b)
                for half_ in range(2):
                    for g in range(NHG):
                        for r in (2 * half_, 2 * half_ + 1):
                            lo = 32 * r
                            mm = nc.tensor.matmul(psum[:, 4 + r, 128 * g:128 * g + 128], qkT[lo:lo + DH, 1, g, NPATCH:N],
                                                  qkT[lo:lo + DH, 0, g, NPATCH:N], start=True, stop=True)
                    mm.then_inc(s["sc_ps"], 1)
                pe.wait_ge(s["kbd_ready"], b + 1)
                pe.wait_ge(s["vo_out"], 2 * B if last(b) else 2 * b + 4)
                pe.wait_ge(s["mso_ready"], b)
                for g in range(NHG):
                    mm = nc.tensor.matmul(psum[:, 1, g * N:g * N + N], kbd[:, g, :, :].rearrange("p r m -> p (r m)"),
                                          qkT[:, 0, g, :], start=True, stop=True)
                mm.then_inc(s["scp_ps"], 1)

            def values(b, u):
                pe.wait_ge(s["masked_p"], b + 1)
                pe.wait_ge(s["masked"], 2 * b + 2)
                pe.wait_ge(s["vg_ready"], b + 1)
                pe.wait_ge(s["x2_ready"], b)
                for g in range(NHG):
                    nc.tensor.matmul(psum[:, 3, g * N:g * N + N], vgb[:, u, g, :, :].rearrange("p r d -> p (r d)"), ap_[:, g, :],
                                     start=True, stop=False, skip_group_check=True)
                    for r in range(4):
                        lo = 32 * r
                        mm = nc.tensor.matmul(psum[lo:lo + DH, 3, g * N + NPATCH:g * N + N], vg[:, u, 4 * g + r, :], at_[:, r, g, :],
                                              start=False, stop=True, skip_group_check=True)
                mm.then_inc(s["ov_ps"], 1)

            def sums(b):
                pe.wait_ge(s["kr_ready"], b + 1)
                if not first(b):
                    pe.wait_ge(s["kbd_ready"], b)
                else:
                    pe.wait_ge(s["qk_out"], 2)
                nc.tensor.matmul(psum[:, 2, 0:D], causal[:, :], kr[:, 0, :], start=True, stop=False)
                nc.tensor.matmul(psum[:, 2, 0:D], causal_b[0:NPATCH, NPATCH:N], kr[0:NPATCH, 1, :], start=False, stop=True)
                nc.tensor.matmul(psum[:, 2, D:2 * D], causal_b[0:NPATCH, 0:128], kr[0:NPATCH, 1, :], start=True, stop=True).then_inc(s["kc_ps"], 1)

            def out(b):
                pe.wait_ge(s["oT_ready"], 2 * b + 2)
                for tile in range(2):
                    at = TILE_AT[tile]
                    for g in range(NHG):
                        mm = nc.tensor.matmul(psum[:, 1, tile:tile + 1], osq[:, g, at:at + 128], ones[:, :],
                                              start=(g == 0), stop=(g == NHG - 1))
                mm.then_inc(s["ss_ps"], 1)
                for tile in range(2):
                    at = TILE_AT[tile]
                    for g in range(NHG):
                        mm = nc.tensor.matmul(psum[:, 3, tile * D:tile * D + D], oT[:, g, at:at + 128], wproj[:, g, :],
                                              start=(g == 0), stop=(g == NHG - 1))
                mm.then_inc(s["pr_ps"], 1)

            def turn(b, u, k, before):
                project(b, u, k)
                if not first(b):
                    turn_qk(b - 1)
                    scores(b - 1)
                    values(b - 1, 1 - u)
                sums(b)
                if not first(b):
                    out(b - 1)
            run(pe, turn)
            turn_qk(B - 1)
            scores(B - 1)
            values(B - 1, 1)
            out(B - 1)


TM = 102
NT = B * N // TM
PER = 4
BLOCKS = NT // PER
BT = PER * TM
FJ = F1 // 128
NE = E1 + 1


def gated_ffn(nc, t, psum, h3, wguT, wdT):
    HID = 512
    HJ = HID // 128
    BUFS = 4
    BANKS = (2, 3, 1, 0)
    with ExitStack() as ctx:
        def sb(name, shape, dt=FP32):
            return ctx.enter_context(nc.sbuf_tensor("ffn_" + name, shape, dt))

        ident = sb("ident", [128, 128])
        half = sb("half", [128, NT])
        nwt = sb("nwt", [DC, 2])
        w1 = sb("w1", [DC, 2, HID])
        w2 = sb("w2", [DC, 2, HID])
        w3 = sb("w3", [128, HJ, D])
        stage_gu = sb("stage_gu", [128, BUFS, 2, FJ, D])
        stage_d = sb("stage_d", [DC, BUFS, 2, F1])
        x2 = sb("x2", [TM, NT, D])
        xr = sb("xr", [TM, NT, D])
        ss = sb("ss", [TM, NT])
        r = sb("r", [TM, NT])
        xrT = sb("xrT", [DC, 2, B * N])
        gth = sb("gth", [128, HJ, BT])
        hid = sb("hid", [128, HJ, BT])
        s = phase_sems(ctx, nc, "ffn", "consts_in w_ready w_in0 w_in1 w_in2 w_in3 wt_ps wt_out x2_in h2_in half_ready mss r_ready "
                       "xr_ready xrT_ps xrT_ready g_ps gth_ready g2_ready hid_ready o_ps sum_ready h3_ready chain")
        block = ctx.enter_context(nc.Block())
        w_in = [s[f"w_in{n}"] for n in range(BUFS)]

        def tiles(x):
            return x.rearrange("b n d -> (b n) d").rearrange("(k p) d -> p k d", p=TM)

        def experts(eng, turn):
            with eng.Fori(0, E1 // BUFS) as k:
                for u in range(BUFS):
                    turn(k * BUFS + u, u, k)
            turn(E1, 0, E1 // BUFS)

        @block.sync
        def _(sp):
            sp.dma_start(ident[:, :], t["ident"]).then_inc(s["consts_in"], 16)
            sp.dma_start(x2[:, :, :], tiles(t["x2_dram"])).then_inc(s["x2_in"], 16)
            for dst, src in ((w1[:, :, :], t["attn_w1"].rearrange("(c p) k -> p c k", p=DC)),
                             (w2[:, :, :], t["attn_w2"].rearrange("(c p) k -> p c k", p=DC)),
                             (w3[:, :, :], t["attn_w3"].rearrange("(j p) k -> p j k", p=128))):
                sp.dma_start(dst, src).then_inc(s["consts_in"], 16)
            sp.dma_start(nwt[:, :], t["attn_ffn_ln_w"].rearrange("(c p) -> p c", p=DC), allow_slow_non_contiguous=True).then_inc(s["consts_in"], 16)
            sp.dma_start(h3[:, :, :], tiles(t["h2_dram"])).then_inc(s["h2_in"], 16)

        @block.gpsimd
        def _(pool):
            nc.gpsimd.memset(half[:, :], -0.5).then_inc(s["half_ready"], 1)
            pool.wait_ge(s["half_ready"], 1)
            pool.wait_ge(s["mss"], 1)
            nc.gpsimd.tensor_tensor(r[:, :], ss[:, :], half[0:TM, :], ALU.pow).then_inc(s["r_ready"], 1)

        @block.vector
        def _(dve):
            ch = Chain(dve, s["chain"])
            dve.wait_ge(s["x2_in"], 16)
            ch.link(nc.vector.tensor_tensor(xr[:, :, :], x2[:, :, :], x2[:, :, :], ALU.mult))
            ch.link(nc.vector.tensor_reduce(ss[:, :], xr[:, :, :], AXX, ALU.add))
            nc.vector.tensor_scalar(ss[:, :], ss[:, :], 1.0 / D, RMS_EPS, ALU.mult, ALU.add).then_inc(s["mss"], 1)
            dve.wait_ge(s["consts_in"], 5 * 16)
            for w in (w1, w2):
                nc.vector.tensor_tensor(w[:, :, :], w[:, :, :], nwt[:, :].unsqueeze(2).to_broadcast([DC, 2, HID]),
                                        ALU.mult).then_inc(s["w_ready"], 1)
            dve.wait_ge(s["h2_in"], 16)
            nc.vector.tensor_tensor(h3[:, :, :], h3[:, :, :], x2[:, :, :], ALU.add).then_inc(s["sum_ready"], 1)
            dve.wait_ge(s["r_ready"], 1)
            for k in range(NT):
                nc.vector.tensor_scalar(xr[:, k, :], x2[:, k, :], r[:, k:k + 1], None, ALU.mult).then_inc(s["xr_ready"], 1)
            dve.wait_ge(s["sum_ready"], 1)

            with dve.Fori(0, BLOCKS) as i:
                for n, j in enumerate(BANKS):
                    dve.wait_ge(s["gth_ready"], HJ * i + n + 1)
                    nc.vector.scalar_tensor_tensor(gth[:, j, :], gth[:, j, :], 1.0, psum[:, 2 * j, 0:BT], ALU.add, ALU.mult).then_inc(s["g2_ready"], 1)
                    dve.wait_ge(s["g2_ready"], HJ * i + n + 1)
                    dve.wait_ge(s["o_ps"], 2 * i)
                    nc.vector.scalar_tensor_tensor(hid[:, j, :], gth[:, j, :], 0.5, psum[:, 2 * j + 1, 0:BT], ALU.mult, ALU.mult).then_inc(s["hid_ready"], 1)
                for m in range(2):
                    dve.wait_ge(s["o_ps"], 2 * i + m + 1)
                    part = h3[:, bass.ds(i * PER + 2 * m, 2), :]
                    nc.vector.tensor_tensor(part, part, psum[0:TM, m, 0:2 * D].rearrange("p (a d) -> p a d", a=2), ALU.add).then_inc(s["h3_ready"], 1)

        @block.scalar
        def _(act):
            def load(e, u, gate, up, down):
                act.dma_start(stage_gu[:, u, 0, :, :], gate.rearrange("(j p) d -> p j d", p=128)).then_inc(w_in[u], 16)
                act.dma_start(stage_gu[:, u, 1, :, :], up.rearrange("(j p) d -> p j d", p=128)).then_inc(w_in[u], 16)
                act.dma_start(stage_d[:, u, :, :], down.rearrange("(c p) f -> p c f", p=DC)).then_inc(w_in[u], 16)

            def copy(e):
                for n in range(2):
                    act.wait_ge(s["wt_ps"], 3 * e + n + 1)
                    nc.scalar.copy(wguT[:, e, n, :, :], psum[0:DC, 2 * n:2 * n + 2, 0:F1]).then_inc(s["wt_out"], 1)
                act.wait_ge(s["wt_ps"], 3 * e + 3)
                nc.scalar.copy(wdT[:, e, 0:2, :], psum[:, 4, 0:2 * D].rearrange("p (j d) -> p j d", j=2)).then_inc(s["wt_out"], 1)
                nc.scalar.copy(wdT[:, e, 2, :], psum[:, 5, 0:D]).then_inc(s["wt_out"], 1)

            def load_expert(e, u):
                load(e, u, t["ffn_Wg"][e, :, :], t["ffn_Wu"][e, :, :], t["ffn_Wd"][e, :, :])

            for e in range(BUFS):
                load_expert(e, e)
            for e in range(BUFS):
                copy(e)
                load_expert(BUFS + e, e)
            copy(BUFS)
            load(E1, 0, t["ffn_sg"], t["ffn_su"], t["ffn_sd"])
            for e in range(BUFS + 1, NE):
                copy(e)
            for k in range(BLOCKS):
                act.wait_ge(s["xrT_ps"], k + 1)
                nc.scalar.copy(xrT[:, :, k * BT:k * BT + BT], psum[0:DC, 6:8, 0:BT]).then_inc(s["xrT_ready"], 1)
            with act.Fori(0, BLOCKS) as i:
                for n, j in enumerate(BANKS):
                    act.wait_ge(s["g_ps"], 2 * HJ * i + 2 * n + 2)
                    act.wait_ge(s["hid_ready"], HJ * i)
                    nc.scalar.activation(gth[:, j, :], psum[:, 2 * j, 0:BT], ACT.Tanh, scale=0.5).then_inc(s["gth_ready"], 1)

        @block.tensor
        def _(pe):
            pe.wait_ge(s["consts_in"], 5 * 16)

            def turn(e, u, k):
                pe.wait_ge(w_in[u], 48 * k + 48)
                pe.wait_ge(s["wt_out"], 4 * e)
                for n in range(2):
                    for c in range(2):
                        for j in range(FJ):
                            mm = nc.tensor.transpose(psum[0:DC, 2 * n + c, 128 * j:128 * j + 128],
                                                     stage_gu[:, u, n, j, c * DC:c * DC + DC], ident[:, :])
                    mm.then_inc(s["wt_ps"], 1)
                for j in range(FJ):
                    for c in range(2):
                        at = (j % 2) * D + c * DC
                        mm = nc.tensor.transpose(psum[:, 4 + j // 2, at:at + DC], stage_d[:, u, c, 128 * j:128 * j + 128],
                                                 ident[0:DC, 0:DC])
                mm.then_inc(s["wt_ps"], 1)
            experts(pe, turn)
            for k in range(BLOCKS):
                pe.wait_ge(s["xr_ready"], PER * k + PER)
                pe.wait_ge(s["xrT_ready"], k)
                for c in range(2):
                    for a in range(PER):
                        mm = nc.tensor.transpose(psum[0:DC, 6 + c, a * TM:a * TM + TM],
                                                 xr[:, PER * k + a, c * DC:c * DC + DC], ident[0:TM, 0:TM])
                mm.then_inc(s["xrT_ps"], 1)
            pe.wait_ge(s["wt_out"], 4 * NE)
            pe.wait_ge(s["xrT_ready"], BLOCKS)
            pe.wait_ge(s["w_ready"], 2)

            with pe.Fori(0, BLOCKS) as i:
                for step, j in enumerate(BANKS):
                    if step == len(BANKS) - 1:
                        pe.wait_ge(s["h3_ready"], 2 * i)
                    for n, w in enumerate((w1, w2)):
                        for c in range(2):
                            mm = nc.tensor.matmul(psum[:, 2 * j + n, 0:BT], w[:, c, 128 * j:128 * j + 128],
                                                  xrT[:, c, bass.ds(i * BT, BT)], start=(c == 0), stop=(c == 1))
                        mm.then_inc(s["g_ps"], 1)
                pe.wait_ge(s["hid_ready"], HJ * i + HJ)
                for m in range(2):
                    for a in range(2):
                        at = (2 * m + a) * TM
                        for j in range(HJ):
                            mm = nc.tensor.matmul(psum[0:TM, m, a * D:a * D + D], hid[:, j, at:at + TM], w3[:, j, :],
                                                  start=(j == 0), stop=(j == HJ - 1))
                    mm.then_inc(s["o_ps"], 1)


def temporal_attention(nc, t, psum):
    with ExitStack() as ctx:
        def sb(name, shape):
            return ctx.enter_context(nc.sbuf_tensor("l1_" + name, shape, FP32))

        vgate = sb("vgate", [128, B + 1, 2, HEADS])
        decay = sb("decay", [128, 2, HEADS])
        with nc.sbuf_tensor("l1_th", [128, B, 2, 4 * HEADS], FP32) as th:
            combine(nc, t, psum, th)
            decay_attention(nc, t, psum, th, vgate, decay)


def routed_mixture(nc, t, psum, h3, wguT, wdT):
    ORDER = [E1] + list(range(E1))
    with ExitStack() as ctx:
        def sb(name, shape, dt=FP32):
            return ctx.enter_context(nc.sbuf_tensor("moe_" + name, shape, dt))

        ident = sb("ident", [128, 128])
        half = sb("half", [128, NT])
        before = sb("before", [128, E1, E1])
        ebias = sb("ebias", [128, E1])
        wr = sb("wr", [E1, D])
        wrT = sb("wrT", [DC, 2, E1])
        y = sb("y", [TM, NT, D])
        stats = sb("stats", [TM, NT, 6])
        mv = sb("mv", [TM, NT, 2])
        rstd = sb("rstd", [TM, NT])
        yT = sb("yT", [DC, 2, B * N])
        lg = sb("lg", [TM, NT, E1])
        sel = sb("sel", [TM, NT, E1])
        v1 = sb("v1", [TM, NT])
        cmp = sb("cmp", [TM, NT, E1, E1])
        eq = sb("eq", [TM, NT, E1, E1])
        comb = sb("comb", [TM, NT, E1])
        cb = sb("cb", [TM, PER, E1])
        sg = sb("sg", [128, FJ, BT])
        hT = sb("hT", [128, 2, FJ, BT])
        acc = sb("acc", [TM, PER, D])
        s = phase_sems(ctx, nc, "moe", "consts_in half_ready mv_ready rstd_ready y_ready yT_ps yT_out wrT_ps wrT_out "
                 "lg_ps lg_ready lg_exp comb_ready cb_ready g_ps sg_ready h_ready o_ps o_used0 o_used1 acc_ready out_stored chain")
        block = ctx.enter_context(nc.Block())
        o_used = (s["o_used0"], s["o_used1"])
        out_v = t["out"].rearrange("b n d -> (b n) d").rearrange("(k p) d -> p k d", p=TM)

        @block.sync
        def _(sp):
            for dst, src in ((ident[:, :], t["ident"]), (before[:, :, :], t["before"].unsqueeze(0).to_broadcast([128, E1, E1])),
                             (ebias[:, :], row_bc(t["ffn_expert_bias"], 128)), (wr[:, :], t["ffn_w_router"])):
                sp.dma_start(dst, src).then_inc(s["consts_in"], 16)
            with sp.Fori(0, BLOCKS) as k:
                sp.wait_ge(s["acc_ready"], k + 1)
                sp.dma_start(out_v[:, bass.ds(k * PER, PER), :], acc[:, :, :]).then_inc(s["out_stored"], 16)
            sp.wait_ge(s["out_stored"], 16 * BLOCKS)

        @block.gpsimd
        def _(pool):
            nc.gpsimd.memset(half[:, :], -0.5).then_inc(s["half_ready"], 1)
            pool.wait_ge(s["half_ready"], 1)
            for n, (k0, k1) in enumerate(((0, PER), (PER, NT))):
                pool.wait_ge(s["mv_ready"], n + 1)
                nc.gpsimd.tensor_tensor(rstd[:, k0:k1], mv[:, k0:k1, 1], half[0:TM, k0:k1], ALU.pow).then_inc(s["rstd_ready"], 1)

        @block.vector
        def _(dve):
            ch = Chain(dve, s["chain"])
            for part in (range(PER), range(PER, NT)):
                for k in part:
                    st = nc.vector.bn_stats(stats[:, k, :], h3[:, k, :])
                ch.link(st)
                for k in part:
                    st = nc.vector.bn_aggr(mv[:, k, :], stats[:, k, :])
                ch.link(st)
                of = mv[:, part[0]:NT if part[0] else PER, 1]
                nc.vector.tensor_scalar(of, of, LN_EPS, None, ALU.add).then_inc(s["mv_ready"], 1)
            for k in range(NT):
                dve.wait_ge(s["rstd_ready"], 1 if k < PER else 2)
                nc.vector.tensor_scalar(y[:, k, :], h3[:, k, :], mv[:, k, 0:1], rstd[:, k:k + 1],
                                        ALU.subtract, ALU.mult).then_inc(s["y_ready"], 1)
            dve.wait_ge(s["consts_in"], 64)
            dve.wait_ge(s["lg_ps"], 1)
            lps = psum[0:TM, 0, 0:NT * E1].rearrange("p (k e) -> p k e", e=E1)

            def over_experts(x):
                return x.unsqueeze(2).to_broadcast([TM, NT, E1])

            ch.link(nc.vector.tensor_reduce(v1[:, :], lps, AXX, ALU.max))
            nc.vector.tensor_tensor(lg[:, :, :], lps, over_experts(v1[:, :]), ALU.subtract).then_inc(s["lg_ready"], 1)
            dve.wait_ge(s["lg_exp"], 1)
            ch.link(nc.vector.tensor_reduce(v1[:, :], lg[:, :, :], AXX, ALU.add))
            ch.link(nc.vector.reciprocal(v1[:, :], v1[:, :]))
            ch.link(nc.vector.tensor_tensor(lg[:, :, :], lg[:, :, :], over_experts(v1[:, :]), ALU.mult))
            ch.link(nc.vector.tensor_tensor(sel[:, :, :], lg[:, :, :], ebias[0:TM, :].unsqueeze(1).to_broadcast([TM, NT, E1]), ALU.add))
            for k in range(NT):
                mine = sel[:, k, :].unsqueeze(2).to_broadcast([TM, E1, E1])
                other = sel[:, k, :].unsqueeze(1).to_broadcast([TM, E1, E1])
                nc.vector.tensor_tensor(cmp[:, k, :, :], other, mine, ALU.is_gt)
                st = nc.vector.tensor_tensor(eq[:, k, :, :], other, mine, ALU.is_equal)
            ch.link(st)
            ch.link(nc.vector.tensor_tensor(eq[:, :, :, :].rearrange("p k a b -> p k (a b)"), eq[:, :, :, :].rearrange("p k a b -> p k (a b)"),
                                            before[0:TM, :, :].rearrange("p a b -> p (a b)").unsqueeze(1).to_broadcast([TM, NT, E1 * E1]), ALU.mult))
            ch.link(nc.vector.tensor_tensor(cmp[:, :, :, :], cmp[:, :, :, :], eq[:, :, :, :], ALU.add))
            ch.link(nc.vector.tensor_reduce(sel[:, :, :].rearrange("p k e -> p (k e)"), cmp[:, :, :, :].rearrange("p k a b -> p (k a) b"), AXX, ALU.add))
            ch.link(nc.vector.tensor_scalar(sel[:, :, :], sel[:, :, :], 2.0, None, ALU.is_lt))
            ch.link(nc.vector.tensor_tensor(comb[:, :, :], sel[:, :, :], lg[:, :, :], ALU.mult))
            ch.link(nc.vector.tensor_reduce(v1[:, :], comb[:, :, :], AXX, ALU.add))
            ch.link(nc.vector.tensor_scalar(v1[:, :], v1[:, :], 1e-9, None, ALU.add))
            ch.link(nc.vector.reciprocal(v1[:, :], v1[:, :]))
            nc.vector.tensor_tensor(comb[:, :, :], comb[:, :, :], over_experts(v1[:, :]), ALU.mult).then_inc(s["comb_ready"], 1)
            dve.wait_ge(s["comb_ready"], 1)
            SETUP = ch.n
            ADDS = 2 * NE

            def hidden(k, n):
                for j in range(FJ):
                    dve.wait_ge(s["sg_ready"], (k * NE + n) * FJ + j + 1)
                    if n >= 2:
                        dve.wait_ge(s["o_ps"], (k * NE + n - 2) * 2 + 2)
                    else:
                        dve.wait_ge(s["o_ps"], k * NE * 2)
                    nc.vector.tensor_tensor(hT[:, n % 2, j, :], sg[:, j, :], psum[:, 2 * j + 1, 0:BT], ALU.mult).then_inc(s["h_ready"], 1)

            def add(k, n):
                for m in range(2):
                    dve.wait_ge(s["o_ps"], (k * NE + n) * 2 + m + 1)
                    part = psum[0:TM, 6 + m, 0:2 * D].rearrange("p (a d) -> p a d", a=2)
                    if n == 0:
                        nc.vector.tensor_tensor(acc[:, 2 * m:2 * m + 2, :], part, h3[:, bass.ds(k * PER + 2 * m, 2), :],
                                                ALU.add).then_inc(o_used[m], 1)
                    else:
                        dve.wait_ge(o_used[m], k * NE + n)
                        for a in range(2):
                            st = nc.vector.scalar_tensor_tensor(acc[:, 2 * m + a, :], part[:, a, :], cb[:, 2 * m + a, ORDER[n]:ORDER[n] + 1],
                                                                acc[:, 2 * m + a, :], ALU.mult, ALU.add)
                        st.then_inc(o_used[m], 1)

            with dve.Fori(0, BLOCKS) as k:
                nc.vector.tensor_copy(cb[:, :, :], comb[:, bass.ds(k * PER, PER), :]).then_inc(s["cb_ready"], 1)
                dve.wait_ge(s["cb_ready"], k + 1)
                dve.wait_ge(s["out_stored"], 16 * k)
                for n in range(NE):
                    hidden(k, n)
                    if n:
                        add(k, n - 1)
                add(k, NE - 1)
                for m in range(2):
                    dve.wait_ge(o_used[m], k * NE + NE)
                nc.vector.tensor_copy(acc[:, 0, 0:2], acc[:, 0, 0:2]).then_inc(s["acc_ready"], 1)

        @block.scalar
        def _(act):
            act.wait_ge(s["wrT_ps"], 1)
            nc.scalar.copy(wrT[:, :, :], psum[0:DC, 6, 0:2 * E1].rearrange("p (c e) -> p c e", c=2)).then_inc(s["wrT_out"], 1)

            for k in range(BLOCKS):
                act.wait_ge(s["yT_ps"], k + 1)
                b0 = 2 * (k % 2)
                nc.scalar.copy(yT[:, :, k * BT:k * BT + BT], psum[0:DC, b0:b0 + 2, 0:BT]).then_inc(s["yT_out"], 1)
            act.wait_ge(s["lg_ready"], 1)
            nc.scalar.activation(lg[:, :, :], lg[:, :, :], ACT.Exp).then_inc(s["lg_exp"], 1)
            with act.Fori(0, BLOCKS) as k:
                for n in range(NE):
                    for j in range(FJ):
                        act.wait_ge(s["g_ps"], (k * NE + n) * FJ + j + 1)
                        if n == 0:
                            act.wait_ge(s["h_ready"], k * NE * FJ)
                        else:
                            act.wait_ge(s["h_ready"], (k * NE + n - 1) * FJ + j + 1)
                        nc.scalar.activation(sg[:, j, :], psum[:, 2 * j, 0:BT], ACT.Silu).then_inc(s["sg_ready"], 1)

        @block.tensor
        def _(pe):
            pe.wait_ge(s["consts_in"], 64)
            for c in range(2):
                mm = nc.tensor.transpose(psum[0:DC, 6, c * E1:c * E1 + E1], wr[:, c * DC:c * DC + DC], ident[0:E1, 0:E1])
            mm.then_inc(s["wrT_ps"], 1)
            for k in range(BLOCKS):
                pe.wait_ge(s["y_ready"], PER * k + PER)
                if k >= 2:
                    pe.wait_ge(s["yT_out"], k - 1)
                for c in range(2):
                    for a in range(PER):
                        mm = nc.tensor.transpose(psum[0:DC, 2 * (k % 2) + c, a * TM:a * TM + TM],
                                                 y[:, PER * k + a, c * DC:c * DC + DC], ident[0:TM, 0:TM])
                mm.then_inc(s["yT_ps"], 1)
            pe.wait_ge(s["yT_out"], BLOCKS)
            pe.wait_ge(s["wrT_out"], 1)
            for k in range(NT):
                for c in range(2):
                    mm = nc.tensor.matmul(psum[0:TM, 0, k * E1:k * E1 + E1], yT[:, c, k * TM:k * TM + TM], wrT[:, c, :],
                                          start=(c == 0), stop=(c == 1))
            mm.then_inc(s["lg_ps"], 1)
            pe.wait_ge(s["lg_ready"], 1)

            def hidden(k, n):
                for j in range(FJ):
                    if n == 0:
                        pe.wait_ge(s["h_ready"], k * NE * FJ)
                    else:
                        pe.wait_ge(s["h_ready"], (k * NE + n - 1) * FJ + j + 1)
                    for a in range(2):
                        for c in range(2):
                            mm = nc.tensor.matmul(psum[:, 2 * j + a, 0:BT], wguT[:, ORDER[n], a, c, 128 * j:128 * j + 128],
                                                  yT[:, c, bass.ds(k * BT, BT)], start=(c == 0), stop=(c == 1))
                    mm.then_inc(s["g_ps"], 1)

            def output(k, n):
                pe.wait_ge(s["h_ready"], (k * NE + n) * FJ + FJ)
                for m in range(2):
                    pe.wait_ge(o_used[m], k * NE + n)
                    for a in range(2):
                        at = (2 * m + a) * TM
                        for j in range(FJ):
                            mm = nc.tensor.matmul(psum[0:TM, 6 + m, a * D:a * D + D], hT[:, n % 2, j, at:at + TM],
                                                  wdT[:, ORDER[n], j, :], start=(j == 0), stop=(j == FJ - 1))
                    mm.then_inc(s["o_ps"], 1)

            with pe.Fori(0, BLOCKS) as k:
                for n in range(NE):
                    hidden(k, n)
                    if n:
                        output(k, n - 1)
                output(k, NE - 1)


def feed_forwards(nc, t, psum):
    with ExitStack() as ctx:
        def sb(name, shape):
            return ctx.enter_context(nc.sbuf_tensor("ff_" + name, shape, FP32))

        h3 = sb("h3", [TM, NT, D])
        wguT = sb("wguT", [DC, NE, 2, 2, F1])
        wdT = sb("wdT", [128, NE, FJ, D])
        gated_ffn(nc, t, psum, h3, wguT, wdT)
        routed_mixture(nc, t, psum, h3, wguT, wdT)


def build(nc, ins, outs, consts, scratch):
    t = {"x": ins["x"], "txt": ins["txt"], "tok_W": ins["L0_tok_W"], "tok_b": ins["L0_tok_b"],
         "tok_alpha_w": ins["L0_tok_alpha_w"], "tok_alpha_a": ins["L0_tok_alpha_a"], "attn_W": ins["L0_attn_W"],
         "attn_params": [ins["L0_attn_" + n] for n in ("b", "bn_gamma", "bn_beta", "bn_mean", "bn_var")],
         "out": outs[0], **consts, **scratch}
    t.update({n.split("_", 1)[1]: a for n, a in ins.items() if n.startswith(("L0_ffn", "L1_"))})
    with nc.psum_tensor("banks", [128, 8, 512], FP32) as psum:
        for phase in (patches, spiking_attention, soft_mixture, temporal_attention, feed_forwards):
            phase(nc, t, psum)


_SCRATCH = {"h_dram": (B, N, D), "h1_dram": (B, N, D), "xn_dram": (B, N, D), "xnT_dram": (B, 2, DC, N),
            "cwT_dram": (B, NG, 128, N), "eo_dram": (B, SLOTS, D), "h2_dram": (B, N, D), "y3_dram": (B, N, D),
            "lat_dram": (B, 128, N), "x2_dram": (B, N, D)}


def _constants():
    import numpy as np
    f32 = np.float32
    token = np.stack([np.arange(128) + NPATCH, np.arange(128)], 1)
    freq = (f32(1.0) / f32(10000.0) ** (np.arange(0, DH, 2, dtype=f32) / f32(DH))).astype(f32)
    angle = token[:, :, None].astype(f32) * np.concatenate([freq, freq])
    sign = np.concatenate([-np.ones(DH // 2), np.ones(DH // 2)])
    tokens = np.arange(N)
    return {"ident": np.eye(128, dtype=f32),
            "heads_mask": np.kron(np.eye(DC // DH), np.ones((DH, DH))).astype(f32),
            "cos": np.cos(angle).astype(f32), "sin": (np.sin(angle) * sign).astype(f32),
            "pos": (token + 1).astype(f32),
            "causal": np.triu(np.ones((128, 128), f32)),
            "causal_b": ((tokens[:128, None] % 32 < NPATCH) & (tokens[:128, None] % 32 <= tokens[None, :])).astype(f32),
            "before": np.tril(np.ones((E1, E1), f32), -1)}


def kernel(**inputs):
    import numpy as _np
    import concourse.bacc as _bacc
    from concourse import mybir as _mybir
    from concourse.bass_utils import run_bass_kernel_spmd as _run

    nc = _bacc.Bacc("TRN2", target_bir_lowering=False, num_devices=1)
    arrays, ins, consts, scratch = {}, {}, {}, {}
    for name, value in inputs.items():
        a = _np.ascontiguousarray(value)
        if a.ndim == 0:
            a = a.reshape(1)
        arrays[f"in_{name}_dram"] = a
        ins[name] = nc.dram_tensor(f"in_{name}_dram", a.shape, _mybir.dt.from_np(a.dtype), kind="ExternalInput").ap()
    for name, a in _constants().items():
        arrays[f"const_{name}_dram"] = a
        consts[name] = nc.dram_tensor(f"const_{name}_dram", a.shape, _mybir.dt.from_np(a.dtype), kind="ExternalInput").ap()
    for name, shape in _SCRATCH.items():
        scratch[name] = nc.dram_tensor(name, shape, _mybir.dt.float32, kind="Internal").ap()
    outs = [nc.dram_tensor("out_0_dram", (B, N, D), _mybir.dt.float32, kind="ExternalOutput").ap()]
    build(nc, ins, outs, consts, scratch)
    r = _run(nc, [arrays], core_ids=[0])
    return r.results[0]["out_0_dram"]
```
